# Optimizing a Trainium2 kernel written in Bass

```python
import numpy as np
import jax
import jax.numpy as jnp

def _softmax(x, axis=-1):
    return jax.nn.softmax(x, axis=axis)

def _gelu(x):
    return jax.nn.gelu(x, approximate=True)

def _silu(x):
    return jax.nn.silu(x)

def _sigmoid(x):
    return jax.nn.sigmoid(x)

def _layernorm(x, axis=-1, eps=1e-05):
    m = jnp.mean(x, axis=axis, keepdims=True)
    v = jnp.var(x, axis=axis, keepdims=True)
    return (x - m) / jnp.sqrt(v + eps)

def _scatter_add(tgt, idx, src, axis=0):
    return tgt.at[idx].add(src)

def _segment_sum(src, seg, n):
    return jax.ops.segment_sum(src, seg, n)
kernel_name = 'mk_early_fusion_d1_tok_img512_r4_66f2b7'

def setup_inputs(seed: int=0):
    np.random.seed(seed)
    _w = jnp.asarray

    def _rec_inputs():
        import jax
        import jax.numpy as jnp
        _rk = jax.random.key(seed)
        x = -0.00136767 + 1.0008 * jax.random.normal(jax.random.fold_in(_rk, 1), (32, 128, 50, 3), jnp.float32)
        txt = -3.48788e-10 + 0.999988 * jax.random.normal(jax.random.fold_in(_rk, 2), (32, 128, 128), jnp.float32)
        return (x, txt)
    x, txt = _rec_inputs()

    def _L0_tok_setup():
        import jax, jax.numpy as jnp
        import numpy as np
        J = 50
        HEADS = 4
        DIMS = [3, 64, 128, 64]
        POSE_DIM = 128
        B, T = (16, 128)

        def build_edge_index():
            e = []
            for i in range(J - 1):
                e.append((i, i + 1))
                e.append((i + 1, i))
            for i in range(J):
                e.append((i, i))
            e = sorted(e)
            return jnp.array(e, dtype=jnp.int32).T

        def _layer_norm(x, g, b, eps=1e-05):
            mu = jnp.mean(x, axis=-1, keepdims=True)
            var = jnp.mean(jnp.square(x - mu), axis=-1, keepdims=True)
            return (x - mu) * jax.lax.rsqrt(var + eps) * g + b

        def _gat(x, src, dst, W, a_s, a_d, bias):
            G, Jn, _ = x.shape
            H, C = a_s.shape
            h = (x @ W).reshape(G, Jn, H, C)
            es = jnp.einsum('gjhc,hc->gjh', h, a_s)[:, src]
            ed = jnp.einsum('gjhc,hc->gjh', h, a_d)[:, dst]
            e = jax.nn.leaky_relu(es + ed, 0.2)
            m = jnp.full((G, Jn, H), -jnp.inf, e.dtype).at[:, dst].max(e)
            m = jax.lax.stop_gradient(m)
            w = jnp.exp(e - m[:, dst])
            den = jnp.zeros((G, Jn, H), e.dtype).at[:, dst].add(w)
            alpha = w / den[:, dst]
            out = jnp.zeros((G, Jn, H, C), e.dtype).at[:, dst].add(alpha[..., None] * h[:, src])
            return out.reshape(G, Jn, H * C) + bias

        def _forward(pose_seq, layers, fpW, fpb, fng, fnb, edge_index):
            Bb, Tt = (pose_seq.shape[0], pose_seq.shape[1])
            x = pose_seq.reshape(Bb * Tt, J, 3)
            src, dst = (edge_index[0], edge_index[1])
            for W, a_s, a_d, bg, R, g, b in layers:
                h = _gat(x, src, dst, W, a_s, a_d, bg)
                res = x @ R
                x = jax.nn.gelu(_layer_norm(h + res, g, b), approximate=False)
            x = x.reshape(Bb * Tt, J * DIMS[-1]) @ fpW + fpb
            x = _layer_norm(x, fng, fnb)
            return x.reshape(Bb, Tt, POSE_DIM)
        key = jax.random.key(seed)
        ks = iter(jax.random.split(key, 64))

        def nrm(shape, s):
            return jax.random.normal(next(ks), shape, jnp.float32) * s
        inp = {'pose_seq': jax.random.normal(next(ks), (B, T, J, 3), jnp.float32)}
        for i in range(3):
            din, dout = (DIMS[i], DIMS[i + 1])
            C = dout // HEADS
            inp[f'W{i}'] = nrm((din, dout), din ** (-0.5))
            inp[f'as{i}'] = nrm((HEADS, C), 0.1)
            inp[f'ad{i}'] = nrm((HEADS, C), 0.1)
            inp[f'bg{i}'] = jnp.zeros((dout,), jnp.float32)
            inp[f'R{i}'] = nrm((din, dout), din ** (-0.5))
            inp[f'g{i}'] = jnp.ones((dout,), jnp.float32)
            inp[f'b{i}'] = jnp.zeros((dout,), jnp.float32)
        inp['fpW'] = nrm((J * DIMS[-1], POSE_DIM), (J * DIMS[-1]) ** (-0.5))
        inp['fpb'] = jnp.zeros((POSE_DIM,), jnp.float32)
        inp['fng'] = jnp.ones((POSE_DIM,), jnp.float32)
        inp['fnb'] = jnp.zeros((POSE_DIM,), jnp.float32)
        inp['edge_index'] = build_edge_index()
        return inp
    _L0_tok_all = _L0_tok_setup()
    _L0_tok_in = {k: v for k, v in _L0_tok_all.items() if k in ('W0', 'as0', 'ad0', 'bg0', 'R0', 'g0', 'b0', 'W1', 'as1', 'ad1', 'bg1', 'R1', 'g1', 'b1', 'W2', 'as2', 'ad2', 'bg2', 'R2', 'g2', 'b2', 'fpW', 'fpb', 'fng', 'fnb', 'edge_index')}
    del _L0_tok_all

    def _L0_attn_setup():
        import jax, jax.numpy as jnp
        import numpy as np
        B, S, DIM, HID, K = (4, 2048, 128, 256, 4)
        MEM_LR, MEM_MOM = (0.01, 0.9)
        EPS = 1e-12

        def _proj2(x, w1, w2):
            return jax.nn.silu(x @ w1.T) @ w2.T

        def _causal_dwconv(x, w, b):
            xp = jnp.pad(x, ((0, 0), (K - 1, 0), (0, 0)))
            kern = jnp.transpose(w, (2, 1, 0))
            out = jax.lax.conv_general_dilated(xp, kern, (1,), 'VALID', dimension_numbers=('NWC', 'WIO', 'NWC'), feature_group_count=x.shape[-1])
            return out + b

        def _l2norm(x):
            n = jnp.linalg.norm(x, axis=-1, keepdims=True)
            return x / jnp.maximum(n, EPS)

        def _mem_fwd(h, ws):
            for i, w in enumerate(ws):
                h = h @ w.T
                if i < len(ws) - 1:
                    h = jax.nn.silu(h)
            return h

        def _reference_tuple_inner(x, w_k1, w_k2, w_v1, w_v2, w_q1, w_q2, conv_k_w, conv_k_b, conv_v_w, conv_v_b, conv_q_w, conv_q_b, gate_d_w, gate_d_b, gate_lr_w, gate_lr_b, gate_m_w, gate_m_b, w_out, mem_w1, mem_w2, mom1, mom2):
            keys = _proj2(x, w_k1, w_k2)
            values = _proj2(x, w_v1, w_v2)
            queries = _proj2(x, w_q1, w_q2)
            keys = _causal_dwconv(keys, conv_k_w, conv_k_b)
            values = _causal_dwconv(values, conv_v_w, conv_v_b)
            queries = _causal_dwconv(queries, conv_q_w, conv_q_b)
            keys = _l2norm(jax.nn.silu(keys))
            values = jax.nn.silu(values)
            queries = _l2norm(jax.nn.silu(queries))
            retrieved = _mem_fwd(queries, (mem_w1, mem_w2))
            x_mean = jnp.mean(x, axis=1, keepdims=True)
            alpha = jnp.mean(jax.nn.sigmoid(x_mean @ gate_d_w.T + gate_d_b))
            theta = jnp.mean(jax.nn.sigmoid(x_mean @ gate_lr_w.T + gate_lr_b)) * MEM_LR
            eta = jnp.mean(jax.nn.sigmoid(x_mean @ gate_m_w.T + gate_m_b)) * MEM_MOM

            def loss_fn(ws):
                pred = _mem_fwd(keys, ws)
                return jnp.mean((pred - values) ** 2)
            g1, g2 = jax.grad(loss_fn)((mem_w1, mem_w2))
            s1 = eta * mom1 - theta * g1
            s2 = eta * mom2 - theta * g2
            nw1 = (1.0 - alpha) * mem_w1 + s1
            nw2 = (1.0 - alpha) * mem_w2 + s2
            output = retrieved @ w_out.T
            return (output, nw1, nw2, s1, s2)
        if __name__ == '__main__':
            out = reference(**setup_inputs())
            print([o.shape for o in out])
        key = jax.random.key(seed)
        ks = jax.random.split(key, 16)
        n = lambda k, shp: jax.random.normal(k, shp, jnp.float32) * 0.02
        inp = {'x': jax.random.normal(ks[0], (B, S, DIM), jnp.float32), 'w_k1': n(ks[1], (DIM, DIM)), 'w_k2': n(ks[2], (DIM, DIM)), 'w_v1': n(ks[3], (DIM, DIM)), 'w_v2': n(ks[4], (DIM, DIM)), 'w_q1': n(ks[5], (DIM, DIM)), 'w_q2': n(ks[6], (DIM, DIM)), 'conv_k_w': n(ks[7], (DIM, 1, K)), 'conv_k_b': jnp.zeros((DIM,), jnp.float32), 'conv_v_w': n(ks[8], (DIM, 1, K)), 'conv_v_b': jnp.zeros((DIM,), jnp.float32), 'conv_q_w': n(ks[9], (DIM, 1, K)), 'conv_q_b': jnp.zeros((DIM,), jnp.float32), 'gate_d_w': n(ks[10], (DIM, DIM)), 'gate_d_b': jnp.zeros((DIM,), jnp.float32), 'gate_lr_w': n(ks[11], (DIM, DIM)), 'gate_lr_b': jnp.zeros((DIM,), jnp.float32), 'gate_m_w': n(ks[12], (DIM, DIM)), 'gate_m_b': jnp.zeros((DIM,), jnp.float32), 'w_out': n(ks[13], (DIM, DIM)), 'mem_w1': n(ks[14], (HID, DIM)), 'mem_w2': n(ks[15], (DIM, HID)), 'mom1': jnp.zeros((HID, DIM), jnp.float32), 'mom2': jnp.zeros((DIM, HID), jnp.float32)}
        return inp
    _L0_attn_all = _L0_attn_setup()
    _L0_attn_in = {k: v for k, v in _L0_attn_all.items() if k in ('w_k1', 'w_k2', 'w_v1', 'w_v2', 'w_q1', 'w_q2', 'conv_k_w', 'conv_k_b', 'conv_v_w', 'conv_v_b', 'conv_q_w', 'conv_q_b', 'gate_d_w', 'gate_d_b', 'gate_lr_w', 'gate_lr_b', 'gate_m_w', 'gate_m_b', 'w_out', 'mem_w1', 'mem_w2', 'mom1', 'mom2')}
    del _L0_attn_all

    def _L0_ffn_setup():
        import jax, jax.numpy as jnp
        import numpy as np
        D_MODEL = 128
        D_FF = 512
        N_EXPERTS = 8
        TOP_K = 2
        key = jax.random.key(seed)
        ks = jax.random.split(key, 6)
        x = jax.random.normal(ks[0], (4, 256, D_MODEL), dtype=jnp.float32)
        router_w = jax.random.normal(ks[1], (N_EXPERTS, D_MODEL), dtype=jnp.float32) * 0.02
        lim1 = float(np.sqrt(6.0 / (D_FF + D_MODEL)))
        w1 = jax.random.uniform(ks[2], (N_EXPERTS, D_FF, D_MODEL), minval=-lim1, maxval=lim1, dtype=jnp.float32)
        b1 = jnp.zeros((N_EXPERTS, D_FF), dtype=jnp.float32)
        lim2 = float(np.sqrt(6.0 / (D_MODEL + D_FF)))
        w2 = jax.random.uniform(ks[3], (N_EXPERTS, D_MODEL, D_FF), minval=-lim2, maxval=lim2, dtype=jnp.float32)
        b2 = jnp.zeros((N_EXPERTS, D_MODEL), dtype=jnp.float32)
        return {'x': x, 'router_w': router_w, 'w1': w1, 'b1': b1, 'w2': w2, 'b2': b2}
    _L0_ffn_all = _L0_ffn_setup()
    _L0_ffn_in = {k: v for k, v in _L0_ffn_all.items() if k in ('router_w', 'w1', 'b1', 'w2', 'b2')}
    del _L0_ffn_all
    return {'x': x, 'txt': txt, 'L0_tok_W0': _L0_tok_in['W0'], 'L0_tok_as0': _L0_tok_in['as0'], 'L0_tok_ad0': _L0_tok_in['ad0'], 'L0_tok_bg0': _L0_tok_in['bg0'], 'L0_tok_R0': _L0_tok_in['R0'], 'L0_tok_g0': _L0_tok_in['g0'], 'L0_tok_b0': _L0_tok_in['b0'], 'L0_tok_W1': _L0_tok_in['W1'], 'L0_tok_as1': _L0_tok_in['as1'], 'L0_tok_ad1': _L0_tok_in['ad1'], 'L0_tok_bg1': _L0_tok_in['bg1'], 'L0_tok_R1': _L0_tok_in['R1'], 'L0_tok_g1': _L0_tok_in['g1'], 'L0_tok_b1': _L0_tok_in['b1'], 'L0_tok_W2': _L0_tok_in['W2'], 'L0_tok_as2': _L0_tok_in['as2'], 'L0_tok_ad2': _L0_tok_in['ad2'], 'L0_tok_bg2': _L0_tok_in['bg2'], 'L0_tok_R2': _L0_tok_in['R2'], 'L0_tok_g2': _L0_tok_in['g2'], 'L0_tok_b2': _L0_tok_in['b2'], 'L0_tok_fpW': _L0_tok_in['fpW'], 'L0_tok_fpb': _L0_tok_in['fpb'], 'L0_tok_fng': _L0_tok_in['fng'], 'L0_tok_fnb': _L0_tok_in['fnb'], 'L0_tok_edge_index': _L0_tok_in['edge_index'], 'L0_attn_w_k1': _L0_attn_in['w_k1'], 'L0_attn_w_k2': _L0_attn_in['w_k2'], 'L0_attn_w_v1': _L0_attn_in['w_v1'], 'L0_attn_w_v2': _L0_attn_in['w_v2'], 'L0_attn_w_q1': _L0_attn_in['w_q1'], 'L0_attn_w_q2': _L0_attn_in['w_q2'], 'L0_attn_conv_k_w': _L0_attn_in['conv_k_w'], 'L0_attn_conv_k_b': _L0_attn_in['conv_k_b'], 'L0_attn_conv_v_w': _L0_attn_in['conv_v_w'], 'L0_attn_conv_v_b': _L0_attn_in['conv_v_b'], 'L0_attn_conv_q_w': _L0_attn_in['conv_q_w'], 'L0_attn_conv_q_b': _L0_attn_in['conv_q_b'], 'L0_attn_gate_d_w': _L0_attn_in['gate_d_w'], 'L0_attn_gate_d_b': _L0_attn_in['gate_d_b'], 'L0_attn_gate_lr_w': _L0_attn_in['gate_lr_w'], 'L0_attn_gate_lr_b': _L0_attn_in['gate_lr_b'], 'L0_attn_gate_m_w': _L0_attn_in['gate_m_w'], 'L0_attn_gate_m_b': _L0_attn_in['gate_m_b'], 'L0_attn_w_out': _L0_attn_in['w_out'], 'L0_attn_mem_w1': _L0_attn_in['mem_w1'], 'L0_attn_mem_w2': _L0_attn_in['mem_w2'], 'L0_attn_mom1': _L0_attn_in['mom1'], 'L0_attn_mom2': _L0_attn_in['mom2'], 'L0_ffn_router_w': _L0_ffn_in['router_w'], 'L0_ffn_w1': _L0_ffn_in['w1'], 'L0_ffn_b1': _L0_ffn_in['b1'], 'L0_ffn_w2': _L0_ffn_in['w2'], 'L0_ffn_b2': _L0_ffn_in['b2']}

def reference(x, txt, L0_tok_W0, L0_tok_as0, L0_tok_ad0, L0_tok_bg0, L0_tok_R0, L0_tok_g0, L0_tok_b0, L0_tok_W1, L0_tok_as1, L0_tok_ad1, L0_tok_bg1, L0_tok_R1, L0_tok_g1, L0_tok_b1, L0_tok_W2, L0_tok_as2, L0_tok_ad2, L0_tok_bg2, L0_tok_R2, L0_tok_g2, L0_tok_b2, L0_tok_fpW, L0_tok_fpb, L0_tok_fng, L0_tok_fnb, L0_tok_edge_index, L0_attn_w_k1, L0_attn_w_k2, L0_attn_w_v1, L0_attn_w_v2, L0_attn_w_q1, L0_attn_w_q2, L0_attn_conv_k_w, L0_attn_conv_k_b, L0_attn_conv_v_w, L0_attn_conv_v_b, L0_attn_conv_q_w, L0_attn_conv_q_b, L0_attn_gate_d_w, L0_attn_gate_d_b, L0_attn_gate_lr_w, L0_attn_gate_lr_b, L0_attn_gate_m_w, L0_attn_gate_m_b, L0_attn_w_out, L0_attn_mem_w1, L0_attn_mem_w2, L0_attn_mom1, L0_attn_mom2, L0_ffn_router_w, L0_ffn_w1, L0_ffn_b1, L0_ffn_w2, L0_ffn_b2):
    import jax
    import jax.numpy as jnp

    def _L0_tok_ref(pose_seq, W0, as0, ad0, bg0, R0, g0, b0, W1, as1, ad1, bg1, R1, g1, b1, W2, as2, ad2, bg2, R2, g2, b2, fpW, fpb, fng, fnb, edge_index):
        import jax, jax.numpy as jnp
        import numpy as np
        J = 50
        HEADS = 4
        DIMS = [3, 64, 128, 64]
        POSE_DIM = 128
        B, T = (16, 128)

        def build_edge_index():
            e = []
            for i in range(J - 1):
                e.append((i, i + 1))
                e.append((i + 1, i))
            for i in range(J):
                e.append((i, i))
            e = sorted(e)
            return jnp.array(e, dtype=jnp.int32).T

        def _layer_norm(x, g, b, eps=1e-05):
            mu = jnp.mean(x, axis=-1, keepdims=True)
            var = jnp.mean(jnp.square(x - mu), axis=-1, keepdims=True)
            return (x - mu) * jax.lax.rsqrt(var + eps) * g + b

        def _gat(x, src, dst, W, a_s, a_d, bias):
            G, Jn, _ = x.shape
            H, C = a_s.shape
            h = (x @ W).reshape(G, Jn, H, C)
            es = jnp.einsum('gjhc,hc->gjh', h, a_s)[:, src]
            ed = jnp.einsum('gjhc,hc->gjh', h, a_d)[:, dst]
            e = jax.nn.leaky_relu(es + ed, 0.2)
            m = jnp.full((G, Jn, H), -jnp.inf, e.dtype).at[:, dst].max(e)
            m = jax.lax.stop_gradient(m)
            w = jnp.exp(e - m[:, dst])
            den = jnp.zeros((G, Jn, H), e.dtype).at[:, dst].add(w)
            alpha = w / den[:, dst]
            out = jnp.zeros((G, Jn, H, C), e.dtype).at[:, dst].add(alpha[..., None] * h[:, src])
            return out.reshape(G, Jn, H * C) + bias

        def _forward(pose_seq, layers, fpW, fpb, fng, fnb, edge_index):
            Bb, Tt = (pose_seq.shape[0], pose_seq.shape[1])
            x = pose_seq.reshape(Bb * Tt, J, 3)
            src, dst = (edge_index[0], edge_index[1])
            for W, a_s, a_d, bg, R, g, b in layers:
                h = _gat(x, src, dst, W, a_s, a_d, bg)
                res = x @ R
                x = jax.nn.gelu(_layer_norm(h + res, g, b), approximate=False)
            x = x.reshape(Bb * Tt, J * DIMS[-1]) @ fpW + fpb
            x = _layer_norm(x, fng, fnb)
            return x.reshape(Bb, Tt, POSE_DIM)
        layers = [(W0, as0, ad0, bg0, R0, g0, b0), (W1, as1, ad1, bg1, R1, g1, b1), (W2, as2, ad2, bg2, R2, g2, b2)]
        return _forward(pose_seq, layers, fpW, fpb, fng, fnb, edge_index)

    def _L0_attn_ref(x, w_k1, w_k2, w_v1, w_v2, w_q1, w_q2, conv_k_w, conv_k_b, conv_v_w, conv_v_b, conv_q_w, conv_q_b, gate_d_w, gate_d_b, gate_lr_w, gate_lr_b, gate_m_w, gate_m_b, w_out, mem_w1, mem_w2, mom1, mom2):
        import jax, jax.numpy as jnp
        import numpy as np
        B, S, DIM, HID, K = (4, 2048, 128, 256, 4)
        MEM_LR, MEM_MOM = (0.01, 0.9)
        EPS = 1e-12

        def _proj2(x, w1, w2):
            return jax.nn.silu(x @ w1.T) @ w2.T

        def _causal_dwconv(x, w, b):
            xp = jnp.pad(x, ((0, 0), (K - 1, 0), (0, 0)))
            kern = jnp.transpose(w, (2, 1, 0))
            out = jax.lax.conv_general_dilated(xp, kern, (1,), 'VALID', dimension_numbers=('NWC', 'WIO', 'NWC'), feature_group_count=x.shape[-1])
            return out + b

        def _l2norm(x):
            n = jnp.linalg.norm(x, axis=-1, keepdims=True)
            return x / jnp.maximum(n, EPS)

        def _mem_fwd(h, ws):
            for i, w in enumerate(ws):
                h = h @ w.T
                if i < len(ws) - 1:
                    h = jax.nn.silu(h)
            return h

        def _reference_tuple_inner(x, w_k1, w_k2, w_v1, w_v2, w_q1, w_q2, conv_k_w, conv_k_b, conv_v_w, conv_v_b, conv_q_w, conv_q_b, gate_d_w, gate_d_b, gate_lr_w, gate_lr_b, gate_m_w, gate_m_b, w_out, mem_w1, mem_w2, mom1, mom2):
            keys = _proj2(x, w_k1, w_k2)
            values = _proj2(x, w_v1, w_v2)
            queries = _proj2(x, w_q1, w_q2)
            keys = _causal_dwconv(keys, conv_k_w, conv_k_b)
            values = _causal_dwconv(values, conv_v_w, conv_v_b)
            queries = _causal_dwconv(queries, conv_q_w, conv_q_b)
            keys = _l2norm(jax.nn.silu(keys))
            values = jax.nn.silu(values)
            queries = _l2norm(jax.nn.silu(queries))
            retrieved = _mem_fwd(queries, (mem_w1, mem_w2))
            x_mean = jnp.mean(x, axis=1, keepdims=True)
            alpha = jnp.mean(jax.nn.sigmoid(x_mean @ gate_d_w.T + gate_d_b))
            theta = jnp.mean(jax.nn.sigmoid(x_mean @ gate_lr_w.T + gate_lr_b)) * MEM_LR
            eta = jnp.mean(jax.nn.sigmoid(x_mean @ gate_m_w.T + gate_m_b)) * MEM_MOM

            def loss_fn(ws):
                pred = _mem_fwd(keys, ws)
                return jnp.mean((pred - values) ** 2)
            g1, g2 = jax.grad(loss_fn)((mem_w1, mem_w2))
            s1 = eta * mom1 - theta * g1
            s2 = eta * mom2 - theta * g2
            nw1 = (1.0 - alpha) * mem_w1 + s1
            nw2 = (1.0 - alpha) * mem_w2 + s2
            output = retrieved @ w_out.T
            return (output, nw1, nw2, s1, s2)
        if __name__ == '__main__':
            out = reference(**setup_inputs())
            print([o.shape for o in out])
        return _reference_tuple_inner(x, w_k1, w_k2, w_v1, w_v2, w_q1, w_q2, conv_k_w, conv_k_b, conv_v_w, conv_v_b, conv_q_w, conv_q_b, gate_d_w, gate_d_b, gate_lr_w, gate_lr_b, gate_m_w, gate_m_b, w_out, mem_w1, mem_w2, mom1, mom2)[0]

    def _L0_ffn_ref(x, router_w, w1, b1, w2, b2):
        import jax, jax.numpy as jnp
        import numpy as np
        D_MODEL = 128
        D_FF = 512
        N_EXPERTS = 8
        TOP_K = 2
        router_logits = jnp.einsum('bnc,ec->bne', x, router_w)
        router_probs = jax.nn.softmax(router_logits, axis=-1)
        expert_weights, expert_indices = jax.lax.top_k(router_probs, TOP_K)
        expert_weights = expert_weights / (jnp.sum(expert_weights, axis=-1, keepdims=True) + 1e-09)
        hidden = jnp.einsum('bnc,edc->bned', x, w1) + b1
        hidden = jax.nn.gelu(hidden, approximate=False)
        expert_outputs = jnp.einsum('bned,ecd->bnec', hidden, w2) + b2
        idx = expert_indices[..., None]
        selected = jnp.take_along_axis(expert_outputs, idx, axis=2)
        output = jnp.sum(selected * expert_weights[..., None], axis=2)
        return output
    h = _L0_tok_ref(x, L0_tok_W0, L0_tok_as0, L0_tok_ad0, L0_tok_bg0, L0_tok_R0, L0_tok_g0, L0_tok_b0, L0_tok_W1, L0_tok_as1, L0_tok_ad1, L0_tok_bg1, L0_tok_R1, L0_tok_g1, L0_tok_b1, L0_tok_W2, L0_tok_as2, L0_tok_ad2, L0_tok_bg2, L0_tok_R2, L0_tok_g2, L0_tok_b2, L0_tok_fpW, L0_tok_fpb, L0_tok_fng, L0_tok_fnb, L0_tok_edge_index)
    h = jnp.concatenate([h, txt], axis=1)
    h = h + _L0_attn_ref(_layernorm(h, axis=-1), L0_attn_w_k1, L0_attn_w_k2, L0_attn_w_v1, L0_attn_w_v2, L0_attn_w_q1, L0_attn_w_q2, L0_attn_conv_k_w, L0_attn_conv_k_b, L0_attn_conv_v_w, L0_attn_conv_v_b, L0_attn_conv_q_w, L0_attn_conv_q_b, L0_attn_gate_d_w, L0_attn_gate_d_b, L0_attn_gate_lr_w, L0_attn_gate_lr_b, L0_attn_gate_m_w, L0_attn_gate_m_b, L0_attn_w_out, L0_attn_mem_w1, L0_attn_mem_w2, L0_attn_mom1, L0_attn_mom2)
    h = h + _L0_ffn_ref(_layernorm(h, axis=-1), L0_ffn_router_w, L0_ffn_w1, L0_ffn_b1, L0_ffn_w2, L0_ffn_b2)
    return h

_drawn_inputs = setup_inputs


def setup_inputs(seed=0):
    import zlib

    import numpy as np

    out = dict(_drawn_inputs(seed))
    spreads = {'L0_tok_bg0': (0.0, 0.1),
     'L0_tok_g0': (1.0, 0.2),
     'L0_tok_b0': (0.0, 0.1),
     'L0_tok_bg1': (0.0, 0.1),
     'L0_tok_g1': (1.0, 0.2),
     'L0_tok_b1': (0.0, 0.1),
     'L0_tok_bg2': (0.0, 0.1),
     'L0_tok_g2': (1.0, 0.2),
     'L0_tok_b2': (0.0, 0.1),
     'L0_tok_fpb': (0.0, 0.1),
     'L0_tok_fng': (1.0, 0.2),
     'L0_tok_fnb': (0.0, 0.1),
     'L0_attn_conv_k_b': (0.0, 0.1),
     'L0_attn_conv_v_b': (0.0, 0.1),
     'L0_attn_conv_q_b': (0.0, 0.558),
     'L0_attn_gate_d_b': (0.0, 0.1),
     'L0_attn_gate_lr_b': (0.0, 0.1),
     'L0_attn_gate_m_b': (0.0, 0.1),
     'L0_attn_mom1': (0.0, 0.1),
     'L0_attn_mom2': (0.0, 0.1),
     'L0_ffn_b1': (0.0, 0.1),
     'L0_ffn_b2': (0.0, 0.1)}
    factors = {'L0_attn_w_q1': 8.0,
     'L0_attn_w_q2': 8.0,
     'L0_attn_conv_q_w': 8.0,
     'L0_attn_w_out': 6.415,
     'L0_attn_mem_w1': 5.625,
     'L0_attn_mem_w2': 8.0}
    for name, (base, spread) in spreads.items():
        noise = np.random.default_rng([zlib.crc32(name.encode()), seed]).standard_normal(out[name].shape)
        drawn = base * np.exp(spread * noise) if base else spread * noise
        out[name] = jnp.asarray(drawn.astype(out[name].dtype))
    for name, factor in factors.items():
        out[name] = (out[name] * factor).astype(out[name].dtype)
    return out
```

```python
import numpy as np
import concourse.bass as bass
from concourse import mybir
from contextlib import ExitStack

G, J, DIN = 4096, 50, 3
HEADS = 4
F0, F1, F2 = 64, 128, 64
P = 128
GH = 2
STEPS = G // (P * GH)
CJ = 4
NCH = (J + CJ - 1) // CJ
NCOL = CJ * P
JP = NCH * CJ
JS = 10
AR = 3 * JS * HEADS
NT = [NCH, GH * NCH, NCH]
T0 = [0, NCH, 3 * NCH]
TASKS = 4 * NCH
AGG = TASKS - NCH
TOK = GH * 2 * P
E, FF = 8, 512
MT = FF // P
HID = 256
VR = GH * NCH
RR = 64 + VR
NEG = -3.0e38
EPS = 1e-5


def joints(c):
    return min(CJ, J - CJ * c)


def task(l, n):
    return (n // GH, n % GH) if l == 1 else (n, None)


def build(nc, A, out):
    fp32, bf16, i32, u32 = mybir.dt.float32, mybir.dt.bfloat16, mybir.dt.int32, mybir.dt.uint32
    ALU, ACT = mybir.AluOpType, mybir.ActivationFunctionType
    ctx = ExitStack()
    with ctx:
        def sb(name, shape, dt=fp32):
            return ctx.enter_context(nc.sbuf_tensor(name, shape, dt))

        def sem(name):
            return ctx.enter_context(nc.semaphore(name))

        consts = {}

        def const(name):
            consts[name] = sb("c_" + name, list(A[name].shape))[:]
            return consts[name]

        X2 = sb("X2", [P, GH, J * P])
        X2f = X2[:].rearrange("p a n -> p (a n)")
        setup_at = [0]

        def setup_const(name):
            p, n = A[name].shape
            consts[name] = X2f[0:p, setup_at[0]:setup_at[0] + n]
            setup_at[0] += n
            return consts[name]

        W0T, abd0 = setup_const("W0T"), setup_const("abd0")
        raw0 = setup_const("raw0")
        W1T, R1T, abd1, W1 = setup_const("W1T"), setup_const("R1T"), setup_const("abd1"), const("W1")
        W2T, R2T, abd2, W2 = setup_const("W2T"), setup_const("R2T"), setup_const("abd2"), const("W2")
        C1, C2, ones, ident = (const(n) for n in ("C1", "C2", "ones", "ident"))
        V1, V2 = const("V1"), const("V2")
        sel1f, sel2f = setup_const("sel1"), setup_const("sel2")
        selr1f, selr2f = setup_const("selr1"), setup_const("selr2")
        vec = const("vec")
        rows = const("rows")
        fpW = const("fpW")
        wq1, wq2, mw1, mw2, wout = (const(n) for n in ("wq1", "wq2", "mw1", "mw2", "wout"))
        rw, w1, w2, b2 = const("rw"), const("w1"), const("w2"), const("b2")
        iota8 = const("iota8")
        VEC = {n: k for k, n in enumerate(["bg1", "bg2", "g0", "b0", "g1", "b1", "g2", "b2",
                                           "cb", "cw0", "cw1", "cw2", "cw3"])}
        FB1 = len(VEC)

        def v(name):
            return vec[:, VEC[name]:VEC[name] + 1]

        A0b = sb("A0b", [P, DIN, 8])
        A1 = sb("A1", [P, 8])
        A2 = sb("A2", [P, 8])
        WR1 = sb("WR1", [P, F1])
        WR2 = sb("WR2", [P, F2])
        W0bd = sb("W0bd", [P, CJ, P])
        bgc = sb("bgc", [P, 2])
        sel1 = sb("sel1b", [AR, JS, P], bf16)
        sel2 = sb("sel2b", [AR, JS, F2], bf16)
        selr1 = sb("selr1b", [RR, GH * NCH, P], bf16)
        selr2 = sb("selr2b", [RR, NCH, P], bf16)
        identb = sb("identb", [P, P], bf16)

        X0 = sb("X0", [P, GH, J, DIN])
        dX0 = sb("dX0", [P, GH, J + 1, DIN])
        N4 = GH * JP * HEADS
        NS = GH * (JP + 2) * 8
        R = sb("R", [P, 2 * NS + 6 * N4])
        DX = R[:, 0:2 * NCOL].rearrange("p (a n) -> p a n", a=2)
        DR = R[:, 2 * NCOL:6 * NCOL].rearrange("p (g a n) -> p g a n", g=GH, a=2)
        TA = R[:, 6 * NCOL:8 * NCOL].rearrange("p (a n) -> p a n", a=2)
        S = R[:, 0:NS].rearrange("p (a j r) -> p a j r", a=GH, r=8)
        S2 = R[:, NS:2 * NS].rearrange("p (a j r) -> p a j r", a=GH, r=8)
        Res = R[:, NS:NS + 2 * N4].rearrange("p (a n) -> p a n", a=2)
        Fb = R[:, 2 * NS:2 * NS + 3 * N4].rearrange("p (a n) -> p a n", a=3)
        Tc = R[:, 2 * NS:2 * NS + 12 * J].rearrange("p (j r) -> p j r", j=J)
        Td = R[:, 2 * NS + 12 * J:2 * NS + 24 * J].rearrange("p (j r) -> p j r", j=J)
        Mx = R[:, 2 * NS + 3 * N4:2 * NS + 4 * N4]
        Al = R[:, 2 * NS + 4 * N4:2 * NS + 6 * N4].rearrange("p (a n) -> p a n", a=2)
        Pt = sb("Pt", [P, 4 * CJ, 2, 3, JS * HEADS], bf16)
        AT = sb("AT", [AR, 2, GH, 2 * CJ * P], bf16)
        NY = GH * NCH * CJ * 16
        Y = X2f[:, NCH * P:NCH * P + NY].rearrange("p (c a j r) -> p c a j r", c=NCH, a=GH, r=16)
        YT = X2f[:, 0:NCH * P]
        X1 = sb("X1", [P, (J + 1) * P])
        HS = [R[:, k * NCOL:(k + 1) * NCOL] for k in (0, 1, 4)]
        TB = sb("TB", [P, NCOL])

        def edge_scores(l):
            at = X2f[:, 2 * MT * TOK:2 * MT * TOK + 3 * N4] if l < 2 else X1[:, 0:3 * N4]
            return at.rearrange("p (k a n) -> p k a n", k=3, a=GH)

        SQ = sb("SQ", [P, 2, NCOL])
        VB = TA[0:VR, 0, :]
        RV = TB[0:VR, :]
        RN = DR[0:VR, 0, 1, :]
        RM = DR[0:VR, 0, 0, 0:NCOL // 2].bitcast(bf16)
        RP = sb("RP", [RR, NCOL], bf16)
        mhalf = sb("mhalf", [P, 1])
        carrier = sb("carrier", [P, 2])
        Hf = sb("Hf", [P, 4, P])
        Ho = sb("Ho", [P, 4, P])
        Xn = R[:, NCOL:2 * NCOL].rearrange("p (t d) -> p t d", t=4)
        st = sb("st", [P, 4, 6])
        mv = sb("mv", [P, 4, 2])
        rs, rv, rt = sb("rs", [P, 4]), sb("rv", [P, 4]), sb("rt", [P, 4])
        XT = R[:, 0:TOK]
        Q1, QD, KN, GT = (X1[:, k * NCOL:(k + 1) * NCOL] for k in range(4))
        NV, NR = VB[0:1, :], RV[0:1, :]
        QC = sb("QC", [P, GH, 3 + 2 * P])
        QS = SQ[:, 0, :]
        MH = TA
        RT = TB[:]
        LG = sb("LG", [P, 4, 8])
        PB = sb("PB", [P, 4, 8])
        mx4 = sb("mx4", [P, 4])
        den4 = sb("den4", [P, 4])
        top = sb("top", [P, 4, 8])
        tix = sb("tix", [P, 4, 8], u32)
        tif = sb("tif", [P, 4, 8])
        gw = sb("gw", [P, 4, 2])
        gate = sb("gate", [P, 4, 8])
        gtmp = sb("gtmp", [P, 4, 8])
        HD = X2f[:, 0:2 * MT * TOK].rearrange("p (a m t) -> p a m t", a=2, m=MT)

        bank = [ctx.enter_context(nc.psum_tensor(f"bank{i}", [P, NCOL], fp32)) for i in range(8)]
        bD, bV = bank[0], bank[5]
        bA = [[bank[1], bank[2]], [bank[6], bank[7]]]
        bZ = [bank[3], bank[4]]

        c_loaded = sem("c_loaded")
        setup_ps = sem("setup_ps")
        setup_sb = sem("setup_sb")
        seeded = sem("seeded")
        x0_in = sem("x0_in")
        txt_in = sem("txt_in")
        s_ps = sem("s_ps")
        s_sb = sem("s_sb")
        f_ok = sem("f_ok")
        exp_ok = sem("exp_ok")
        parts_ok = sem("parts_ok")
        at_ps = sem("at_ps")
        at_act = sem("at_act")
        at_dve = sem("at_dve")
        y_pad = sem("y_pad")
        y_ok = sem("y_ok")
        yt_ps = sem("yt_ps")
        yt_sb = sem("yt_sb")
        a_ps = sem("a_ps")
        d_ps = sem("d_ps")
        d_sb = sem("d_sb")
        t_ok = sem("t_ok")
        z_ps = sem("z_ps")
        zs_ok = sem("zs_ok")
        sq_ok = sem("sq_ok")
        v_ps = sem("v_ps")
        var_ok = sem("var_ok")
        sd_ok = sem("sd_ok")
        rp_ok = sem("rp_ok")
        r_ps = sem("r_ps")
        u_ok = sem("u_ok")
        x_ok = sem("x_ok")
        dx_ok = sem("dx_ok")
        fp_ps = sem("fp_ps")
        h_ok = sem("h_ok")
        xt_ps = sem("xt_ps")
        xt_sb = sem("xt_sb")
        q1_ps = sem("q1_ps")
        q1_sb = sem("q1_sb")
        q2_ps = sem("q2_ps")
        q2_sb = sem("q2_sb")
        cv_ok = sem("cv_ok")
        cs_self = sem("cs_self")
        cs_ok = sem("cs_ok")
        ss_ps = sem("ss_ps")
        nv_ok = sem("nv_ok")
        nsd_ok = sem("nsd_ok")
        nr_ok = sem("nr_ok")
        nb_ps = sem("nb_ps")
        kn_ok = sem("kn_ok")
        mh_ps = sem("mh_ps")
        mh_sb = sem("mh_sb")
        rt_ps = sem("rt_ps")
        rt_sb = sem("rt_sb")
        o_ps = sem("o_ps")
        ho_ok = sem("ho_ok")
        lg_ps = sem("lg_ps")
        lgm_ok = sem("lgm_ok")
        rexp_ok = sem("rexp_ok")
        gate_ok = sem("gate_ok")
        gt_ps = sem("gt_ps")
        gt_sb = sem("gt_sb")
        bo_ps = sem("bo_ps")
        hid_ps = sem("hid_ps")
        hid_sb = sem("hid_sb")
        eo_ps = sem("eo_ps")
        acc_ok = sem("acc_ok")
        stored = sem("stored")
        dve_link = sem("dve_link")

        block = ctx.enter_context(nc.Block())
        NCONST = len(consts)

        @block.sync
        def _(sp):
            for primed in (y_ok, ho_ok, eo_ps, d_ps, acc_ok, hid_sb, t_ok, stored):
                sp.sem_inc(primed, 1)
            for name, t in consts.items():
                sp.dma_start(t, A[name]).then_inc(c_loaded, 16)
            with sp.Fori(0, STEPS) as s:
                sp.wait_ge(y_ok, s + 1)
                for gh in range(GH):
                    sp.dma_start(X0[:, gh, :, :], A["x"][s, gh]).then_inc(x0_in, 16)
                sp.wait_ge(ho_ok, s + 1)
                for gh in range(GH):
                    sp.dma_start(Hf[:, 2 * gh + 1, :], A["txt"][s, gh]).then_inc(txt_in, 16)

        @block.gpsimd
        def _(pool):
            nc.gpsimd.memset(dX0[:], 0.0)
            nc.gpsimd.memset(RP[:], 0.0)
            nc.gpsimd.memset(mhalf[:], -0.5)
            nc.gpsimd.memset(Pt[:], 0.0)
            nc.gpsimd.memset(X1[:, J * P:], 0.0)
            nc.gpsimd.memset(QC[:], 0.0).then_inc(seeded, 1)
            pool.wait_ge(seeded, 1)
            pool.wait_ge(setup_sb, 2)
            with pool.Fori(0, STEPS) as s:
                pool.wait_ge(eo_ps, s * E + 1)
                nc.gpsimd.tensor_tensor(carrier[:, 0:1], mhalf[:], mhalf[:], ALU.add)
                nc.gpsimd.memset(Y[:].rearrange("p c a j r -> p (c a j r)"), 1.0).then_inc(y_pad, 1)

                pool.wait_ge(parts_ok, s * 2 + 1)
                for c in range(NCH):
                    n = joints(c) * P
                    last = min(NCH - 1, (CJ * c + joints(c)) // CJ)
                    pool.wait_ge(x_ok, s * TASKS + last + 1)
                    if c >= 2:
                        pool.wait_ge(d_ps, s * AGG + GH * (c - 1) + 1)
                    else:
                        pool.wait_ge(d_ps, s * AGG + 1)
                    o = c * NCOL
                    nc.gpsimd.tensor_tensor(DX[:, c % 2, 0:n], X1[:, o + P:o + P + n], X1[:, o:o + n],
                                            ALU.subtract).then_inc(dx_ok, 1)

        @block.tensor
        def _(pe):
            pe.wait_ge(c_loaded, 16 * NCONST)
            mm = nc.tensor.matmul
            for d in range(DIN):
                mm(bank[0][:, 8 * d:8 * d + 8], W0T[:, d:d + 1].to_broadcast([F0, P]), abd0[:], start=True, stop=True)
            mm(bank[0][:, 32:40], W1T[:], abd1[:], start=True, stop=True)
            mm(bank[0][:, 40:48], W2T[:], abd2[:], start=True, stop=True)
            mm(bank[0][:, 48:49], C1[:], v("bg1"), start=True, stop=True)
            mm(bank[0][:, 49:50], C2[:], v("bg2"), start=True, stop=True)
            mm(bank[1][:, 0:F1], W1T[:], C1[:], start=True, stop=False)
            mm(bank[1][:, 0:F1], R1T[:], C1[:], start=False, stop=True)
            mm(bank[2][:, 0:F2], W2T[:], C2[0:F2, 0:F2], start=True, stop=False)
            mm(bank[2][:, 0:F2], R2T[:], C2[0:F2, 0:F2], start=False, stop=True)
            for q in range(CJ * GH):
                last = mm(bank[3][:, F0 * q:F0 * q + F0], raw0[:, P * q:P * q + P], C2[0:F0, 0:F0], start=True, stop=True)
            last.then_inc(setup_ps, 1)
            pe.wait_ge(setup_sb, 2)
            with pe.Fori(0, STEPS) as s:
                pe.wait_ge(y_ok, s + 2)
                pe.wait_ge(acc_ok, s * E + 1)
                pe.wait_ge(hid_sb, s * E * MT + 1)
                for b in range(4):
                    for c in range(4 * b, min(4 * b + 4, NCH)):
                        last = nc.tensor.transpose(bank[4 + b][:, (c - 4 * b) * P:(c - 4 * b + 1) * P],
                                                   Y[:, c, :, :, :].rearrange("p a j r -> p (a j r)"), ident)
                    last.then_inc(yt_ps, 1)
                for l in range(3):
                    base, a0 = T0[l], T0[l] - NCH
                    if l == 0:
                        pe.wait_ge(yt_sb, s * 4 + 4)
                    else:
                        pe.wait_ge(x_ok, s * TASKS + base)
                        for j in range(J):
                            for gh in range(GH):
                                if l == 1:
                                    lhs, rhs = X1[64 * gh:64 * gh + 64, j * P:j * P + P], A1[64 * gh:64 * gh + 64, :]
                                else:
                                    lhs, rhs = X2[:, gh, j * P:j * P + P], A2[:]
                                last = mm(bank[6 + gh][:, 8 * j:8 * j + 8], lhs, rhs, start=True, stop=True)
                        last.then_inc(s_ps, 1)
                        pe.wait_ge(parts_ok, s * 2 + l)
                        pe.wait_ge(v_ps, s * TASKS + base)
                        for k in range(4):
                            sign, gh = k // 2, k % 2
                            atp = bank[k][:].bitcast(bf16)
                            for t in range(2):
                                for q in range(CJ):
                                    src = Pt[:, k * CJ + q, t, :, :].rearrange("p k n -> p (k n)")
                                    o = (t * CJ + q) * P
                                    last = nc.tensor.transpose(atp[0:AR, o:o + P], src, identb[:])
                            last.then_inc(at_ps, 1)
                        pe.wait_ge(at_act, s * 4 + 2 * l)
                        pe.wait_ge(at_dve, s * 4 + 2 * l)

                    def product_d(n):
                        c, gh = task(l, n)
                        k, cols = a0 + n, joints(c) * P
                        o = c * NCOL
                        if k > 0:
                            pe.wait_ge(d_sb, s * AGG + k)
                        if l == 1:
                            pe.wait_ge(dx_ok, s * NCH + c + 1)
                            mm(bD[:, 0:cols], W1[64 * gh:64 * gh + 64, :], DX[64 * gh:64 * gh + 64, c % 2, 0:cols],
                               start=True, stop=True).then_inc(d_ps, 1)
                        else:
                            mm(bD[0:64, 0:cols], W2[:], X2[:, 0, o:o + cols], start=True, stop=True)
                            mm(bD[64:128, 0:cols], W2[:], X2[:, 1, o:o + cols], start=True, stop=True)\
                                .then_inc(d_ps, 1)

                    def spread_alpha(n):
                        c, gh = task(l, n)
                        k, cols = a0 + n, joints(c) * P
                        if k >= 2:
                            pe.wait_ge(t_ok, s * AGG + k)
                        o = (c // JS) * NCOL
                        for sign in range(2):
                            b = bA[k % 2][sign]
                            if l == 1:
                                last = mm(b[:, 0:cols], sel1[:, c % JS, :], AT[:, sign, gh, o:o + cols], start=True, stop=True)
                            else:
                                for g in range(GH):
                                    last = mm(b[64 * g:64 * g + 64, 0:cols], sel2[:, c % JS, :],
                                              AT[:, sign, g, o:o + cols], start=True, stop=True)
                        last.then_inc(a_ps, 1)

                    def centred(n):
                        c, gh = task(l, n)
                        k, cols = base + n, joints(c) * P
                        o = c * NCOL
                        z = bZ[k % 2]
                        if k >= 2:
                            pe.wait_ge(zs_ok, s * TASKS + k - 1)
                            pe.wait_ge(sq_ok, s * TASKS + k - 1)
                        if l == 0:
                            for j in range(joints(c)):
                                last = mm(z[:, j * P:j * P + P], W0bd[:, j, :], YT[:, c * P:c * P + P], start=True, stop=True)
                        elif l == 1:
                            mm(z[:, 0:cols], WR1[64 * gh:64 * gh + 64, :], X1[64 * gh:64 * gh + 64, o:o + cols],
                               start=True, stop=False)
                            pe.wait_ge(t_ok, s * AGG + k - NCH + 2)
                            last = mm(z[:, 0:cols], C1[:], TA[:, (k - NCH) % 2, 0:cols], start=False, stop=True)
                        else:
                            for g in range(GH):
                                mm(z[64 * g:64 * g + 64, 0:cols], WR2[:], X2[:, g, o:o + cols], start=True, stop=False,
                                   skip_group_check=True)
                            pe.wait_ge(t_ok, s * AGG + k - NCH + 2)
                            last = mm(z[:, 0:cols], C2[:], TA[:, (k - NCH) % 2, 0:cols], start=False, stop=True,
                                      skip_group_check=True)
                        last.then_inc(z_ps, 1)

                    def variance(n):
                        c, gh = task(l, n)
                        k, cols = base + n, joints(c) * P
                        pe.wait_ge(sq_ok, s * TASKS + k + 1)
                        row = c if gh is None else gh * NCH + c
                        mm(bV[0:VR, 0:cols], (V1 if l == 1 else V2)[:, VR - 1 - row:2 * VR - 1 - row], SQ[:, k % 2, 0:cols],
                           start=(n == 0), stop=(n == NT[l] - 1), skip_group_check=True).then_inc(v_ps, 1)

                    def spread_rstd(n):
                        c, gh = task(l, n)
                        k, cols = base + n, joints(c) * P
                        if n >= 4:
                            pe.wait_ge(u_ok, s * TASKS + k - 3)
                        sel = selr2[:, c, :] if gh is None else selr1[:, gh * NCH + c, :]
                        mm(bA[n % 2][n // 2 % 2][:, 0:cols], sel, RP[:, 0:cols], start=True, stop=True)\
                            .then_inc(r_ps, 1)

                    if l == 2:
                        product_d(0)
                    for n in range(NT[l] + 2):
                        if l and n < NT[l]:
                            spread_alpha(n)
                            if l == 1:
                                product_d(n)
                            elif n + 1 < NT[l]:
                                product_d(n + 1)
                        if 1 <= n <= NT[l]:
                            centred(n - 1)
                        if n >= 2:
                            variance(n - 2)
                    pe.wait_ge(rp_ok, s * 3 + l + 1)
                    for n in range(NT[l]):
                        spread_rstd(n)
                pe.wait_ge(x_ok, s * TASKS + TASKS)
                for j in range(J):
                    for gh in range(GH):
                        r = slice(64 * gh, 64 * gh + 64)
                        last = mm(bank[gh][:, 0:P], X1[r, j * P:j * P + P], fpW[r, j * P:j * P + P],
                                  start=(j == 0), stop=(j == J - 1))
                last.then_inc(fp_ps, 1)
                pe.wait_ge(h_ok, s + 1)
                for t in range(4):
                    last = nc.tensor.transpose(bank[1][:, t * P:t * P + P], Xn[:, t, :], ident[:])
                last.then_inc(xt_ps, 1)
                pe.wait_ge(xt_sb, s * 2 + 1)
                mm(bank[2][:], wq1[:], XT[:], start=True, stop=True).then_inc(q1_ps, 1)
                pe.wait_ge(q1_sb, s + 1)
                mm(bank[3][:], wq2[:], Q1, start=True, stop=True).then_inc(q2_ps, 1)
                pe.wait_ge(cs_ok, s + 1)
                mm(bank[4][0:1, :], ones[:, 0:1], QS, start=True, stop=True).then_inc(ss_ps, 1)
                pe.wait_ge(nr_ok, s + 1)
                mm(bank[5][:], ones[0:1, :], NR, start=True, stop=True).then_inc(nb_ps, 1)
                pe.wait_ge(kn_ok, s + 1)
                for m in range(2):
                    mm(bank[6 - m][:], mw1[:, m * P:m * P + P], KN, start=True, stop=True).then_inc(mh_ps, 1)
                pe.wait_ge(mh_sb, s * 2 + 2)
                for m in range(2):
                    last = mm(bank[7][:], mw2[:, m * P:m * P + P], MH[:, m, :], start=(m == 0), stop=(m == 1))
                last.then_inc(rt_ps, 1)
                pe.wait_ge(rt_sb, s + 1)
                for t in range(4):
                    last = mm(bank[0][:, t * P:t * P + P], RT[:, t * P:t * P + P], wout[:], start=True, stop=True)
                last.then_inc(o_ps, 1)
                pe.wait_ge(ho_ok, s + 2)
                for t in range(4):
                    last = nc.tensor.transpose(bank[1][:, t * P:t * P + P], Xn[:, t, :], ident[:])
                last.then_inc(xt_ps, 1)
                pe.wait_ge(xt_sb, s * 2 + 2)
                for t in range(4):
                    last = mm(bank[2][:, 8 * t:8 * t + 8], XT[:, t * P:t * P + P], rw[:], start=True, stop=True)
                last.then_inc(lg_ps, 1)

                def up(e):
                    for m in range(MT):
                        k = e * MT + m
                        if k >= 4:
                            pe.wait_ge(hid_sb, s * E * MT + k - 2)
                        mm(bank[4 + k % 4][:], w1[:, (e * MT + m) * P:(e * MT + m + 1) * P], XT[:], start=True, stop=True)\
                            .then_inc(hid_ps, 1)

                def down(e):
                    pe.wait_ge(hid_sb, s * E * MT + (e + 1) * MT + 1)
                    if e >= 2:
                        pe.wait_ge(acc_ok, s * E + e)
                    for t in range(4):
                        b = bank[e % 2][:, t * P:t * P + P]
                        for m in range(MT):
                            last = mm(b, HD[:, e % 2, m, t * P:t * P + P], w2[:, (e * MT + m) * P:(e * MT + m + 1) * P],
                               start=(m == 0), stop=(m == MT - 1))
                    last.then_inc(eo_ps, 1)

                up(0)
                for e in range(E):
                    if e + 1 < E:
                        up(e + 1)
                    if e == 0:
                        pe.wait_ge(gate_ok, s + 1)
                        for t in range(4):
                            last = nc.tensor.transpose(bank[3][0:E, t * P:t * P + P], gate[:, t, :], ident)
                        last.then_inc(gt_ps, 1)
                        pe.wait_ge(gt_sb, s + 1)
                        for t in range(4):
                            last = mm(bank[2][:, t * P:t * P + P], GT[0:E, t * P:t * P + P], b2, start=True, stop=True)
                        last.then_inc(bo_ps, 1)
                    down(e)

        @block.scalar
        def _(act):
            A_ = nc.scalar.activation
            act.wait_ge(setup_ps, 1)
            A_(W0bd[:].rearrange("p j f -> p (j f)"), bank[3][:], ACT.Copy)
            A_(sel1[:].rearrange("p j f -> p (j f)"), sel1f[:], ACT.Copy)
            A_(sel2[:].rearrange("p j f -> p (j f)"), sel2f[:], ACT.Copy)
            A_(selr1[:].rearrange("p j f -> p (j f)"), selr1f[:], ACT.Copy)
            A_(selr2[:].rearrange("p j f -> p (j f)"), selr2f[:], ACT.Copy)
            A_(identb[:], ident[:], ACT.Copy).then_inc(setup_sb, 1)
            with act.Fori(0, STEPS) as s:
                for l in range(3):
                    base, a0 = T0[l], T0[l] - NCH
                    if l:
                        act.wait_ge(s_ps, s * 2 + l)
                        for gh in range(GH):
                            last = A_(S[:, gh, 1:J + 1, :].rearrange("p j r -> p (j r)"), bank[6 + gh][:, 0:8 * J], ACT.Copy)
                        last.then_inc(s_sb, 1)
                    act.wait_ge(f_ok, s * 3 + l + 1)
                    A_(Fb[:].rearrange("p k n -> p (k n)"), Fb[:].rearrange("p k n -> p (k n)"), ACT.Exp)\
                        .then_inc(exp_ok, 1)
                    if l:
                        for k in range(2):
                            act.wait_ge(at_ps, s * 8 + 4 * (l - 1) + k + 1)
                            A_(AT[:, 0, k, :], bank[k][0:AR, :].bitcast(bf16), ACT.Copy).then_inc(at_act, 1)
                    else:
                        for b in range(4):
                            act.wait_ge(yt_ps, s * 4 + b + 1)
                            n = min(4, NCH - 4 * b) * P
                            A_(YT[:, 4 * b * P:4 * b * P + n], bank[4 + b][:, 0:n], ACT.Copy).then_inc(yt_sb, 1)

                    def take_d(n):
                        c, gh = task(l, n)
                        k, cols = a0 + n, joints(c) * P
                        act.wait_ge(d_ps, s * AGG + k + 2)
                        if l == 1:
                            if n >= 2:
                                act.wait_ge(t_ok, s * AGG + k)
                            A_(DR[:, gh, c % 2, 0:cols], bD[:, 0:cols], ACT.Copy).then_inc(d_sb, 1)
                        else:
                            if n >= 3:
                                act.wait_ge(t_ok, s * AGG + k - 1)
                            A_(HS[c % 3][:, 0:cols], bD[:, 0:cols], ACT.Copy).then_inc(d_sb, 1)

                    def square(n):
                        c, gh = task(l, n)
                        k, cols = base + n, joints(c) * P
                        act.wait_ge(z_ps, s * TASKS + k + 1)
                        if k >= 2:
                            act.wait_ge(v_ps, s * TASKS + k - 1)
                        bias = bgc[:, l - 1:l] if l else 0.0
                        o = c * NCOL
                        dst = X2[:, gh, o:o + cols] if l == 1 else X1[:, o:o + cols]
                        A_(dst, bZ[k % 2][:, 0:cols], ACT.Identity, bias=bias).then_inc(zs_ok, 1)
                        A_(SQ[:, k % 2, 0:cols], bZ[k % 2][:, 0:cols], ACT.Square, bias=bias).then_inc(sq_ok, 1)

                    def gelu(n):
                        c, gh = task(l, n)
                        k, cols = base + n, joints(c) * P
                        o = c * NCOL
                        act.wait_ge(u_ok, s * TASKS + k + 1)
                        dst = X2[:, gh, o:o + cols] if l == 1 else X1[:, o:o + cols]
                        A_(dst, dst, ACT.Gelu, bias=v(f"b{l}"), scale=v(f"g{l}"))\
                            .then_inc(x_ok, 1)

                    if l == 2:
                        take_d(0)
                    for n in range(NT[l] + 1):
                        if l == 1 and n < NT[l]:
                            take_d(n)
                        if l == 2 and n + 1 < NT[l]:
                            take_d(n + 1)
                        if 1 <= n <= NT[l]:
                            square(n - 1)
                    act.wait_ge(var_ok, s * 3 + l + 1)
                    A_(RV, VB, ACT.Sqrt).then_inc(sd_ok, 1)
                    for n in range(NT[l]):
                        gelu(n)
                act.wait_ge(xt_ps, s * 2 + 1)
                A_(XT[:], bank[1][:], ACT.Copy).then_inc(xt_sb, 1)
                act.wait_ge(q1_ps, s + 1)
                A_(Q1, bank[2][:], ACT.Silu).then_inc(q1_sb, 1)
                act.wait_ge(q2_ps, s + 1)
                A_(QC[:, :, 3:], bank[3][:].rearrange("p (b t) -> p b t", b=GH), ACT.Copy).then_inc(q2_sb, 1)
                act.wait_ge(cv_ok, s + 1)
                A_(QD, QD, ACT.Silu, bias=v("cb")).then_inc(cs_self, 1)
                act.wait_ge(cs_self, s + 1)
                A_(QS, QD, ACT.Square).then_inc(cs_ok, 1)
                act.wait_ge(nv_ok, s + 1)
                A_(NR, NV, ACT.Sqrt).then_inc(nsd_ok, 1)
                for m in range(2):
                    act.wait_ge(mh_ps, s * 2 + m + 1)
                    A_(MH[:, m, :], bank[6 - m][:], ACT.Silu).then_inc(mh_sb, 1)
                act.wait_ge(rt_ps, s + 1)
                A_(RT[:], bank[7][:], ACT.Copy).then_inc(rt_sb, 1)
                act.wait_ge(xt_ps, s * 2 + 2)
                A_(XT[:], bank[1][:], ACT.Copy).then_inc(xt_sb, 1)
                act.wait_ge(lgm_ok, s + 1)
                A_(LG[:].rearrange("p t e -> p (t e)"), LG[:].rearrange("p t e -> p (t e)"), ACT.Exp)\
                    .then_inc(rexp_ok, 1)
                for k in range(E * MT):
                    e, m = k // MT, k % MT
                    if k == 2 * MT:
                        act.wait_ge(gt_ps, s + 1)
                        A_(GT[0:E, :], bank[3][0:E, :], ACT.Copy).then_inc(gt_sb, 1)
                    act.wait_ge(hid_ps, s * E * MT + k + 1)
                    if e >= 2 and m == 0:
                        act.wait_ge(eo_ps, s * E + e)
                    A_(HD[:, e % 2, m, :], bank[4 + k % 4][:], ACT.Gelu,
                       bias=vec[:, FB1 + k:FB1 + k + 1]).then_inc(hid_sb, 1)
                act.wait_ge(acc_ok, s * E + E + 1)
                for gh in range(GH):
                    act.dma_start(out[s, gh].rearrange("h p d -> p h d"), Ho[:, 2 * gh:2 * gh + 2, :])\
                        .then_inc(stored, 16)
            act.wait_ge(stored, STEPS * 32 + 1)

        @block.vector
        def _(dve):
            TT, TS, STT = nc.vector.tensor_tensor, nc.vector.tensor_scalar, nc.vector.scalar_tensor_tensor
            LINKS = 193
            links = [0]
            dve.wait_ge(setup_ps, 1)
            nc.vector.tensor_copy(A0b[:].rearrange("p d r -> p (d r)"), bank[0][:, 0:24])
            nc.vector.tensor_copy(A1[:], bank[0][:, 32:40])
            nc.vector.tensor_copy(A2[:], bank[0][:, 40:48])
            nc.vector.tensor_copy(bgc[:], bank[0][:, 48:50])
            nc.vector.tensor_copy(WR1[:], bank[1][:, 0:F1])
            nc.vector.tensor_copy(WR2[:], bank[2][:, 0:F2]).then_inc(setup_sb, 1)
            dve.wait_ge(setup_sb, 2)
            dve.wait_ge(seeded, 1)
            with dve.Fori(0, STEPS) as s:
                links[0] = 0

                def link(ins):
                    links[0] += 1
                    ins.then_inc(dve_link, 1)
                    dve.wait_ge(dve_link, s * LINKS + links[0])

                def newton(y, v, t):
                    link(STT(t, y, -0.5, v, ALU.mult, ALU.mult))
                    link(TT(t, t, y, ALU.mult))
                    link(STT(y, t, 1.5, y, ALU.add, ALU.mult))

                def rsqrt(y, v, t):
                    link(TS(t.bitcast(i32), v.bitcast(i32), 1, None, ALU.logical_shift_right))
                    link(TS(y.bitcast(i32), t.bitcast(i32), -1.0, float(0x5f3759df), ALU.mult, ALU.add))
                    for _ in range(3):
                        newton(y, v, t)

                for l in range(3):
                    base, a0 = T0[l], T0[l] - NCH
                    if l == 0:
                        dve.wait_ge(acc_ok, s * E + 1)
                        dve.wait_ge(x0_in, s * 32 + 32)
                        for gh in range(GH):
                            sg, s2 = S[:, gh, 1:J + 1, :], S2[:, gh, 1:J + 1, :]
                            for d in range(DIN):
                                xd = X0[:, gh, :, d:d + 1].to_broadcast([P, J, 8])
                                ad = A0b[:, d:d + 1, :].to_broadcast([P, J, 8])
                                if d == 0:
                                    TT(sg, xd, ad, ALU.mult)
                                else:
                                    link(TT(s2, xd, ad, ALU.mult))
                                    link(TT(sg, sg, s2, ALU.add))
                        nc.vector.tensor_tensor(dX0[:, :, 1:J, :].rearrange("p a j d -> p a (j d)"),
                                                X0[:, :, 1:J, :].rearrange("p a j d -> p a (j d)"),
                                                X0[:, :, 0:J - 1, :].rearrange("p a j d -> p a (j d)"), ALU.subtract)
                    else:
                        dve.wait_ge(s_sb, s * 2 + l)
                    nc.vector.memset(S[:, :, 0, :], 0.0)
                    link(nc.vector.memset(S[:, :, J + 1:, :], 0.0))
                    Eb = edge_scores(l)
                    for k, (a, b) in enumerate(((1, 1), (2, 1), (0, 1))):
                        for gh in range(GH):
                            es, ed = S[:, gh, a:a + JP, 0:4], S[:, gh, b:b + JP, 4:8]
                            eo = Eb[:, k, gh, :]
                            if l == 0:
                                last = TT(eo.rearrange("p (j h) -> p j h", h=4), es, ed, ALU.add)
                            else:
                                last = TT(eo.rearrange("p (q m h) -> p q m h", q=CJ, h=4),
                                          es.rearrange("p (m q) h -> p q m h", q=CJ),
                                          ed.rearrange("p (m q) h -> p q m h", q=CJ), ALU.add)
                    link(last)
                    end = (J - 1) * 4 if l == 0 else ((J - 1) % CJ * NCH + (J - 1) // CJ) * 4
                    nc.vector.memset(Eb[:, 1, :, end:end + 4], NEG)
                    link(nc.vector.memset(Eb[:, 2, :, 0:4], NEG))
                    ef = Eb[:].rearrange("p k a n -> p (k a n)")
                    ff = Fb[:].rearrange("p k n -> p (k n)")
                    link(STT(ff, ef, 0.2, ef, ALU.mult, ALU.max))
                    link(TT(Mx[:], Fb[:, 0, :], Fb[:, 1, :], ALU.max))
                    link(TT(Mx[:], Mx[:], Fb[:, 2, :], ALU.max))
                    TT(Fb[:], Fb[:], Mx[:].unsqueeze(1).to_broadcast([P, 3, N4]), ALU.subtract).then_inc(f_ok, 1)
                    dve.wait_ge(exp_ok, s * 3 + l + 1)
                    link(TT(Mx[:], Fb[:, 0, :], Fb[:, 1, :], ALU.add))
                    link(TT(Mx[:], Mx[:], Fb[:, 2, :], ALU.add))
                    link(nc.vector.reciprocal(Mx[:], Mx[:]))
                    link(TT(Al[:], Fb[:, 1:3, :], Mx[:].unsqueeze(1).to_broadcast([P, 2, N4]), ALU.mult))
                    if l == 0:
                        dve.wait_ge(y_pad, s + 1)
                        for gh in range(GH):
                            if gh:
                                link(last)
                            def al(k):
                                o = gh * JP * HEADS
                                return Al[:, k, o:o + J * HEADS].rearrange("p (j h) -> p j h", h=4)\
                                    .unsqueeze(3).to_broadcast([P, J, HEADS, DIN])

                            def heads(a):
                                return a.unsqueeze(2).to_broadcast([P, J, HEADS, DIN])

                            def t4(t):
                                return t[:].rearrange("p j (h d) -> p j h d", h=HEADS)

                            TT(t4(Tc), al(0), heads(dX0[:, gh, 1:J + 1, :]), ALU.mult)
                            link(TT(t4(Td), al(1), heads(dX0[:, gh, 0:J, :]), ALU.mult))
                            link(TT(Tc[:], Tc[:], Td[:], ALU.subtract))
                            link(TT(t4(Tc), t4(Tc), heads(X0[:, gh, :, :]), ALU.add))
                            for c0, c1 in ((0, NCH - 1), (NCH - 1, NCH)):
                                a, b = CJ * c0, min(CJ * c1, J)
                                w4 = (b - a) // (c1 - c0)
                                for r0, src in ((0, Tc[:, a:b, :]), (12, X0[:, gh, a:b, :])):
                                    n = src.shape[2]
                                    last = nc.vector.tensor_copy(Y[:, c0:c1, gh, 0:w4, r0:r0 + n],
                                                                 src.rearrange("p (c j) r -> p c j r", j=w4))
                        last.then_inc(y_ok, 1)
                    else:
                        def sets(fn):
                            for t, (m0, m1) in enumerate(((0, JS), (JS, NCH))):
                                last = fn(lambda k: Pt[:, :, t, k, 0:(m1 - m0) * 4],
                                          *(x.rearrange("p s (q n) -> p (s q) n", n=NCH * 4)[:, :, m0 * 4:m1 * 4]
                                            for x in (Al, Res)))
                            return last
                        link(sets(lambda part, al, re: nc.vector.tensor_copy(part(0), al)))
                        link(sets(lambda part, al, re: TT(re, al, part(0), ALU.subtract)))
                        link(sets(lambda part, al, re: nc.vector.tensor_copy(part(1), re)))
                        sets(lambda part, al, re: TT(part(2), re, part(1), ALU.subtract)).then_inc(parts_ok, 1)
                        for k in range(2):
                            dve.wait_ge(at_ps, s * 8 + 4 * (l - 1) + k + 3)
                            nc.vector.tensor_copy(AT[:, 1, k, :], bank[2 + k][0:AR, :].bitcast(bf16))\
                                .then_inc(at_dve, 1)

                    def neighbours(n):
                        c, gh = task(l, n)
                        k, cols = a0 + n, joints(c) * P
                        slot = gh or 0
                        if l == 2:
                            dve.wait_ge(t_ok, s * AGG + k + 1)
                            dve.wait_ge(d_sb, s * AGG + a0 + min(n + 2, NCH))
                            d, h = DR[:, 0, c % 2, :], HS[c % 3]
                            if c + 1 < NCH:
                                TT(d[:, cols - P:cols], HS[(c + 1) % 3][:, 0:P], h[:, cols - P:cols], ALU.subtract)
                            else:
                                nc.vector.memset(d[:, cols - P:cols], 0.0)
                            link(TT(d[:, 0:cols - P], h[:, P:cols], h[:, 0:cols - P], ALU.subtract))
                        else:
                            dve.wait_ge(d_sb, s * AGG + k + 1)
                        dve.wait_ge(a_ps, s * AGG + k + 1)
                        if k >= 2:
                            dve.wait_ge(z_ps, s * TASKS + NCH + k - 1)
                        dve.wait_ge(t_ok, s * AGG + k + 1)
                        ap, am = bA[k % 2]
                        ta = TA[:, k % 2, :]
                        TT(ta[:, 0:cols], ap[:, 0:cols], DR[:, slot, c % 2, 0:cols], ALU.mult)
                        if c == 0:
                            nc.vector.memset(TB[:, 0:P], 0.0)
                        else:
                            TT(TB[:, 0:P], am[:, 0:P], DR[:, slot, (c - 1) % 2, NCOL - P:NCOL], ALU.mult)
                        link(TT(TB[:, P:cols], am[:, P:cols], DR[:, slot, c % 2, 0:cols - P], ALU.mult))
                        TT(ta[:, 0:cols], ta[:, 0:cols], TB[:, 0:cols], ALU.subtract).then_inc(t_ok, 1)

                    def normalise(n):
                        c, gh = task(l, n)
                        k, cols = base + n, joints(c) * P
                        o = c * NCOL
                        dve.wait_ge(r_ps, s * TASKS + k + 1)
                        dst = X2[:, gh, o:o + cols] if l == 1 else X1[:, o:o + cols]
                        TT(dst, dst, bA[n % 2][n // 2 % 2][:, 0:cols], ALU.mult).then_inc(u_ok, 1)

                    if l:
                        for n in range(NT[l]):
                            neighbours(n)
                    dve.wait_ge(v_ps, s * TASKS + base + NT[l])
                    TS(VB, bV[0:VR, :], EPS, None, ALU.add).then_inc(var_ok, 1)
                    dve.wait_ge(sd_ok, s * 3 + l + 1)
                    link(nc.vector.reciprocal(RV, RV))
                    newton(RV, VB, RN)
                    link(nc.vector.tensor_copy(RP[0:VR, :], RV))
                    link(TT(VB, RV, RP[0:VR, :], ALU.subtract))
                    nc.vector.tensor_copy(RP[32:32 + VR, :], VB)
                    link(nc.vector.tensor_copy(RM, VB))
                    TT(RP[64:64 + VR, :], VB, RM, ALU.subtract).then_inc(rp_ok, 1)
                    dve.wait_ge(zs_ok, s * TASKS + base + NT[l])
                    for n in range(NT[l]):
                        normalise(n)

                def stats(srcs):
                    n = len(srcs)
                    for t, src in enumerate(srcs):
                        last = nc.vector.bn_stats(st[:, t, :], src)
                    link(last)
                    nc.vector.memset(carrier[:, 1:2], 0.0)
                    for t in range(n):
                        last = nc.vector.bn_aggr(mv[:, t, :], st[:, t, :])
                    link(last)
                    link(TS(rv[:, 0:n], mv[:, 0:n, 1], EPS, None, ALU.add))
                    rsqrt(rs[:, 0:n], rv[:, 0:n], rt[:, 0:n])

                dve.wait_ge(fp_ps, s + 1)
                pose = Hf[:].rearrange("p (g h) d -> p g h d", g=GH)[:, :, 0, :]

                def row(k):
                    return rows[:, k * P:k * P + P].unsqueeze(1).to_broadcast([P, GH, P])

                for gh in range(GH):
                    last = TT(Hf[:, 2 * gh, :], bank[gh][:, 0:P], rows[:, 0:P], ALU.add)
                link(last)
                stats([Hf[:, 0, :], Hf[:, 2, :]])
                for gh in range(GH):
                    h = Hf[:, 2 * gh, :]
                    last = TS(h, h, mv[:, gh, 0:1], rs[:, gh:gh + 1], ALU.subtract, ALU.mult)
                link(last)
                link(TT(pose, pose, row(1), ALU.mult))
                link(TT(pose, pose, row(2), ALU.add))
                dve.wait_ge(txt_in, s * 32 + 32)
                stats([Hf[:, t, :] for t in range(4)])
                for t in range(4):
                    last = TS(Xn[:, t, :], Hf[:, t, :], mv[:, t, 0:1], rs[:, t:t + 1], ALU.subtract, ALU.mult)
                last.then_inc(h_ok, 1)
                dve.wait_ge(q2_sb, s + 1)
                qd = QD.rearrange("p (b t) -> p b t", b=GH)
                link(TS(qd, QC[:, :, 3:3 + 2 * P], v("cw3"), None, ALU.mult))
                for k in range(3):
                    ins = STT(qd, QC[:, :, k:k + 2 * P], v(f"cw{k}"), qd, ALU.mult, ALU.add)
                    if k < 2:
                        link(ins)
                ins.then_inc(cv_ok, 1)
                dve.wait_ge(ss_ps, s + 1)
                TS(NV, bank[4][0:1, :], 1e-24, None, ALU.max).then_inc(nv_ok, 1)
                dve.wait_ge(nsd_ok, s + 1)
                link(nc.vector.reciprocal(NR, NR))
                link(STT(RN[0:1, :], NR, -0.5, NV, ALU.mult, ALU.mult))
                link(TT(RN[0:1, :], RN[0:1, :], NR, ALU.mult))
                STT(NR, RN[0:1, :], 1.5, NR, ALU.add, ALU.mult).then_inc(nr_ok, 1)
                dve.wait_ge(nb_ps, s + 1)
                TT(KN, QD, bank[5][:], ALU.mult).then_inc(kn_ok, 1)
                dve.wait_ge(o_ps, s + 1)
                dve.wait_ge(stored, s * 32 + 1)
                hof, hff = Ho[:].rearrange("p t d -> p (t d)"), Hf[:].rearrange("p t d -> p (t d)")
                link(TT(hof, bank[0][:], hff, ALU.add))
                stats([Ho[:, t, :] for t in range(4)])
                for t in range(4):
                    last = TS(Xn[:, t, :], Ho[:, t, :], mv[:, t, 0:1], rs[:, t:t + 1], ALU.subtract, ALU.mult)
                last.then_inc(ho_ok, 1)
                dve.wait_ge(lg_ps, s + 1)
                lg3 = bank[2][:, 0:32].rearrange("p (t e) -> p t e", t=4)
                link(nc.vector.tensor_reduce(mx4[:], lg3, mybir.AxisListType.X, ALU.max))
                m3 = mx4[:].unsqueeze(2).to_broadcast([P, 4, 8])
                TT(LG[:], lg3, m3, ALU.subtract).then_inc(lgm_ok, 1)
                dve.wait_ge(rexp_ok, s + 1)
                link(nc.vector.tensor_reduce(den4[:], LG[:], mybir.AxisListType.X, ALU.add))
                link(nc.vector.reciprocal(den4[:], den4[:]))
                link(TT(PB[:], LG[:], den4[:].unsqueeze(2).to_broadcast([P, 4, 8]), ALU.mult))
                nc.vector.memset(carrier[:, 1:2], 0.0)
                for t in range(4):
                    last = nc.vector.max(top[:, t, :], PB[:, t, :])
                link(last)
                nc.vector.memset(carrier[:, 1:2], 0.0)
                for t in range(4):
                    last = nc.vector.max_index(tix[:, t, :], top[:, t, :], PB[:, t, :])
                link(last)
                link(nc.vector.tensor_copy(tif[:], tix[:]))
                link(TT(mx4[:], top[:, :, 0], top[:, :, 1], ALU.add))
                link(TS(mx4[:], mx4[:], 1e-9, None, ALU.add))
                link(nc.vector.reciprocal(mx4[:], mx4[:]))
                link(TT(gw[:], top[:, :, 0:2], mx4[:].unsqueeze(2).to_broadcast([P, 4, 2]), ALU.mult))
                i3 = iota8[:].rearrange("p (t e) -> p t e", t=4)
                for k in range(2):
                    g = gate if k == 0 else gtmp
                    link(TT(g[:], i3, tif[:, :, k:k + 1].to_broadcast([P, 4, 8]), ALU.is_equal))
                    link(TT(g[:], g[:], gw[:, :, k:k + 1].to_broadcast([P, 4, 8]), ALU.mult))
                TT(gate[:], gate[:], gtmp[:], ALU.add).then_inc(gate_ok, 1)
                dve.wait_ge(gate_ok, s + 1)
                dve.wait_ge(bo_ps, s + 1)
                link(TT(hof, bank[2][:], hof, ALU.add))
                for e in range(E):
                    dve.wait_ge(eo_ps, s * E + e + 2)
                    if e:
                        dve.wait_ge(acc_ok, s * E + e + 1)
                    for t in range(4):
                        last = STT(Ho[:, t, :], bank[e % 2][:, t * P:t * P + P], gate[:, t, e:e + 1], Ho[:, t, :],
                                   ALU.mult, ALU.add)
                    last.then_inc(acc_ok, 1)
                assert links[0] == LINKS, links[0]


def _layout(i):
    f = np.float32
    a = {k: np.asarray(x) for k, x in i.items()}
    t = {k[7:]: x for k, x in a.items() if k.startswith("L0_tok_")}
    m = {k[8:]: x for k, x in a.items() if k.startswith("L0_attn_")}
    n = {k[7:]: x for k, x in a.items() if k.startswith("L0_ffn_")}
    o = {}
    o["x"] = a["x"].reshape(STEPS, GH, P, J, DIN)
    o["txt"] = a["txt"].reshape(STEPS, GH, P, P)

    def blocks(s, d):
        h, c = s.shape
        r = np.zeros((h, c, 2, h), f)
        for k in range(h):
            r[k, :, 0, k] = s[k]
            r[k, :, 1, k] = d[k]
        return r.reshape(h * c, 2 * h)

    def twice(x, axis=0):
        return np.concatenate([x, x], axis)

    for l in range(3):
        o[f"abd{l}"] = blocks(t[f"as{l}"], t[f"ad{l}"])
    o["W0T"] = t["W0"].T
    rows0 = np.zeros((16, HEADS, F0 // HEADS), f)
    for h in range(HEADS):
        rows0[3 * h:3 * h + 3, h] = t["W0"].reshape(DIN, HEADS, -1)[:, h]
    rows0[12:15] = t["R0"].reshape(DIN, HEADS, -1)
    rows0[15] = t["bg0"].reshape(HEADS, -1)
    raw = np.zeros((F0, CJ, GH, GH, CJ, 16), f)
    for j in range(CJ):
        for g in range(GH):
            raw[:, j, g, g, j, :] = rows0.reshape(16, F0).T
    o["raw0"] = raw.reshape(F0, CJ * GH * P)
    o["W1T"], o["R1T"], o["W1"] = twice(t["W1"].T, 1), twice(t["R1"].T, 1), twice(t["W1"])
    o["W2T"], o["R2T"], o["W2"] = t["W2"].T, t["R2"].T, t["W2"]

    def centre(k):
        return np.eye(k, dtype=f) - f(1.0 / k)

    def twin(x):
        z = np.zeros_like(x)
        return np.block([[x, z], [z, x]])

    o["C1"], o["C2"] = centre(F1), twin(centre(F2))
    v1, v2 = np.zeros((P, 2 * VR - 1), f), np.zeros((P, 2 * VR - 1), f)
    v1[:, VR - 1] = 1.0 / F1
    v2[:F2, VR - 1] = 1.0 / F2
    v2[F2:, VR - 1 + NCH] = 1.0 / F2
    o["V1"], o["V2"] = v1, v2
    r1, r2 = np.zeros((RR, GH * NCH, P), f), np.zeros((RR, NCH, P), f)
    for part in range(3):
        for c in range(NCH):
            for g in range(GH):
                r1[32 * part + g * NCH + c, g * NCH + c] = 1.0
                r2[32 * part + g * NCH + c, c, F2 * g:F2 * g + F2] = 1.0
    o["selr1"], o["selr2"] = r1.reshape(RR, -1), r2.reshape(RR, -1)
    o["ones"], o["ident"] = np.ones((P, P), f), np.eye(P, dtype=f)
    for name, width in (("sel1", F1), ("sel2", F2)):
        s = np.zeros((3, JS, HEADS, JS, HEADS, width // HEADS), f)
        for j in range(JS):
            for h in range(HEADS):
                s[:, j, h, j, h, :] = 1.0
        o[name] = s.reshape(AR, JS * width)
    cols = [t["bg1"], twice(t["bg2"]), twice(t["g0"]), twice(t["b0"]), t["g1"], t["b1"], twice(t["g2"]), twice(t["b2"]),
            m["conv_q_b"]] + [m["conv_q_w"][:, 0, k] for k in range(4)]
    o["vec"] = np.concatenate([np.stack(cols, 1), n["b1"].reshape(E * MT, P).T], 1)
    o["rows"] = np.broadcast_to(np.concatenate([t["fpb"], t["fng"], t["fnb"]])[None], (P, 3 * P))
    o["fpW"] = twice(t["fpW"].reshape(J, F2, P).transpose(1, 0, 2).reshape(F2, J * P))
    o["wq1"], o["wq2"], o["wout"] = m["w_q1"].T, m["w_q2"].T, m["w_out"].T
    o["mw1"] = m["mem_w1"].T
    o["mw2"] = m["mem_w2"].T.reshape(2, P, P).transpose(1, 0, 2).reshape(P, 2 * P)
    o["rw"] = n["router_w"].T
    o["w1"] = n["w1"].transpose(2, 0, 1).reshape(P, E * FF)
    o["w2"] = n["w2"].transpose(2, 0, 1).reshape(MT, P, E, P).transpose(1, 2, 0, 3).reshape(P, E * FF)
    o["b2"] = n["b2"]
    o["iota8"] = np.broadcast_to(np.tile(np.arange(8, dtype=f), 4)[None], (P, 32))
    return {k: np.ascontiguousarray(x) for k, x in o.items()}


def kernel(**inputs):
    import concourse.bacc as _bacc
    from concourse.bass_utils import run_bass_kernel_spmd as _run

    laid = _layout(inputs)
    nc = _bacc.Bacc("TRN2", target_bir_lowering=False, num_devices=1)
    arrays, aps = {}, {}
    for name, a in laid.items():
        arrays[f"in_{name}"] = a
        aps[name] = nc.dram_tensor(f"in_{name}", a.shape, mybir.dt.from_np(a.dtype), kind="ExternalInput").ap()
    out = nc.dram_tensor("out_0", (STEPS, GH, 2, P, P), mybir.dt.float32, kind="ExternalOutput").ap()
    build(nc, aps, out)
    r = _run(nc, [arrays], core_ids=[0])
    return r.results[0]["out_0"].reshape(STEPS * GH, 2 * P, P)
```

```python
import numpy as np
import concourse.bass as bass
from concourse import mybir
from contextlib import ExitStack

G, J, DIN = 4096, 50, 3
HEADS = 4
F0, F1, F2 = 64, 128, 64
P = 128
GH = 2
STEPS = G // (P * GH)
J_EDGES = 2 * (J - 1) + J
CJ = 4
NCH = (J + CJ - 1) // CJ
NCOL = CJ * P
JP = NCH * CJ
JS = 10
AR = 3 * JS * HEADS
NT = [NCH, GH * NCH, NCH]
T0 = [0, NCH, 3 * NCH]
TASKS = 4 * NCH
AGG = TASKS - NCH
TOK = GH * 2 * P
E, FF = 8, 512
MT = FF // P
HID = 256
GROUPS1, GROUPS2 = (J + 1) * 7, (J + 1) * 4
GROUPS = GROUPS1 + GROUPS2
VR = GH * NCH
SR = 8 * NCH
RR = 64 + VR
NEG = -3.0e38
EPS = 1e-5


def joints(c):
    return min(CJ, J - CJ * c)


def task(l, n):
    return (n // GH, n % GH) if l == 1 else (n, None)


def build(nc, A, out):
    fp32, bf16, i32, u32 = mybir.dt.float32, mybir.dt.bfloat16, mybir.dt.int32, mybir.dt.uint32
    ALU, ACT = mybir.AluOpType, mybir.ActivationFunctionType
    ctx = ExitStack()
    with ctx:
        def sb(name, shape, dt=fp32):
            return ctx.enter_context(nc.sbuf_tensor(name, shape, dt))

        def sem(name):
            return ctx.enter_context(nc.semaphore(name))

        consts = {}

        def const(name):
            consts[name] = sb("c_" + name, list(A[name].shape))[:]
            return consts[name]

        X2 = sb("X2", [P, GH, J * P])
        X2f = X2[:].rearrange("p a n -> p (a n)")
        setup_at = [0]

        def setup_const(name, dtype=fp32):
            p, n = A[name].shape
            consts[name] = X2f[0:p, setup_at[0]:setup_at[0] + n].bitcast(dtype)
            setup_at[0] += n
            return consts[name]

        W0T, abd0 = setup_const("W0T"), setup_const("abd0")
        raw0 = setup_const("raw0")
        W1T, R1T, abd1, W1 = setup_const("W1T"), setup_const("R1T"), setup_const("abd1"), const("W1")
        W2T, R2T, abd2, W2 = setup_const("W2T"), setup_const("R2T"), setup_const("abd2"), const("W2")
        C1, C2, ones, ident = (const(n) for n in ("C1", "C2", "ones", "ident"))
        V1, V2 = const("V1"), const("V2")
        sel1f, sel2f = setup_const("sel1"), setup_const("sel2")
        selr1f, selr2f = setup_const("selr1"), setup_const("selr2")
        vec = const("vec")
        rows = const("rows")
        fpW = const("fpW")
        wq1, wq2, mw1, mw2, wout = (const(n) for n in ("wq1", "wq2", "mw1", "mw2", "wout"))
        rw, w1, w2, b2 = const("rw"), const("w1"), const("w2"), const("b2")
        iota8 = const("iota8")
        VEC = {n: k for k, n in enumerate(["bg1", "bg2", "g0", "b0", "g1", "b1", "g2", "b2",
                                           "cb", "cw0", "cw1", "cw2", "cw3"])}
        FB1 = len(VEC)

        def v(name):
            return vec[:, VEC[name]:VEC[name] + 1]

        edges, iota = setup_const("edges", i32), setup_const("iota")
        chain_counts = setup_const("chain")

        A0b = sb("A0b", [P, DIN, 8])
        A1 = sb("A1", [P, 2 * SR - 8])
        A2 = sb("A2", [P, 2 * SR - 8])
        WR1 = sb("WR1", [P, F1])
        WR2 = sb("WR2", [P, F2])
        W0bd = sb("W0bd", [P, CJ, P])
        bgc = sb("bgc", [P, 2])
        sel1 = sb("sel1b", [AR, JS, P], bf16)
        sel2 = sb("sel2b", [AR, JS, F2], bf16)
        selr1 = sb("selr1b", [RR, GH * NCH, P], bf16)
        selr2 = sb("selr2b", [RR, NCH, P], bf16)
        identb = sb("identb", [P, P], bf16)

        X0 = sb("X0", [P, GH, J, DIN])
        dX0 = sb("dX0", [P, GH, J + 1, DIN])
        N4 = GH * JP * HEADS
        NS = GH * (JP + 2) * 8
        R = sb("R", [P, 2 * NS + 6 * N4])
        DX = R[:, 0:2 * NCOL].rearrange("p (a n) -> p a n", a=2)
        DR = R[:, 2 * NCOL:6 * NCOL].rearrange("p (g a n) -> p g a n", g=GH, a=2)
        TA = R[:, 6 * NCOL:8 * NCOL].rearrange("p (a n) -> p a n", a=2)
        S = R[:, 0:NS].rearrange("p (a j r) -> p a j r", a=GH, r=8)
        Res = R[:, NS:NS + 2 * N4].rearrange("p (a n) -> p a n", a=2)
        Fb = R[:, 2 * NS:2 * NS + 3 * N4].rearrange("p (a n) -> p a n", a=3)
        Tc = R[:, 2 * NS:2 * NS + 12 * J].rearrange("p (j r) -> p j r", j=J)
        Td = R[:, 2 * NS + 12 * J:2 * NS + 24 * J].rearrange("p (j r) -> p j r", j=J)
        Mx = R[:, 2 * NS + 3 * N4:2 * NS + 4 * N4]
        Al = R[:, 2 * NS + 4 * N4:2 * NS + 6 * N4].rearrange("p (a n) -> p a n", a=2)
        Pt = sb("Pt", [P, 4 * CJ, 2, 3, JS * HEADS], bf16)
        AT = sb("AT", [AR, 2, GH, 2 * CJ * P], bf16)
        NY = GH * NCH * CJ * 16
        Y = X2f[:, NCH * P:NCH * P + NY].rearrange("p (c a j r) -> p c a j r", c=NCH, a=GH, r=16)
        YT = X2f[:, 0:NCH * P]
        X1 = sb("X1", [P, (J + 1) * P])
        S2 = X1[:, 4 * NCOL:4 * NCOL + NS].rearrange("p (a j r) -> p a j r", a=GH, r=8)
        HS = [R[:, k * NCOL:(k + 1) * NCOL] for k in (0, 1, 4)]
        TB = sb("TB", [P, NCOL])

        def edge_scores(l):
            at = X2f[:, 2 * MT * TOK:2 * MT * TOK + 3 * N4] if l < 2 else X1[:, 0:3 * N4]
            return at.rearrange("p (k a n) -> p k a n", k=3, a=GH)

        def score_rows(l):
            at = X2f[0:SR, 0:2 * NCOL] if l < 2 else X1[0:SR, 4 * NCOL:6 * NCOL]
            return at.rearrange("p (g n) -> p g n", g=GH)

        SQ = sb("SQ", [P, 2, NCOL])
        EH = J_EDGES // 2
        EN = SQ[0:EH, 1, 0:4]
        HOT_S = SQ[0:EH, 0, 0:2 * J].rearrange("e (t j) -> e t j", t=2)
        HOT_D = SQ[0:EH, 0, 2 * J:2 * J + 2 * JP].rearrange("e (t j) -> e t j", t=2)
        CN = R[:, 2 * NCOL:2 * NCOL + J * JP // 2].bitcast(bf16).rearrange("p (j i) -> p j i", j=J)
        other = sb("other", [P, 1])
        flag = sb("flag", [P, 1], i32)
        g0 = 2 * NCOL + J * JP // 2 + 8
        GM, GD, GW, GR = (R[:, g0 + k * N4:g0 + (k + 1) * N4] for k in range(4))
        GK = SQ[:, 0, 2 * P:2 * P + JP]
        XJ = SQ[:, 1, 0:2 * P].rearrange("p (g n) -> p g n", g=GH)
        HG = SQ[:, 0, 0:2 * P].rearrange("p (g n) -> p g n", g=GH)
        GY = X1[:, 0:GH * J * 12].rearrange("p (g j r) -> p g j r", g=GH, r=12)
        GT4 = X1[:, GH * J * 12:GH * J * 12 + J * 12].rearrange("p (j h d) -> p j h d", h=HEADS, d=DIN)
        VB = TA[0:VR, 0, :]
        RV = TB[0:VR, :]
        RN = DX[0:VR, 0, :]
        RM = DX[0:VR, 1, 0:NCOL // 2].bitcast(bf16)
        RP = sb("RP", [RR, NCOL], bf16)
        mhalf = sb("mhalf", [P, 1])
        carrier = sb("carrier", [P, 2])
        Hf = sb("Hf", [P, 4, P])
        Ho = sb("Ho", [P, 4, P])
        Xn = R[:, NCOL:2 * NCOL].rearrange("p (t d) -> p t d", t=4)
        st = sb("st", [P, 4, 6])
        mv = sb("mv", [P, 4, 2])
        rs, rv, rt = sb("rs", [P, 4]), sb("rv", [P, 4]), sb("rt", [P, 4])
        XT = R[:, 0:TOK]
        Q1, QD, KN, GT = (X1[:, k * NCOL:(k + 1) * NCOL] for k in range(4))
        NV, NR = VB[0:1, :], RV[0:1, :]
        QC = sb("QC", [P, GH, 3 + 2 * P])
        QS = SQ[:, 0, :]
        MH = TA
        RT = TB[:]
        LG, PB, top, gtmp = (R[:, k:k + 32].rearrange("p (t e) -> p t e", t=4)
                             for k in range(8 * NCOL, 8 * NCOL + 128, 32))
        mx4 = sb("mx4", [P, 4])
        den4 = sb("den4", [P, 4])
        tix = sb("tix", [P, 4, 8], u32)
        gw = sb("gw", [P, 4, 2])
        gate, tif = LG, PB
        HD = X2f[:, 0:2 * MT * TOK].rearrange("p (a m t) -> p a m t", a=2, m=MT)

        bank = [ctx.enter_context(nc.psum_tensor(f"bank{i}", [P, NCOL], fp32)) for i in range(8)]
        bD, bV = bank[0], bank[5]
        bA = [[bank[1], bank[2]], [bank[6], bank[7]]]
        bZ = [bank[3], bank[4]]

        c_loaded = sem("c_loaded")
        setup_ps = sem("setup_ps")
        setup_sb = sem("setup_sb")
        seeded = sem("seeded")
        x0_in = sem("x0_in")
        txt_in = sem("txt_in")
        sr_ps = sem("sr_ps")
        sr_sb = sem("sr_sb")
        s_ps = sem("s_ps")
        s_sb = sem("s_sb")
        f_ok = sem("f_ok")
        exp_ok = sem("exp_ok")
        parts_ok = sem("parts_ok")
        at_ps = sem("at_ps")
        at_act = sem("at_act")
        at_dve = sem("at_dve")
        y_pad = sem("y_pad")
        y_ok = sem("y_ok")
        yt_ps = sem("yt_ps")
        yt_sb = sem("yt_sb")
        a_ps = sem("a_ps")
        d_ps = sem("d_ps")
        d_sb = sem("d_sb")
        t_ok = sem("t_ok")
        z_ps = sem("z_ps")
        zs_ok = sem("zs_ok")
        sq_ok = sem("sq_ok")
        v_ps = sem("v_ps")
        var_ok = sem("var_ok")
        sd_ok = sem("sd_ok")
        rp_ok = sem("rp_ok")
        r_ps = sem("r_ps")
        u_ok = sem("u_ok")
        x_ok = sem("x_ok")
        dx_ok = sem("dx_ok")
        fp_ps = sem("fp_ps")
        h_ok = sem("h_ok")
        xt_ps = sem("xt_ps")
        xt_sb = sem("xt_sb")
        q1_ps = sem("q1_ps")
        q1_sb = sem("q1_sb")
        q2_ps = sem("q2_ps")
        q2_sb = sem("q2_sb")
        cv_ok = sem("cv_ok")
        cs_self = sem("cs_self")
        cs_ok = sem("cs_ok")
        ss_ps = sem("ss_ps")
        nv_ok = sem("nv_ok")
        nsd_ok = sem("nsd_ok")
        nr_ok = sem("nr_ok")
        nb_ps = sem("nb_ps")
        kn_ok = sem("kn_ok")
        mh_ps = sem("mh_ps")
        mh_sb = sem("mh_sb")
        rt_ps = sem("rt_ps")
        rt_sb = sem("rt_sb")
        o_ps = sem("o_ps")
        ho_ok = sem("ho_ok")
        lg_ps = sem("lg_ps")
        lgm_ok = sem("lgm_ok")
        rexp_ok = sem("rexp_ok")
        gate_ok = sem("gate_ok")
        gt_ps = sem("gt_ps")
        gt_sb = sem("gt_sb")
        bo_ps = sem("bo_ps")
        hid_ps = sem("hid_ps")
        hid_sb = sem("hid_sb")
        eo_ps = sem("eo_ps")
        acc_ok = sem("acc_ok")
        stored = sem("stored")
        dve_link = sem("dve_link")
        en_ok = sem("en_ok")
        hot_ok = sem("hot_ok")
        cn_ps = sem("cn_ps")
        flag_ok = sem("flag_ok")
        ge_in = sem("ge_in")
        ge_out = sem("ge_out")
        g_xj = sem("g_xj")
        g_parts = sem("g_parts")
        g_tp = sem("g_tp")
        g_at = sem("g_at")
        g_mm = sem("g_mm")
        g_use = sem("g_use")

        block = ctx.enter_context(nc.Block())
        NCONST = len(consts)

        @block.sync
        def _(sp):
            for primed in (g_use, y_ok, ho_ok, eo_ps, d_ps, acc_ok, hid_sb, t_ok, stored):
                sp.sem_inc(primed, 1)
            for name, t in consts.items():
                sp.dma_start(t, A[name]).then_inc(c_loaded, 16)
            def step(s, chain):
                sp.wait_ge(y_ok, s + 1)
                for gh in range(GH):
                    sp.dma_start(X0[:, gh, :, :], A["x"][s, gh]).then_inc(x0_in, 16)
                sp.wait_ge(ho_ok, s + 1)
                for gh in range(GH):
                    sp.dma_start(Hf[:, 2 * gh + 1, :], A["txt"][s, gh]).then_inc(txt_in, 16)

            sp.wait_ge(flag_ok, 1)
            graph = sp.value_load(flag[0:1, 0:1])
            with sp.If(graph == 0):
                with sp.Fori(0, STEPS) as s:
                    step(s, True)
            with sp.If(graph != 0):
                with sp.Fori(0, STEPS) as s:
                    step(s, False)

        @block.gpsimd
        def _(pool):
            nc.gpsimd.memset(dX0[:], 0.0)
            nc.gpsimd.memset(RP[:], 0.0)
            nc.gpsimd.memset(mhalf[:], -0.5)
            nc.gpsimd.memset(Pt[:], 0.0)
            nc.gpsimd.memset(A1[:], 0.0)
            nc.gpsimd.memset(A2[:], 0.0)
            nc.gpsimd.memset(X1[:, J * P:], 0.0)
            nc.gpsimd.memset(QC[:], 0.0).then_inc(seeded, 1)
            pool.wait_ge(seeded, 1)
            pool.wait_ge(setup_sb, 2)
            def step(s, chain):
                pool.wait_ge(eo_ps, s * E + 1)
                nc.gpsimd.tensor_tensor(carrier[:, 0:1], mhalf[:], mhalf[:], ALU.add)
                nc.gpsimd.memset(Y[:].rearrange("p c a j r -> p (c a j r)"), 1.0).then_inc(y_pad, 1)

                if not chain:
                    return
                pool.wait_ge(parts_ok, s * 2 + 1)
                for c in range(NCH):
                    n = joints(c) * P
                    last = min(NCH - 1, (CJ * c + joints(c)) // CJ)
                    pool.wait_ge(x_ok, s * TASKS + last + 1)
                    if c >= 2:
                        pool.wait_ge(d_ps, s * AGG + GH * (c - 1) + 1)
                    else:
                        pool.wait_ge(d_ps, s * AGG + 1)
                    o = c * NCOL
                    nc.gpsimd.tensor_tensor(DX[:, c % 2, 0:n], X1[:, o + P:o + P + n], X1[:, o:o + n],
                                            ALU.subtract).then_inc(dx_ok, 1)

            pool.wait_ge(flag_ok, 1)
            graph = pool.value_load(flag[0:1, 0:1])
            with pool.If(graph == 0):
                with pool.Fori(0, STEPS) as s:
                    step(s, True)
            with pool.If(graph != 0):
                with pool.Fori(0, STEPS) as s:
                    step(s, False)

        @block.tensor
        def _(pe):
            pe.wait_ge(c_loaded, 16 * NCONST)
            mm = nc.tensor.matmul
            for d in range(DIN):
                mm(bank[0][:, 8 * d:8 * d + 8], W0T[:, d:d + 1].to_broadcast([F0, P]), abd0[:], start=True, stop=True)
            mm(bank[0][:, 32:40], W1T[:], abd1[:], start=True, stop=True)
            mm(bank[0][:, 40:48], W2T[:], abd2[:], start=True, stop=True)
            mm(bank[0][:, 48:49], C1[:], v("bg1"), start=True, stop=True)
            mm(bank[0][:, 49:50], C2[:], v("bg2"), start=True, stop=True)
            mm(bank[1][:, 0:F1], W1T[:], C1[:], start=True, stop=False)
            mm(bank[1][:, 0:F1], R1T[:], C1[:], start=False, stop=True)
            mm(bank[2][:, 0:F2], W2T[:], C2[0:F2, 0:F2], start=True, stop=False)
            mm(bank[2][:, 0:F2], R2T[:], C2[0:F2, 0:F2], start=False, stop=True)
            for q in range(CJ * GH):
                last = mm(bank[3][:, F0 * q:F0 * q + F0], raw0[:, P * q:P * q + P], C2[0:F0, 0:F0], start=True, stop=True)
            last.then_inc(setup_ps, 1)
            pe.wait_ge(setup_sb, 2)
            pe.wait_ge(hot_ok, 1)
            for j in range(J):
                for t in range(2):
                    last = mm(bank[j // 9][:, j % 9 * JP:(j % 9 + 1) * JP], HOT_S[:, t, j:j + 1].to_broadcast([EH, P]),
                              HOT_D[:, t, :], start=(t == 0), stop=(t == 1))
            last.then_inc(cn_ps, 1)
            pe.wait_ge(setup_sb, 2)
            def neighbours_any(s, l):
                nt = NT[l]
                ng = (nt + 3) // 4

                def group(jp1, g):
                    gi = s * GROUPS + (0 if l == 1 else GROUPS1) + jp1 * ng + g
                    pe.wait_ge(g_use, gi + 1)

                for g in range(ng):
                    group(0, g)
                    for n in range(4 * g, min(4 * g + 4, nt)):
                        c, gh = task(l, n)
                        cols, o, b = joints(c) * P, c * NCOL, bank[2 + n % 4]
                        if l == 1:
                            r = slice(64 * gh, 64 * gh + 64)
                            last = mm(b[:, 0:cols], W1[r, :], X1[r, o:o + cols], start=True, stop=True)
                        else:
                            for h in range(GH):
                                last = mm(b[64 * h:64 * h + 64, 0:cols], W2[:], X2[:, h, o:o + cols], start=True, stop=True)
                    last.then_inc(g_mm, 1)
                with pe.Fori(0, J) as jp:
                    pe.wait_ge(g_parts, (s * 2 + (l - 1)) * J + jp + 1)
                    for gh in range(GH):
                        atp = bank[gh][:].bitcast(bf16)
                        for t in range(2):
                            for q in range(CJ):
                                o = (t * CJ + q) * P
                                nc.tensor.transpose(atp[0:AR, o:o + P],
                                                    Pt[:, gh * CJ + q, t, :, :].rearrange("p k n -> p (k n)"), identb[:])
                    pe.wait_ge(g_xj, (s * 2 + (l - 1)) * J + jp + 1)
                    for gh in range(GH):
                        if l == 1:
                            r = slice(64 * gh, 64 * gh + 64)
                            last = mm(bank[6 + gh][:, 0:P], W1[r, :], XJ[r, 0, :], start=True, stop=True)
                        else:
                            last = mm(bank[6][64 * gh:64 * gh + 64, 0:P], W2[:], XJ[:, gh, :], start=True, stop=True)
                    last.then_inc(g_tp, 1)
                    pe.wait_ge(g_at, (s * 2 + (l - 1)) * J + jp + 1)
                    for g in range(ng):
                        group(jp + 1, g)
                        for n in range(4 * g, min(4 * g + 4, nt)):
                            c, gh = task(l, n)
                            cols, o, b = joints(c) * P, (c // JS) * NCOL, bank[2 + n % 4]
                            if l == 1:
                                last = mm(b[:, 0:cols], sel1[:, c % JS, :], AT[:, 0, gh, o:o + cols], start=True, stop=True)
                            else:
                                for h in range(GH):
                                    last = mm(b[64 * h:64 * h + 64, 0:cols], sel2[:, c % JS, :], AT[:, 0, h, o:o + cols],
                                              start=True, stop=True)
                        last.then_inc(g_mm, 1)

            def step(s, chain):
                pe.wait_ge(y_ok, s + 2)
                pe.wait_ge(acc_ok, s * E + 1)
                pe.wait_ge(hid_sb, s * E * MT + 1)
                for b in range(4):
                    for c in range(4 * b, min(4 * b + 4, NCH)):
                        last = nc.tensor.transpose(bank[4 + b][:, (c - 4 * b) * P:(c - 4 * b + 1) * P],
                                                   Y[:, c, :, :, :].rearrange("p a j r -> p (a j r)"), ident)
                    last.then_inc(yt_ps, 1)
                for l in range(3):
                    base, a0 = T0[l], T0[l] - NCH
                    if l == 0:
                        pe.wait_ge(yt_sb, s * 4 + 4)
                    else:
                        pe.wait_ge(sr_sb, s * 2 + l)
                        SC = score_rows(l)
                        for gh in range(GH):
                            for q in range(CJ):
                                last = nc.tensor.transpose(bank[6 + gh][:, q * SR:q * SR + SR], SC[:, gh, q * P:q * P + P],
                                                           ident[0:SR, 0:SR])
                        last.then_inc(s_ps, 1)
                    if l and not chain:
                        neighbours_any(s, l)
                    elif l:
                        pe.wait_ge(parts_ok, s * 2 + l)
                        pe.wait_ge(v_ps, s * TASKS + base)
                        for k in range(4):
                            sign, gh = k // 2, k % 2
                            atp = bank[k][:].bitcast(bf16)
                            for t in range(2):
                                for q in range(CJ):
                                    src = Pt[:, k * CJ + q, t, :, :].rearrange("p k n -> p (k n)")
                                    o = (t * CJ + q) * P
                                    last = nc.tensor.transpose(atp[0:AR, o:o + P], src, identb[:])
                            last.then_inc(at_ps, 1)
                        pe.wait_ge(at_act, s * 4 + 2 * l)
                        pe.wait_ge(at_dve, s * 4 + 2 * l)

                    def product_d(n):
                        c, gh = task(l, n)
                        k, cols = a0 + n, joints(c) * P
                        o = c * NCOL
                        if k > 0:
                            pe.wait_ge(d_sb, s * AGG + k)
                        if l == 1:
                            pe.wait_ge(dx_ok, s * NCH + c + 1)
                            mm(bD[:, 0:cols], W1[64 * gh:64 * gh + 64, :], DX[64 * gh:64 * gh + 64, c % 2, 0:cols],
                               start=True, stop=True).then_inc(d_ps, 1)
                        else:
                            mm(bD[0:64, 0:cols], W2[:], X2[:, 0, o:o + cols], start=True, stop=True)
                            mm(bD[64:128, 0:cols], W2[:], X2[:, 1, o:o + cols], start=True, stop=True)\
                                .then_inc(d_ps, 1)

                    def spread_alpha(n):
                        c, gh = task(l, n)
                        k, cols = a0 + n, joints(c) * P
                        if k >= 2:
                            pe.wait_ge(t_ok, s * AGG + k)
                        o = (c // JS) * NCOL
                        for sign in range(2):
                            b = bA[k % 2][sign]
                            if l == 1:
                                last = mm(b[:, 0:cols], sel1[:, c % JS, :], AT[:, sign, gh, o:o + cols], start=True, stop=True)
                            else:
                                for g in range(GH):
                                    last = mm(b[64 * g:64 * g + 64, 0:cols], sel2[:, c % JS, :],
                                              AT[:, sign, g, o:o + cols], start=True, stop=True)
                        last.then_inc(a_ps, 1)

                    def centred(n):
                        c, gh = task(l, n)
                        k, cols = base + n, joints(c) * P
                        o = c * NCOL
                        z = bZ[k % 2]
                        if k >= 2:
                            pe.wait_ge(zs_ok, s * TASKS + k - 1)
                            pe.wait_ge(sq_ok, s * TASKS + k - 1)
                        if l == 0:
                            for j in range(joints(c)):
                                last = mm(z[:, j * P:j * P + P], W0bd[:, j, :], YT[:, c * P:c * P + P], start=True, stop=True)
                        elif l == 1:
                            mm(z[:, 0:cols], WR1[64 * gh:64 * gh + 64, :], X1[64 * gh:64 * gh + 64, o:o + cols],
                               start=True, stop=False)
                            pe.wait_ge(t_ok, s * AGG + k - NCH + 2)
                            last = mm(z[:, 0:cols], C1[:], TA[:, (k - NCH) % 2, 0:cols], start=False, stop=True)
                        else:
                            for g in range(GH):
                                mm(z[64 * g:64 * g + 64, 0:cols], WR2[:], X2[:, g, o:o + cols], start=True, stop=False,
                                   skip_group_check=True)
                            pe.wait_ge(t_ok, s * AGG + k - NCH + 2)
                            last = mm(z[:, 0:cols], C2[:], TA[:, (k - NCH) % 2, 0:cols], start=False, stop=True,
                                      skip_group_check=True)
                        last.then_inc(z_ps, 1)

                    def variance(n):
                        c, gh = task(l, n)
                        k, cols = base + n, joints(c) * P
                        pe.wait_ge(sq_ok, s * TASKS + k + 1)
                        row = c if gh is None else gh * NCH + c
                        mm(bV[0:VR, 0:cols], (V1 if l == 1 else V2)[:, VR - 1 - row:2 * VR - 1 - row], SQ[:, k % 2, 0:cols],
                           start=(n == 0), stop=(n == NT[l] - 1), skip_group_check=True).then_inc(v_ps, 1)

                    def spread_rstd(n):
                        c, gh = task(l, n)
                        k, cols = base + n, joints(c) * P
                        if n >= 4:
                            pe.wait_ge(u_ok, s * TASKS + k - 3)
                        sel = selr2[:, c, :] if gh is None else selr1[:, gh * NCH + c, :]
                        mm(bA[n % 2][n // 2 % 2][:, 0:cols], sel, RP[:, 0:cols], start=True, stop=True)\
                            .then_inc(r_ps, 1)

                    def scores(n):
                        c, gh = task(l, n)
                        cols, o, w = joints(c) * P, c * NCOL, SR - 8 - 8 * c
                        pe.wait_ge(x_ok, s * TASKS + base + n + 1)
                        for g in range(GH) if gh is None else (gh,):
                            if l == 0:
                                lhs, rhs = A1[64 * g:64 * g + 64, w:w + SR], X1[64 * g:64 * g + 64, o:o + cols]
                            else:
                                lhs, rhs = A2[:, w:w + SR], X2[:, g, o:o + cols]
                            last = mm(bank[3 + g][0:SR, 0:cols], lhs, rhs, start=(c == 0), stop=(c == NCH - 1),
                                      skip_group_check=True)
                        if n == NT[l] - 1:
                            last.then_inc(sr_ps, 1)

                    def projection(n):
                        pe.wait_ge(x_ok, s * TASKS + base + n + 1)
                        for j in range(CJ * n, CJ * n + joints(n)):
                            for gh in range(GH):
                                r = slice(64 * gh, 64 * gh + 64)
                                last = mm(bank[3 + gh][:, 0:P], X1[r, j * P:j * P + P], fpW[r, j * P:j * P + P],
                                          start=(j == 0), stop=(j == J - 1))
                        if n == NCH - 1:
                            last.then_inc(fp_ps, 1)

                    if l == 2 and chain:
                        product_d(0)
                    for n in range(NT[l] + 2):
                        if l and n < NT[l] and chain:
                            spread_alpha(n)
                            if l == 1:
                                product_d(n)
                            elif n + 1 < NT[l]:
                                product_d(n + 1)
                        if 1 <= n <= NT[l]:
                            centred(n - 1)
                        if n >= 2:
                            variance(n - 2)
                    pe.wait_ge(rp_ok, s * 3 + l + 1)
                    for n in range(NT[l] + 3):
                        if n < NT[l]:
                            spread_rstd(n)
                        if n >= 3:
                            if l < 2:
                                scores(n - 3)
                            else:
                                projection(n - 3)
                pe.wait_ge(h_ok, s + 1)
                for t in range(4):
                    last = nc.tensor.transpose(bank[1][:, t * P:t * P + P], Xn[:, t, :], ident[:])
                last.then_inc(xt_ps, 1)
                pe.wait_ge(xt_sb, s * 2 + 1)
                mm(bank[2][:], wq1[:], XT[:], start=True, stop=True).then_inc(q1_ps, 1)
                pe.wait_ge(q1_sb, s + 1)
                mm(bank[3][:], wq2[:], Q1, start=True, stop=True).then_inc(q2_ps, 1)
                pe.wait_ge(cs_ok, s + 1)
                mm(bank[4][0:1, :], ones[:, 0:1], QS, start=True, stop=True).then_inc(ss_ps, 1)
                pe.wait_ge(nr_ok, s + 1)
                mm(bank[5][:], ones[0:1, :], NR, start=True, stop=True).then_inc(nb_ps, 1)
                pe.wait_ge(kn_ok, s + 1)
                for m in range(2):
                    mm(bank[6 - m][:], mw1[:, m * P:m * P + P], KN, start=True, stop=True).then_inc(mh_ps, 1)
                pe.wait_ge(mh_sb, s * 2 + 2)
                for m in range(2):
                    last = mm(bank[7][:], mw2[:, m * P:m * P + P], MH[:, m, :], start=(m == 0), stop=(m == 1))
                last.then_inc(rt_ps, 1)
                pe.wait_ge(rt_sb, s + 1)
                for t in range(4):
                    last = mm(bank[0][:, t * P:t * P + P], RT[:, t * P:t * P + P], wout[:], start=True, stop=True)
                last.then_inc(o_ps, 1)
                pe.wait_ge(ho_ok, s + 2)
                for t in range(4):
                    last = nc.tensor.transpose(bank[1][:, t * P:t * P + P], Xn[:, t, :], ident[:])
                last.then_inc(xt_ps, 1)
                pe.wait_ge(xt_sb, s * 2 + 2)
                for t in range(4):
                    last = mm(bank[2][:, 8 * t:8 * t + 8], XT[:, t * P:t * P + P], rw[:], start=True, stop=True)
                last.then_inc(lg_ps, 1)

                def up(e):
                    for m in range(MT):
                        k = e * MT + m
                        if k >= 4:
                            pe.wait_ge(hid_sb, s * E * MT + k - 2)
                        mm(bank[4 + k % 4][:], w1[:, (e * MT + m) * P:(e * MT + m + 1) * P], XT[:], start=True, stop=True)\
                            .then_inc(hid_ps, 1)

                def down(e):
                    pe.wait_ge(hid_sb, s * E * MT + (e + 1) * MT + 1)
                    if e >= 2:
                        pe.wait_ge(acc_ok, s * E + e)
                    for t in range(4):
                        b = bank[e % 2][:, t * P:t * P + P]
                        for m in range(MT):
                            last = mm(b, HD[:, e % 2, m, t * P:t * P + P], w2[:, (e * MT + m) * P:(e * MT + m + 1) * P],
                               start=(m == 0), stop=(m == MT - 1))
                    last.then_inc(eo_ps, 1)

                up(0)
                for e in range(E):
                    if e + 1 < E:
                        up(e + 1)
                    if e == 0:
                        pe.wait_ge(gate_ok, s + 1)
                        for t in range(4):
                            last = nc.tensor.transpose(bank[3][0:E, t * P:t * P + P], gate[:, t, :], ident)
                        last.then_inc(gt_ps, 1)
                        pe.wait_ge(gt_sb, s + 1)
                        for t in range(4):
                            last = mm(bank[2][:, t * P:t * P + P], GT[0:E, t * P:t * P + P], b2, start=True, stop=True)
                        last.then_inc(bo_ps, 1)
                    down(e)

            pe.wait_ge(flag_ok, 1)
            graph = pe.value_load(flag[0:1, 0:1])
            with pe.If(graph == 0):
                with pe.Fori(0, STEPS) as s:
                    step(s, True)
            with pe.If(graph != 0):
                with pe.Fori(0, STEPS) as s:
                    step(s, False)

        @block.scalar
        def _(act):
            A_ = nc.scalar.activation
            act.wait_ge(setup_ps, 1)
            A_(W0bd[:].rearrange("p j f -> p (j f)"), bank[3][:], ACT.Copy)
            A_(sel1[:].rearrange("p j f -> p (j f)"), sel1f[:], ACT.Copy)
            A_(sel2[:].rearrange("p j f -> p (j f)"), sel2f[:], ACT.Copy)
            A_(selr1[:].rearrange("p j f -> p (j f)"), selr1f[:], ACT.Copy)
            A_(selr2[:].rearrange("p j f -> p (j f)"), selr2f[:], ACT.Copy)
            A_(identb[:], ident[:], ACT.Copy).then_inc(setup_sb, 1)
            def softmax_any(s, l):
                for again in range(2):
                    with act.Fori(0, J) as jp:
                        if l == 1 and again:
                            A_(XJ[:, 0, :], X1[:, bass.ds(jp * P, P)], ACT.Copy).then_inc(g_xj, 1)
                        if l == 2 and again:
                            A_(XJ, X2[:, :, bass.ds(jp * P, P)], ACT.Copy).then_inc(g_xj, 1)
                        act.wait_ge(ge_in, ((s * 3 + l) * 2 + again) * J + jp + 1)
                        A_(GW, GW, ACT.Exp).then_inc(ge_out, 1)
                        if l and again:
                            act.wait_ge(g_tp, (s * 2 + (l - 1)) * J + jp + 1)
                            for gh in range(GH):
                                A_(AT[:, 0, gh, :], bank[gh][0:AR, :].bitcast(bf16), ACT.Copy)
                            if l == 1:
                                A_(HG[:, 0, :], bank[6][:, 0:P], ACT.Copy)
                                A_(HG[:, 1, :], bank[7][:, 0:P], ACT.Copy).then_inc(g_at, 1)
                            else:
                                A_(HG[:, 0, :], bank[6][:, 0:P], ACT.Copy).then_inc(g_at, 1)

            def step(s, chain):
                for l in range(3):
                    base, a0 = T0[l], T0[l] - NCH
                    if l:
                        act.wait_ge(sr_ps, s * 2 + l)
                        SC = score_rows(l)
                        A_(SC[:, 0, :], bank[3][0:SR, :], ACT.Copy)
                        A_(SC[:, 1, :], bank[4][0:SR, :], ACT.Copy).then_inc(sr_sb, 1)
                        act.wait_ge(s_ps, s * 2 + l)
                        for gh in range(GH):
                            last = A_(S[:, gh, 1:JP + 1, :].rearrange("p (c q) r -> p q c r", q=CJ),
                                      bank[6 + gh][:, 0:CJ * SR].rearrange("p (q c r) -> p q c r", q=CJ, r=8), ACT.Copy)
                        last.then_inc(s_sb, 1)
                    if not chain:
                        softmax_any(s, l)
                    if chain:
                        act.wait_ge(f_ok, s * 3 + l + 1)
                        A_(Fb[:].rearrange("p k n -> p (k n)"), Fb[:].rearrange("p k n -> p (k n)"), ACT.Exp)\
                            .then_inc(exp_ok, 1)
                    if l and chain:
                        for k in range(2):
                            act.wait_ge(at_ps, s * 8 + 4 * (l - 1) + k + 1)
                            A_(AT[:, 0, k, :], bank[k][0:AR, :].bitcast(bf16), ACT.Copy).then_inc(at_act, 1)
                    if l == 0:
                        for b in range(4):
                            act.wait_ge(yt_ps, s * 4 + b + 1)
                            n = min(4, NCH - 4 * b) * P
                            A_(YT[:, 4 * b * P:4 * b * P + n], bank[4 + b][:, 0:n], ACT.Copy).then_inc(yt_sb, 1)

                    def take_d(n):
                        c, gh = task(l, n)
                        k, cols = a0 + n, joints(c) * P
                        act.wait_ge(d_ps, s * AGG + k + 2)
                        if l == 1:
                            if n >= 2:
                                act.wait_ge(t_ok, s * AGG + k)
                            A_(DR[:, gh, c % 2, 0:cols], bD[:, 0:cols], ACT.Copy).then_inc(d_sb, 1)
                        else:
                            if n >= 3:
                                act.wait_ge(t_ok, s * AGG + k - 1)
                            A_(HS[c % 3][:, 0:cols], bD[:, 0:cols], ACT.Copy).then_inc(d_sb, 1)

                    def square(n):
                        c, gh = task(l, n)
                        k, cols = base + n, joints(c) * P
                        act.wait_ge(z_ps, s * TASKS + k + 1)
                        if k >= 2:
                            act.wait_ge(v_ps, s * TASKS + k - 1)
                        bias = bgc[:, l - 1:l] if l else 0.0
                        o = c * NCOL
                        dst = X2[:, gh, o:o + cols] if l == 1 else X1[:, o:o + cols]
                        A_(dst, bZ[k % 2][:, 0:cols], ACT.Identity, bias=bias).then_inc(zs_ok, 1)
                        A_(SQ[:, k % 2, 0:cols], bZ[k % 2][:, 0:cols], ACT.Square, bias=bias).then_inc(sq_ok, 1)

                    def gelu(n):
                        c, gh = task(l, n)
                        k, cols = base + n, joints(c) * P
                        o = c * NCOL
                        act.wait_ge(u_ok, s * TASKS + k + 1)
                        dst = X2[:, gh, o:o + cols] if l == 1 else X1[:, o:o + cols]
                        A_(dst, dst, ACT.Gelu, bias=v(f"b{l}"), scale=v(f"g{l}"))\
                            .then_inc(x_ok, 1)

                    if l == 2 and chain:
                        take_d(0)
                    for n in range(NT[l] + 1):
                        if l == 1 and n < NT[l] and chain:
                            take_d(n)
                        if l == 2 and n + 1 < NT[l] and chain:
                            take_d(n + 1)
                        if 1 <= n <= NT[l]:
                            square(n - 1)
                    act.wait_ge(var_ok, s * 3 + l + 1)
                    A_(RV, VB, ACT.Sqrt).then_inc(sd_ok, 1)
                    for n in range(NT[l]):
                        gelu(n)
                act.wait_ge(xt_ps, s * 2 + 1)
                A_(XT[:], bank[1][:], ACT.Copy).then_inc(xt_sb, 1)
                act.wait_ge(q1_ps, s + 1)
                A_(Q1, bank[2][:], ACT.Silu).then_inc(q1_sb, 1)
                act.wait_ge(q2_ps, s + 1)
                A_(QC[:, :, 3:], bank[3][:].rearrange("p (b t) -> p b t", b=GH), ACT.Copy).then_inc(q2_sb, 1)
                act.wait_ge(cv_ok, s + 1)
                A_(QD, QD, ACT.Silu, bias=v("cb")).then_inc(cs_self, 1)
                act.wait_ge(cs_self, s + 1)
                A_(QS, QD, ACT.Square).then_inc(cs_ok, 1)
                act.wait_ge(nv_ok, s + 1)
                A_(NR, NV, ACT.Sqrt).then_inc(nsd_ok, 1)
                for m in range(2):
                    act.wait_ge(mh_ps, s * 2 + m + 1)
                    A_(MH[:, m, :], bank[6 - m][:], ACT.Silu).then_inc(mh_sb, 1)
                act.wait_ge(rt_ps, s + 1)
                A_(RT[:], bank[7][:], ACT.Copy).then_inc(rt_sb, 1)
                act.wait_ge(xt_ps, s * 2 + 2)
                A_(XT[:], bank[1][:], ACT.Copy).then_inc(xt_sb, 1)
                act.wait_ge(lgm_ok, s + 1)
                A_(LG[:].rearrange("p t e -> p (t e)"), LG[:].rearrange("p t e -> p (t e)"), ACT.Exp)\
                    .then_inc(rexp_ok, 1)
                for k in range(E * MT):
                    e, m = k // MT, k % MT
                    if k == 2 * MT:
                        act.wait_ge(gt_ps, s + 1)
                        A_(GT[0:E, :], bank[3][0:E, :], ACT.Copy).then_inc(gt_sb, 1)
                    act.wait_ge(hid_ps, s * E * MT + k + 1)
                    if e >= 2 and m == 0:
                        act.wait_ge(eo_ps, s * E + e)
                    A_(HD[:, e % 2, m, :], bank[4 + k % 4][:], ACT.Gelu,
                       bias=vec[:, FB1 + k:FB1 + k + 1]).then_inc(hid_sb, 1)
                act.wait_ge(acc_ok, s * E + E + 1)
                for gh in range(GH):
                    act.dma_start(out[s, gh].rearrange("h p d -> p h d"), Ho[:, 2 * gh:2 * gh + 2, :])\
                        .then_inc(stored, 16)

            act.wait_ge(flag_ok, 1)
            graph = act.value_load(flag[0:1, 0:1])
            with act.If(graph == 0):
                with act.Fori(0, STEPS) as s:
                    step(s, True)
            with act.If(graph != 0):
                with act.Fori(0, STEPS) as s:
                    step(s, False)
            act.wait_ge(stored, STEPS * 32 + 1)

        @block.vector
        def _(dve):
            TT, TS, STT = nc.vector.tensor_tensor, nc.vector.tensor_scalar, nc.vector.scalar_tensor_tensor
            LINKS_ANY = 101
            LINKS = 193
            links = [0]
            dve.wait_ge(setup_ps, 1)
            nc.vector.tensor_copy(A0b[:].rearrange("p d r -> p (d r)"), bank[0][:, 0:24])
            dve.wait_ge(seeded, 1)
            nc.vector.tensor_copy(A1[:, SR - 8:SR], bank[0][:, 32:40])
            nc.vector.tensor_copy(A2[:, SR - 8:SR], bank[0][:, 40:48])
            nc.vector.tensor_copy(bgc[:], bank[0][:, 48:50])
            nc.vector.tensor_copy(WR1[:], bank[1][:, 0:F1])
            nc.vector.tensor_copy(WR2[:], bank[2][:, 0:F2]).then_inc(setup_sb, 1)
            nc.vector.tensor_copy(EN, edges).then_inc(en_ok, 1)
            dve.wait_ge(en_ok, 1)
            for t in range(2):
                TS(HOT_S[:, t, :], iota[0:EH, 0:J], EN[:, t:t + 1], None, ALU.is_equal)
                last = TS(HOT_D[:, t, :], iota[0:EH, :], EN[:, 2 + t:3 + t], None, ALU.is_equal)
            last.then_inc(hot_ok, 1)
            dve.wait_ge(cn_ps, 1)
            for b in range((J + 8) // 9):
                n = min(9, J - 9 * b)
                last = nc.vector.tensor_copy(CN[:, 9 * b:9 * b + n, :].rearrange("p j i -> p (j i)"), bank[b][:, 0:n * JP])
            last.then_inc(en_ok, 1)
            dve.wait_ge(en_ok, 2)
            cf = CN.rearrange("p j i -> p (j i)")
            TT(chain_counts, chain_counts, cf, ALU.not_equal).then_inc(en_ok, 1)
            dve.wait_ge(en_ok, 3)
            nc.vector.tensor_reduce(other[:], chain_counts, mybir.AxisListType.X, ALU.max).then_inc(en_ok, 1)
            dve.wait_ge(en_ok, 4)
            nc.vector.tensor_copy(flag[:], other[:]).then_inc(flag_ok, 1)
            dve.wait_ge(setup_sb, 2)
            def step(s, chain):
                links[0] = 0
                per_step = LINKS if chain else LINKS_ANY

                def link(ins):
                    links[0] += 1
                    ins.then_inc(dve_link, 1)
                    dve.wait_ge(dve_link, s * per_step + links[0])

                def write_y(gh, heads12):
                    for c0, c1 in ((0, NCH - 1), (NCH - 1, NCH)):
                        a, b = CJ * c0, min(CJ * c1, J)
                        w4 = (b - a) // (c1 - c0)
                        for r0, src in ((0, heads12[:, a:b, :]), (12, X0[:, gh, a:b, :])):
                            n = src.shape[2]
                            last = nc.vector.tensor_copy(Y[:, c0:c1, gh, 0:w4, r0:r0 + n],
                                                         src.rearrange("p (c j) r -> p c j r", j=w4))
                    return last

                def sets(fn, rows16, *tensors):
                    for t, (m0, m1) in enumerate(((0, JS), (JS, NCH))):
                        last = fn(lambda k: Pt[:, 0:rows16, t, k, 0:(m1 - m0) * 4],
                                  *(x.rearrange("p (q n) -> p q n", n=NCH * 4)[:, :, m0 * 4:m1 * 4] for x in tensors))
                    return last

                def attend_chain(l):
                    Eb = edge_scores(l)
                    for k, (a, b) in enumerate(((1, 1), (2, 1), (0, 1))):
                        for gh in range(GH):
                            es, ed = S[:, gh, a:a + JP, 0:4], S[:, gh, b:b + JP, 4:8]
                            eo = Eb[:, k, gh, :]
                            if l == 0:
                                last = TT(eo.rearrange("p (j h) -> p j h", h=4), es, ed, ALU.add)
                            else:
                                last = TT(eo.rearrange("p (q m h) -> p q m h", q=CJ, h=4),
                                          es.rearrange("p (m q) h -> p q m h", q=CJ),
                                          ed.rearrange("p (m q) h -> p q m h", q=CJ), ALU.add)
                    link(last)
                    end = (J - 1) * 4 if l == 0 else ((J - 1) % CJ * NCH + (J - 1) // CJ) * 4
                    nc.vector.memset(Eb[:, 1, :, end:end + 4], NEG)
                    link(nc.vector.memset(Eb[:, 2, :, 0:4], NEG))
                    ef = Eb[:].rearrange("p k a n -> p (k a n)")
                    ff = Fb[:].rearrange("p k n -> p (k n)")
                    link(STT(ff, ef, 0.2, ef, ALU.mult, ALU.max))
                    link(TT(Mx[:], Fb[:, 0, :], Fb[:, 1, :], ALU.max))
                    link(TT(Mx[:], Mx[:], Fb[:, 2, :], ALU.max))
                    TT(Fb[:], Fb[:], Mx[:].unsqueeze(1).to_broadcast([P, 3, N4]), ALU.subtract).then_inc(f_ok, 1)
                    dve.wait_ge(exp_ok, s * 3 + l + 1)
                    link(TT(Mx[:], Fb[:, 0, :], Fb[:, 1, :], ALU.add))
                    link(TT(Mx[:], Mx[:], Fb[:, 2, :], ALU.add))
                    link(nc.vector.reciprocal(Mx[:], Mx[:]))
                    link(TT(Al[:], Fb[:, 1:3, :], Mx[:].unsqueeze(1).to_broadcast([P, 2, N4]), ALU.mult))
                    if l == 0:
                        dve.wait_ge(y_pad, s + 1)
                        for gh in range(GH):
                            if gh:
                                link(last)
                            def al(k):
                                o = gh * JP * HEADS
                                return Al[:, k, o:o + J * HEADS].rearrange("p (j h) -> p j h", h=4)\
                                    .unsqueeze(3).to_broadcast([P, J, HEADS, DIN])

                            def heads(a):
                                return a.unsqueeze(2).to_broadcast([P, J, HEADS, DIN])

                            def t4(t):
                                return t[:].rearrange("p j (h d) -> p j h d", h=HEADS)

                            TT(t4(Tc), al(0), heads(dX0[:, gh, 1:J + 1, :]), ALU.mult)
                            link(TT(t4(Td), al(1), heads(dX0[:, gh, 0:J, :]), ALU.mult))
                            link(TT(Tc[:], Tc[:], Td[:], ALU.subtract))
                            link(TT(t4(Tc), t4(Tc), heads(X0[:, gh, :, :]), ALU.add))
                            last = write_y(gh, Tc)
                        last.then_inc(y_ok, 1)
                    else:
                        alf, ref = Al.rearrange("p s n -> p (s n)"), Res.rearrange("p s n -> p (s n)")
                        link(sets(lambda part, al, re: nc.vector.tensor_copy(part(0), al), 16, alf, ref))
                        link(sets(lambda part, al, re: TT(re, al, part(0), ALU.subtract), 16, alf, ref))
                        link(sets(lambda part, al, re: nc.vector.tensor_copy(part(1), re), 16, alf, ref))
                        sets(lambda part, al, re: TT(part(2), re, part(1), ALU.subtract), 16, alf, ref).then_inc(parts_ok, 1)
                        for k in range(2):
                            dve.wait_ge(at_ps, s * 8 + 4 * (l - 1) + k + 3)
                            nc.vector.tensor_copy(AT[:, 1, k, :], bank[2 + k][0:AR, :].bitcast(bf16))\
                                .then_inc(at_dve, 1)

                def attend_any(l):
                    def per_gh(x, gh):
                        x = x[:, gh * JP * HEADS:(gh + 1) * JP * HEADS]
                        if l == 0:
                            return x.rearrange("p (j h) -> p j h", h=4)
                        return x.rearrange("p (q m h) -> p q m h", q=CJ, h=4)

                    def order(x):
                        if l == 0:
                            return x
                        return x.rearrange("p (m q) h -> p q m h", q=CJ)

                    def every_joint(x):
                        if l == 0:
                            return x.unsqueeze(1).to_broadcast([P, JP, 4])
                        return x.unsqueeze(1).unsqueeze(1).to_broadcast([P, CJ, NCH, 4])

                    def counts(jp):
                        return order(CN[:, jp, :].unsqueeze(2).to_broadcast([P, JP, 4]))

                    def scores(jp):
                        for gh in range(GH):
                            TT(per_gh(GW, gh), every_joint(S[:, gh, jp + 1, 0:4]), order(S[:, gh, 1:JP + 1, 4:8]), ALU.add)
                        TS(GK, CN[:, jp, :], 0.0, NEG, ALU.is_equal, ALU.mult)
                        dve.drain()
                        STT(GW, GW, 0.2, GW, ALU.mult, ALU.max)
                        dve.drain()
                        for gh in range(GH):
                            TT(per_gh(GW, gh), per_gh(GW, gh), order(GK.unsqueeze(2).to_broadcast([P, JP, 4])), ALU.add)
                        dve.drain()

                    def numerators(jp, again):
                        scores(jp)
                        TT(GW, GW, GM, ALU.subtract).then_inc(ge_in, 1)
                        dve.wait_ge(ge_out, ((s * 3 + l) * 2 + again) * J + jp + 1)
                        for gh in range(GH):
                            TT(per_gh(GW, gh), per_gh(GW, gh), counts(jp), ALU.mult)
                        dve.drain()

                    nc.vector.memset(GM, NEG)
                    nc.vector.memset(GD, 0.0)
                    dve.drain()
                    with dve.Fori(0, J) as jp:
                        scores(jp)
                        TT(GM, GM, GW, ALU.max)
                        dve.drain()
                    with dve.Fori(0, J) as jp:
                        numerators(jp, 0)
                        TT(GD, GD, GW, ALU.add)
                        dve.drain()
                    TS(GD, GD, 0.5, None, ALU.max)
                    dve.drain()
                    nc.vector.reciprocal(GD, GD)
                    dve.drain()
                    if l == 0:
                        nc.vector.memset(GY.rearrange("p g j r -> p (g j r)"), 0.0)
                        dve.drain()
                        with dve.Fori(0, J) as jp:
                            numerators(jp, 1)
                            TT(GW, GW, GD, ALU.mult)
                            dve.drain()
                            for gh in range(GH):
                                wj = GW[:, gh * JP * HEADS:gh * JP * HEADS + J * HEADS].rearrange("p (j h) -> p j h", h=4)
                                xj = X0[:, gh, jp, :].unsqueeze(1).unsqueeze(1).to_broadcast([P, J, HEADS, DIN])
                                TT(GT4, wj.unsqueeze(3).to_broadcast([P, J, HEADS, DIN]), xj, ALU.mult)
                                dve.drain()
                                TT(GY[:, gh, :, :], GY[:, gh, :, :], GT4.rearrange("p j h d -> p j (h d)"), ALU.add)
                                dve.drain()
                        dve.wait_ge(y_pad, s + 1)
                        for gh in range(GH):
                            last = write_y(gh, GY[:, gh, :, :])
                        last.then_inc(y_ok, 1)
                        return
                    nt = NT[l]
                    ng = (nt + 3) // 4

                    def group(jp1, g, fn):
                        gi = s * GROUPS + (0 if l == 1 else GROUPS1) + jp1 * ng + g
                        dve.wait_ge(g_mm, gi + 1)
                        for n in range(4 * g, min(4 * g + 4, nt)):
                            c, gh = task(l, n)
                            cols, o = joints(c) * P, c * NCOL
                            dst = X2[:, gh, o:o + cols] if l == 1 else X1[:, o:o + cols]
                            last = fn(dst, bank[2 + n % 4][:, 0:cols], gh or 0, joints(c))
                        last.then_inc(g_use, 1)

                    for g in range(ng):
                        group(0, g, lambda dst, src, gh, k: TS(dst, src, -1.0, None, ALU.mult))

                    def add_source(dst, src, gh, k):
                        h = HG[:, gh, :].unsqueeze(1).to_broadcast([P, k, P])
                        TT(TB[:, 0:k * P].rearrange("p (j g) -> p j g", j=k), src.rearrange("p (j g) -> p j g", j=k), h, ALU.mult)
                        dve.drain()
                        last = TT(dst, dst, TB[:, 0:k * P], ALU.add)
                        dve.drain()
                        return last

                    with dve.Fori(0, J) as jp:
                        numerators(jp, 1)
                        TT(GW, GW, GD, ALU.mult)
                        dve.drain()
                        sets(lambda part, al, re: nc.vector.tensor_copy(part(0), al), 8, GW, GR)
                        dve.drain()
                        sets(lambda part, al, re: TT(re, al, part(0), ALU.subtract), 8, GW, GR)
                        dve.drain()
                        sets(lambda part, al, re: nc.vector.tensor_copy(part(1), re), 8, GW, GR)
                        dve.drain()
                        sets(lambda part, al, re: TT(part(2), re, part(1), ALU.subtract), 8, GW, GR).then_inc(g_parts, 1)
                        dve.wait_ge(g_at, (s * 2 + (l - 1)) * J + jp + 1)
                        for g in range(ng):
                            group(jp + 1, g, add_source)

                def newton(y, v, t):
                    link(STT(t, y, -0.5, v, ALU.mult, ALU.mult))
                    link(TT(t, t, y, ALU.mult))
                    link(STT(y, t, 1.5, y, ALU.add, ALU.mult))

                def rsqrt(y, v, t):
                    link(TS(t.bitcast(i32), v.bitcast(i32), 1, None, ALU.logical_shift_right))
                    link(TS(y.bitcast(i32), t.bitcast(i32), -1.0, float(0x5f3759df), ALU.mult, ALU.add))
                    for _ in range(3):
                        newton(y, v, t)

                for l in range(3):
                    base, a0 = T0[l], T0[l] - NCH
                    if l == 0:
                        dve.wait_ge(acc_ok, s * E + 1)
                        dve.wait_ge(x0_in, s * 32 + 32)
                        for gh in range(GH):
                            sg, s2 = S[:, gh, 1:J + 1, :], S2[:, gh, 1:J + 1, :]
                            for d in range(DIN):
                                xd = X0[:, gh, :, d:d + 1].to_broadcast([P, J, 8])
                                ad = A0b[:, d:d + 1, :].to_broadcast([P, J, 8])
                                if d == 0:
                                    TT(sg, xd, ad, ALU.mult)
                                else:
                                    link(TT(s2, xd, ad, ALU.mult))
                                    link(TT(sg, sg, s2, ALU.add))
                        nc.vector.tensor_tensor(dX0[:, :, 1:J, :].rearrange("p a j d -> p a (j d)"),
                                                X0[:, :, 1:J, :].rearrange("p a j d -> p a (j d)"),
                                                X0[:, :, 0:J - 1, :].rearrange("p a j d -> p a (j d)"), ALU.subtract)
                    else:
                        dve.wait_ge(s_sb, s * 2 + l)
                    nc.vector.memset(S[:, :, 0, :], 0.0)
                    link(nc.vector.memset(S[:, :, J + 1:, :], 0.0))
                    if chain:
                        attend_chain(l)
                    else:
                        attend_any(l)

                    def neighbours(n):
                        c, gh = task(l, n)
                        k, cols = a0 + n, joints(c) * P
                        slot = gh or 0
                        if not chain:
                            if k >= 2:
                                dve.wait_ge(z_ps, s * TASKS + NCH + k - 1)
                            o = c * NCOL
                            dst = X2[:, gh, o:o + cols] if l == 1 else X1[:, o:o + cols]
                            nc.vector.tensor_copy(TA[:, k % 2, 0:cols], dst).then_inc(t_ok, 1)
                            return
                        if l == 2:
                            dve.wait_ge(t_ok, s * AGG + k + 1)
                            dve.wait_ge(d_sb, s * AGG + a0 + min(n + 2, NCH))
                            d, h = DR[:, 0, c % 2, :], HS[c % 3]
                            if c + 1 < NCH:
                                TT(d[:, cols - P:cols], HS[(c + 1) % 3][:, 0:P], h[:, cols - P:cols], ALU.subtract)
                            else:
                                nc.vector.memset(d[:, cols - P:cols], 0.0)
                            link(TT(d[:, 0:cols - P], h[:, P:cols], h[:, 0:cols - P], ALU.subtract))
                        else:
                            dve.wait_ge(d_sb, s * AGG + k + 1)
                        dve.wait_ge(a_ps, s * AGG + k + 1)
                        if k >= 2:
                            dve.wait_ge(z_ps, s * TASKS + NCH + k - 1)
                        dve.wait_ge(t_ok, s * AGG + k + 1)
                        ap, am = bA[k % 2]
                        ta = TA[:, k % 2, :]
                        TT(ta[:, 0:cols], ap[:, 0:cols], DR[:, slot, c % 2, 0:cols], ALU.mult)
                        if c == 0:
                            nc.vector.memset(TB[:, 0:P], 0.0)
                        else:
                            TT(TB[:, 0:P], am[:, 0:P], DR[:, slot, (c - 1) % 2, NCOL - P:NCOL], ALU.mult)
                        link(TT(TB[:, P:cols], am[:, P:cols], DR[:, slot, c % 2, 0:cols - P], ALU.mult))
                        TT(ta[:, 0:cols], ta[:, 0:cols], TB[:, 0:cols], ALU.subtract).then_inc(t_ok, 1)

                    def normalise(n):
                        c, gh = task(l, n)
                        k, cols = base + n, joints(c) * P
                        o = c * NCOL
                        dve.wait_ge(r_ps, s * TASKS + k + 1)
                        dst = X2[:, gh, o:o + cols] if l == 1 else X1[:, o:o + cols]
                        TT(dst, dst, bA[n % 2][n // 2 % 2][:, 0:cols], ALU.mult).then_inc(u_ok, 1)

                    if l:
                        for n in range(NT[l]):
                            neighbours(n)
                    dve.wait_ge(v_ps, s * TASKS + base + NT[l])
                    TS(VB, bV[0:VR, :], EPS, None, ALU.add).then_inc(var_ok, 1)
                    dve.wait_ge(sd_ok, s * 3 + l + 1)
                    link(nc.vector.reciprocal(RV, RV))
                    newton(RV, VB, RN)
                    link(nc.vector.tensor_copy(RP[0:VR, :], RV))
                    link(TT(VB, RV, RP[0:VR, :], ALU.subtract))
                    nc.vector.tensor_copy(RP[32:32 + VR, :], VB)
                    link(nc.vector.tensor_copy(RM, VB))
                    TT(RP[64:64 + VR, :], VB, RM, ALU.subtract).then_inc(rp_ok, 1)
                    dve.wait_ge(zs_ok, s * TASKS + base + NT[l])
                    for n in range(NT[l]):
                        normalise(n)

                def stats(srcs):
                    n = len(srcs)
                    for t, src in enumerate(srcs):
                        last = nc.vector.bn_stats(st[:, t, :], src)
                    link(last)
                    nc.vector.memset(carrier[:, 1:2], 0.0)
                    for t in range(n):
                        last = nc.vector.bn_aggr(mv[:, t, :], st[:, t, :])
                    link(last)
                    link(TS(rv[:, 0:n], mv[:, 0:n, 1], EPS, None, ALU.add))
                    rsqrt(rs[:, 0:n], rv[:, 0:n], rt[:, 0:n])

                dve.wait_ge(fp_ps, s + 1)
                pose = Hf[:].rearrange("p (g h) d -> p g h d", g=GH)[:, :, 0, :]

                def row(k):
                    return rows[:, k * P:k * P + P].unsqueeze(1).to_broadcast([P, GH, P])

                for gh in range(GH):
                    last = TT(Hf[:, 2 * gh, :], bank[3 + gh][:, 0:P], rows[:, 0:P], ALU.add)
                link(last)
                stats([Hf[:, 0, :], Hf[:, 2, :]])
                for gh in range(GH):
                    h = Hf[:, 2 * gh, :]
                    last = TS(h, h, mv[:, gh, 0:1], rs[:, gh:gh + 1], ALU.subtract, ALU.mult)
                link(last)
                link(TT(pose, pose, row(1), ALU.mult))
                link(TT(pose, pose, row(2), ALU.add))
                dve.wait_ge(txt_in, s * 32 + 32)
                stats([Hf[:, t, :] for t in range(4)])
                for t in range(4):
                    last = TS(Xn[:, t, :], Hf[:, t, :], mv[:, t, 0:1], rs[:, t:t + 1], ALU.subtract, ALU.mult)
                last.then_inc(h_ok, 1)
                dve.wait_ge(q2_sb, s + 1)
                qd = QD.rearrange("p (b t) -> p b t", b=GH)
                link(TS(qd, QC[:, :, 3:3 + 2 * P], v("cw3"), None, ALU.mult))
                for k in range(3):
                    ins = STT(qd, QC[:, :, k:k + 2 * P], v(f"cw{k}"), qd, ALU.mult, ALU.add)
                    if k < 2:
                        link(ins)
                ins.then_inc(cv_ok, 1)
                dve.wait_ge(ss_ps, s + 1)
                TS(NV, bank[4][0:1, :], 1e-24, None, ALU.max).then_inc(nv_ok, 1)
                dve.wait_ge(nsd_ok, s + 1)
                link(nc.vector.reciprocal(NR, NR))
                link(STT(RN[0:1, :], NR, -0.5, NV, ALU.mult, ALU.mult))
                link(TT(RN[0:1, :], RN[0:1, :], NR, ALU.mult))
                STT(NR, RN[0:1, :], 1.5, NR, ALU.add, ALU.mult).then_inc(nr_ok, 1)
                dve.wait_ge(nb_ps, s + 1)
                TT(KN, QD, bank[5][:], ALU.mult).then_inc(kn_ok, 1)
                dve.wait_ge(o_ps, s + 1)
                dve.wait_ge(stored, s * 32 + 1)
                hof, hff = Ho[:].rearrange("p t d -> p (t d)"), Hf[:].rearrange("p t d -> p (t d)")
                link(TT(hof, bank[0][:], hff, ALU.add))
                stats([Ho[:, t, :] for t in range(4)])
                for t in range(4):
                    last = TS(Xn[:, t, :], Ho[:, t, :], mv[:, t, 0:1], rs[:, t:t + 1], ALU.subtract, ALU.mult)
                last.then_inc(ho_ok, 1)
                dve.wait_ge(lg_ps, s + 1)
                lg3 = bank[2][:, 0:32].rearrange("p (t e) -> p t e", t=4)
                link(nc.vector.tensor_reduce(mx4[:], lg3, mybir.AxisListType.X, ALU.max))
                m3 = mx4[:].unsqueeze(2).to_broadcast([P, 4, 8])
                TT(LG[:], lg3, m3, ALU.subtract).then_inc(lgm_ok, 1)
                dve.wait_ge(rexp_ok, s + 1)
                link(nc.vector.tensor_reduce(den4[:], LG[:], mybir.AxisListType.X, ALU.add))
                link(nc.vector.reciprocal(den4[:], den4[:]))
                link(TT(PB[:], LG[:], den4[:].unsqueeze(2).to_broadcast([P, 4, 8]), ALU.mult))
                nc.vector.memset(carrier[:, 1:2], 0.0)
                for t in range(4):
                    last = nc.vector.max(top[:, t, :], PB[:, t, :])
                link(last)
                nc.vector.memset(carrier[:, 1:2], 0.0)
                for t in range(4):
                    last = nc.vector.max_index(tix[:, t, :], top[:, t, :], PB[:, t, :])
                link(last)
                link(nc.vector.tensor_copy(tif[:], tix[:]))
                link(TT(mx4[:], top[:, :, 0], top[:, :, 1], ALU.add))
                link(TS(mx4[:], mx4[:], 1e-9, None, ALU.add))
                link(nc.vector.reciprocal(mx4[:], mx4[:]))
                link(TT(gw[:], top[:, :, 0:2], mx4[:].unsqueeze(2).to_broadcast([P, 4, 2]), ALU.mult))
                i3 = iota8[:].rearrange("p (t e) -> p t e", t=4)
                for k in range(2):
                    g = gate if k == 0 else gtmp
                    link(TT(g[:], i3, tif[:, :, k:k + 1].to_broadcast([P, 4, 8]), ALU.is_equal))
                    link(TT(g[:], g[:], gw[:, :, k:k + 1].to_broadcast([P, 4, 8]), ALU.mult))
                TT(gate[:], gate[:], gtmp[:], ALU.add).then_inc(gate_ok, 1)
                dve.wait_ge(gate_ok, s + 1)
                dve.wait_ge(bo_ps, s + 1)
                link(TT(hof, bank[2][:], hof, ALU.add))
                for e in range(E):
                    dve.wait_ge(eo_ps, s * E + e + 2)
                    if e:
                        dve.wait_ge(acc_ok, s * E + e + 1)
                    for t in range(4):
                        last = STT(Ho[:, t, :], bank[e % 2][:, t * P:t * P + P], gate[:, t, e:e + 1], Ho[:, t, :],
                                   ALU.mult, ALU.add)
                    last.then_inc(acc_ok, 1)
                assert links[0] == per_step, links[0]


            dve.wait_ge(flag_ok, 1)
            graph = dve.value_load(flag[0:1, 0:1])
            with dve.If(graph == 0):
                with dve.Fori(0, STEPS) as s:
                    step(s, True)
            with dve.If(graph != 0):
                with dve.Fori(0, STEPS) as s:
                    step(s, False)

def _layout(i):
    f = np.float32
    a = {k: np.asarray(x) for k, x in i.items()}
    t = {k[7:]: x for k, x in a.items() if k.startswith("L0_tok_")}
    m = {k[8:]: x for k, x in a.items() if k.startswith("L0_attn_")}
    n = {k[7:]: x for k, x in a.items() if k.startswith("L0_ffn_")}
    o = {}
    o["x"] = a["x"].reshape(STEPS, GH, P, J, DIN)
    o["txt"] = a["txt"].reshape(STEPS, GH, P, P)

    def blocks(s, d):
        h, c = s.shape
        r = np.zeros((h, c, 2, h), f)
        for k in range(h):
            r[k, :, 0, k] = s[k]
            r[k, :, 1, k] = d[k]
        return r.reshape(h * c, 2 * h)

    def twice(x, axis=0):
        return np.concatenate([x, x], axis)

    for l in range(3):
        o[f"abd{l}"] = blocks(t[f"as{l}"], t[f"ad{l}"])
    o["W0T"] = t["W0"].T
    rows0 = np.zeros((16, HEADS, F0 // HEADS), f)
    for h in range(HEADS):
        rows0[3 * h:3 * h + 3, h] = t["W0"].reshape(DIN, HEADS, -1)[:, h]
    rows0[12:15] = t["R0"].reshape(DIN, HEADS, -1)
    rows0[15] = t["bg0"].reshape(HEADS, -1)
    raw = np.zeros((F0, CJ, GH, GH, CJ, 16), f)
    for j in range(CJ):
        for g in range(GH):
            raw[:, j, g, g, j, :] = rows0.reshape(16, F0).T
    o["raw0"] = raw.reshape(F0, CJ * GH * P)
    o["edges"] = t["edge_index"].reshape(2, 2, J_EDGES // 2).transpose(2, 0, 1).reshape(J_EDGES // 2, 4)
    o["iota"] = np.broadcast_to(np.arange(JP, dtype=f)[None], (P, JP))
    apart = np.arange(J)[:, None] - np.arange(JP)[None]
    chain = ((abs(apart) <= 1) & (np.arange(JP) < J)[None]).astype(f)
    o["chain"] = np.broadcast_to(chain.reshape(1, J * JP), (P, J * JP))
    o["W1T"], o["R1T"], o["W1"] = twice(t["W1"].T, 1), twice(t["R1"].T, 1), twice(t["W1"])
    o["W2T"], o["R2T"], o["W2"] = t["W2"].T, t["R2"].T, t["W2"]

    def centre(k):
        return np.eye(k, dtype=f) - f(1.0 / k)

    def twin(x):
        z = np.zeros_like(x)
        return np.block([[x, z], [z, x]])

    o["C1"], o["C2"] = centre(F1), twin(centre(F2))
    v1, v2 = np.zeros((P, 2 * VR - 1), f), np.zeros((P, 2 * VR - 1), f)
    v1[:, VR - 1] = 1.0 / F1
    v2[:F2, VR - 1] = 1.0 / F2
    v2[F2:, VR - 1 + NCH] = 1.0 / F2
    o["V1"], o["V2"] = v1, v2
    r1, r2 = np.zeros((RR, GH * NCH, P), f), np.zeros((RR, NCH, P), f)
    for part in range(3):
        for c in range(NCH):
            for g in range(GH):
                r1[32 * part + g * NCH + c, g * NCH + c] = 1.0
                r2[32 * part + g * NCH + c, c, F2 * g:F2 * g + F2] = 1.0
    o["selr1"], o["selr2"] = r1.reshape(RR, -1), r2.reshape(RR, -1)
    o["ones"], o["ident"] = np.ones((P, P), f), np.eye(P, dtype=f)
    for name, width in (("sel1", F1), ("sel2", F2)):
        s = np.zeros((3, JS, HEADS, JS, HEADS, width // HEADS), f)
        for j in range(JS):
            for h in range(HEADS):
                s[:, j, h, j, h, :] = 1.0
        o[name] = s.reshape(AR, JS * width)
    cols = [t["bg1"], twice(t["bg2"]), twice(t["g0"]), twice(t["b0"]), t["g1"], t["b1"], twice(t["g2"]), twice(t["b2"]),
            m["conv_q_b"]] + [m["conv_q_w"][:, 0, k] for k in range(4)]
    o["vec"] = np.concatenate([np.stack(cols, 1), n["b1"].reshape(E * MT, P).T], 1)
    o["rows"] = np.broadcast_to(np.concatenate([t["fpb"], t["fng"], t["fnb"]])[None], (P, 3 * P))
    o["fpW"] = twice(t["fpW"].reshape(J, F2, P).transpose(1, 0, 2).reshape(F2, J * P))
    o["wq1"], o["wq2"], o["wout"] = m["w_q1"].T, m["w_q2"].T, m["w_out"].T
    o["mw1"] = m["mem_w1"].T
    o["mw2"] = m["mem_w2"].T.reshape(2, P, P).transpose(1, 0, 2).reshape(P, 2 * P)
    o["rw"] = n["router_w"].T
    o["w1"] = n["w1"].transpose(2, 0, 1).reshape(P, E * FF)
    o["w2"] = n["w2"].transpose(2, 0, 1).reshape(MT, P, E, P).transpose(1, 2, 0, 3).reshape(P, E * FF)
    o["b2"] = n["b2"]
    o["iota8"] = np.broadcast_to(np.tile(np.arange(8, dtype=f), 4)[None], (P, 32))
    return {k: np.ascontiguousarray(x) for k, x in o.items()}


def kernel(**inputs):
    import concourse.bacc as _bacc
    from concourse.bass_utils import run_bass_kernel_spmd as _run

    laid = _layout(inputs)
    nc = _bacc.Bacc("TRN2", target_bir_lowering=False, num_devices=1)
    arrays, aps = {}, {}
    for name, a in laid.items():
        arrays[f"in_{name}"] = a
        aps[name] = nc.dram_tensor(f"in_{name}", a.shape, mybir.dt.from_np(a.dtype), kind="ExternalInput").ap()
    out = nc.dram_tensor("out_0", (STEPS, GH, 2, P, P), mybir.dt.float32, kind="ExternalOutput").ap()
    build(nc, aps, out)
    r = _run(nc, [arrays], core_ids=[0])
    return r.results[0]["out_0"].reshape(STEPS * GH, 2 * P, P)
```

```python
import numpy as np
import concourse.bass as bass
from concourse import mybir
from contextlib import ExitStack

G, J, DIN = 4096, 50, 3
HEADS = 4
F0, F1, F2 = 64, 128, 64
P = 128
GH = 2
STEPS = G // (P * GH)
J_EDGES = 2 * (J - 1) + J
CJ = 4
NCH = (J + CJ - 1) // CJ
NCOL = CJ * P
JP = NCH * CJ
JS = 10
AR = 3 * JS * HEADS
NT = [NCH, GH * NCH, NCH]
T0 = [0, NCH, 3 * NCH]
TASKS = 4 * NCH
AGG = TASKS - NCH
TOK = GH * 2 * P
E, FF = 8, 512
MT = FF // P
HID = 256
GROUPS1, GROUPS2 = (J + 1) * 7, (J + 1) * 4
GROUPS = GROUPS1 + GROUPS2
VR = GH * NCH
SR = 8 * NCH
C1S = (NCH + 1) // 2
SR1 = C1S * GH * 8
RR = 3 * VR
NEG = -3.0e38
EPS = 1e-5


def joints(c):
    return min(CJ, J - CJ * c)


def task(l, n):
    return (n // GH, n % GH) if l == 1 else (n, None)


def build(nc, A, out):
    fp32, bf16, i32, u32 = mybir.dt.float32, mybir.dt.bfloat16, mybir.dt.int32, mybir.dt.uint32
    ALU, ACT = mybir.AluOpType, mybir.ActivationFunctionType
    ctx = ExitStack()
    with ctx:
        def sb(name, shape, dt=fp32):
            return ctx.enter_context(nc.sbuf_tensor(name, shape, dt))

        def sem(name):
            return ctx.enter_context(nc.semaphore(name))

        consts = {}

        def const(name):
            consts[name] = sb("c_" + name, list(A[name].shape))[:]
            return consts[name]

        X2 = sb("X2", [P, GH, J * P])
        X2f = X2[:].rearrange("p a n -> p (a n)")
        setup_at = [0]

        def setup_const(name, dtype=fp32):
            p, n = A[name].shape
            consts[name] = X2f[0:p, setup_at[0]:setup_at[0] + n].bitcast(dtype)
            setup_at[0] += n
            return consts[name]

        W0T, abd0 = setup_const("W0T"), setup_const("abd0")
        raw0 = setup_const("raw0")
        W1T, R1T, abd1, W1 = setup_const("W1T"), setup_const("R1T"), setup_const("abd1"), const("W1")
        W2T, R2T, abd2, W2 = setup_const("W2T"), setup_const("R2T"), setup_const("abd2"), const("W2")
        C1, C2, ones, ident = (const(n) for n in ("C1", "C2", "ones", "ident"))
        V1, V2 = const("V1"), const("V2")
        sel1f, sel2f = setup_const("sel1"), setup_const("sel2")
        selr1f, selr2f = setup_const("selr1"), setup_const("selr2")
        vec = const("vec")
        rows = const("rows")
        fpW = const("fpW")
        wq1, wq2, mw1, mw2, wout = (const(n) for n in ("wq1", "wq2", "mw1", "mw2", "wout"))
        rw, w1, w2, b2 = const("rw"), const("w1"), const("w2"), const("b2")
        iota8 = const("iota8")
        VEC = {n: k for k, n in enumerate(["bg1", "bg2", "g0", "b0", "g1", "b1", "g2", "b2",
                                           "cb", "cw0", "cw1", "cw2", "cw3"])}
        FB1 = len(VEC)

        def v(name):
            return vec[:, VEC[name]:VEC[name] + 1]

        edges, iota = setup_const("edges", i32), setup_const("iota")
        chain_counts = setup_const("chain")

        A0b = sb("A0b", [P, DIN, 8])
        A1 = sb("A1", [P, 2 * SR1 - 16])
        A2 = sb("A2", [P, 2 * SR - 8])
        WR1 = sb("WR1", [P, F1])
        WR2 = sb("WR2", [P, F2])
        W0bd = sb("W0bd", [P, CJ, P])
        bgc = sb("bgc", [P, 2])
        sel1 = sb("sel1b", [AR, JS, P], bf16)
        sel2 = sb("sel2b", [AR, JS, F2], bf16)
        selr1 = sb("selr1b", [RR, GH * NCH, P], bf16)
        selr2 = sb("selr2b", [RR, NCH, P], bf16)
        identb = sb("identb", [P, P], bf16)

        X0 = sb("X0", [P, GH, J, DIN])
        dX0 = sb("dX0", [P, GH, J + 1, DIN])
        N4 = GH * JP * HEADS
        NS = GH * (JP + 2) * 8
        R = sb("R", [P, 2 * NS + 6 * N4])
        DX = R[:, 0:2 * NCOL].rearrange("p (a n) -> p a n", a=2)
        DR = R[:, 2 * NCOL:6 * NCOL].rearrange("p (g a n) -> p g a n", g=GH, a=2)
        TA = R[:, 6 * NCOL:8 * NCOL].rearrange("p (a n) -> p a n", a=2)
        S = R[:, 0:NS].rearrange("p (a j r) -> p a j r", a=GH, r=8)
        Res = R[:, NS:NS + 2 * N4].rearrange("p (a n) -> p a n", a=2)
        Fb = R[:, 2 * NS:2 * NS + 3 * N4].rearrange("p (a n) -> p a n", a=3)
        Mx = R[:, 2 * NS + 3 * N4:2 * NS + 4 * N4]
        Al = R[:, 2 * NS + 4 * N4:2 * NS + 6 * N4].rearrange("p (a n) -> p a n", a=2)
        Pt = sb("Pt", [P, 4 * CJ, 2, 3, JS * HEADS], bf16)
        AT = sb("AT", [AR, 2, GH, 2 * CJ * P], bf16)
        NY = GH * NCH * CJ * 16
        y0 = 2 * MT * TOK + 3 * N4
        Y = X2f[:, y0:y0 + NY].rearrange("p (c a j r) -> p c a j r", c=NCH, a=GH, r=16)
        YT = X2f[:, y0 + NY:y0 + NY + NCH * P]
        X1 = sb("X1", [P, (J + 1) * P])
        t0 = 4 * NCOL + 2 * NS
        S2 = X1[:, 4 * NCOL:4 * NCOL + NS].rearrange("p (a j r) -> p a j r", a=GH, r=8)
        S0 = X1[:, 4 * NCOL + NS:t0].rearrange("p (a j r) -> p a j r", a=GH, r=8)
        Tc = X1[:, t0:t0 + 12 * J].rearrange("p (j r) -> p j r", j=J)
        Td = X1[:, t0 + 12 * J:t0 + 24 * J].rearrange("p (j r) -> p j r", j=J)
        F0b = X1[:, t0 + 24 * J:t0 + 24 * J + 3 * N4].rearrange("p (a n) -> p a n", a=3)
        m0 = y0 + NY + NCH * P
        M0 = X2f[:, m0:m0 + N4]
        Al0 = X2f[:, m0 + N4:m0 + 3 * N4].rearrange("p (a n) -> p a n", a=2)
        HS = [R[:, k * NCOL:(k + 1) * NCOL] for k in (0, 1, 4)]
        TB = sb("TB", [P, NCOL])

        def edge_scores(l):
            at = X2f[:, 2 * MT * TOK:2 * MT * TOK + 3 * N4] if l < 2 else X1[:, 0:3 * N4]
            return at.rearrange("p (k a n) -> p k a n", k=3, a=GH)

        def score_rows(l):
            at = X2f[0:SR1, 0:2 * NCOL] if l < 2 else X1[0:SR, 4 * NCOL:6 * NCOL]
            return at.rearrange("p (g n) -> p g n", g=2)

        SQ = sb("SQ", [P, 2, NCOL])
        EH = J_EDGES // 2
        EN = SQ[0:EH, 1, 0:4]
        HOT_S = SQ[0:EH, 0, 0:2 * J].rearrange("e (t j) -> e t j", t=2)
        HOT_D = SQ[0:EH, 0, 2 * J:2 * J + 2 * JP].rearrange("e (t j) -> e t j", t=2)
        CN = R[:, 2 * NCOL:2 * NCOL + J * JP // 2].bitcast(bf16).rearrange("p (j i) -> p j i", j=J)
        other = sb("other", [P, 1])
        flag = sb("flag", [P, 1], i32)
        g0 = 2 * NCOL + J * JP // 2 + 8
        GM, GD, GW, GR = (R[:, g0 + k * N4:g0 + (k + 1) * N4] for k in range(4))
        GK = SQ[:, 0, 2 * P:2 * P + JP]
        XJ = SQ[:, 1, 0:2 * P].rearrange("p (g n) -> p g n", g=GH)
        HG = SQ[:, 0, 0:2 * P].rearrange("p (g n) -> p g n", g=GH)
        GY = X1[:, 0:GH * J * 12].rearrange("p (g j r) -> p g j r", g=GH, r=12)
        GT4 = X1[:, GH * J * 12:GH * J * 12 + J * 12].rearrange("p (j h d) -> p j h d", h=HEADS, d=DIN)
        NVR = CJ * VR
        VW = TA[0:VR, 1, :]
        VB = TA[:, 0, 0:NVR]
        RV = TB[:, 0:NVR]
        RN = DX[:, 0, 0:NVR]
        RG = DX[:, 1, 0:CJ * RR // 2].bitcast(bf16).rearrange("p (q k n) -> p q k n", q=CJ, k=3)
        RP = sb("RP", [RR, NCOL], bf16)
        mhalf = sb("mhalf", [P, 1])
        carrier = sb("carrier", [P, 3])
        Hf = sb("Hf", [P, 4, P])
        Ho = sb("Ho", [P, 4, P])
        Xn = R[:, NCOL:2 * NCOL].rearrange("p (t d) -> p t d", t=4)
        st = sb("st", [P, 4, 6])
        mv = sb("mv", [P, 4, 2])
        rs, rv, rt = sb("rs", [P, 4]), sb("rv", [P, 4]), sb("rt", [P, 4])
        XT = R[:, 0:TOK]
        Q1, QD, KN, GT = (X1[:, k * NCOL:(k + 1) * NCOL] for k in range(4))
        QC = sb("QC", [P, GH, 3 + 2 * P])
        QS = SQ[:, 0, :]
        MH = TA
        RT = TB[:]
        LG, PB, top, gtmp = (R[:, k:k + 32].rearrange("p (t e) -> p t e", t=4)
                             for k in range(8 * NCOL, 8 * NCOL + 128, 32))
        mx4 = sb("mx4", [P, 4])
        den4 = sb("den4", [P, 4])
        tix = sb("tix", [P, 4, 8], u32)
        gw = sb("gw", [P, 4, 2])
        gate, tif = LG, PB
        HD = X2f[:, 0:2 * MT * TOK].rearrange("p (a m t) -> p a m t", a=2, m=MT)

        bank = [ctx.enter_context(nc.psum_tensor(f"bank{i}", [P, NCOL], fp32)) for i in range(8)]
        bD, bV = bank[0], bank[5]
        bA = [[bank[1], bank[2]], [bank[6], bank[7]]]
        bZ = [bank[3], bank[4]]

        c_loaded = sem("c_loaded")
        setup_ps = sem("setup_ps")
        setup_sb = sem("setup_sb")
        seeded = sem("seeded")
        x0_in = sem("x0_in")
        txt_in = sem("txt_in")
        sr_ps = sem("sr_ps")
        sr_sb = sem("sr_sb")
        s_ps = sem("s_ps")
        s_sb = sem("s_sb")
        f_ok = sem("f_ok")
        exp_ok = sem("exp_ok")
        parts_ok = sem("parts_ok")
        at_ps = sem("at_ps")
        at_act = sem("at_act")
        at_dve = sem("at_dve")
        y_pad = sem("y_pad")
        y_ok = sem("y_ok")
        yt_ps = sem("yt_ps")
        yt_sb = sem("yt_sb")
        a_ps = sem("a_ps")
        d_ps = sem("d_ps")
        d_sb = sem("d_sb")
        t_ok = sem("t_ok")
        z_ps = sem("z_ps")
        zs_ok = sem("zs_ok")
        sq_ok = sem("sq_ok")
        v_ps = sem("v_ps")
        vw_sb = sem("vw_sb")
        vt_ps = sem("vt_ps")
        rg_ok = sem("rg_ok")
        rg_ps = sem("rg_ps")
        rp_ok = sem("rp_ok")
        r_ps = sem("r_ps")
        u_ok = sem("u_ok")
        x_ok = sem("x_ok")
        dx_ok = sem("dx_ok")
        fp_ps = sem("fp_ps")
        h_ok = sem("h_ok")
        xt_ps = sem("xt_ps")
        xt_sb = sem("xt_sb")
        q1_ps = sem("q1_ps")
        q1_sb = sem("q1_sb")
        q2_ps = sem("q2_ps")
        q2_sb = sem("q2_sb")
        cv_ok = sem("cv_ok")
        cs_self = sem("cs_self")
        cs_ok = sem("cs_ok")
        ss_ps = sem("ss_ps")
        nr_ok = sem("nr_ok")
        nb_ps = sem("nb_ps")
        kn_ok = sem("kn_ok")
        mh_ps = sem("mh_ps")
        mh_sb = sem("mh_sb")
        rt_ps = sem("rt_ps")
        rt_sb = sem("rt_sb")
        o_ps = sem("o_ps")
        ho_ok = sem("ho_ok")
        lg_ps = sem("lg_ps")
        lgm_ok = sem("lgm_ok")
        rexp_ok = sem("rexp_ok")
        gate_ok = sem("gate_ok")
        gt_ps = sem("gt_ps")
        gt_sb = sem("gt_sb")
        bo_ps = sem("bo_ps")
        hid_ps = sem("hid_ps")
        hid_sb = sem("hid_sb")
        eo_ps = sem("eo_ps")
        acc_ok = sem("acc_ok")
        stored = sem("stored")
        dve_link = sem("dve_link")
        en_ok = sem("en_ok")
        hot_ok = sem("hot_ok")
        cn_ps = sem("cn_ps")
        flag_ok = sem("flag_ok")
        ge_in = sem("ge_in")
        ge_out = sem("ge_out")
        g_xj = sem("g_xj")
        g_parts = sem("g_parts")
        g_tp = sem("g_tp")
        g_at = sem("g_at")
        g_mm = sem("g_mm")
        g_use = sem("g_use")

        block = ctx.enter_context(nc.Block())
        NCONST = len(consts)

        @block.sync
        def _(sp):
            for primed in (g_use, y_ok, ho_ok, eo_ps, d_ps, acc_ok, hid_sb, t_ok, stored):
                sp.sem_inc(primed, 1)
            for name, t in consts.items():
                sp.dma_start(t, A[name]).then_inc(c_loaded, 16)
            for gh in range(GH):
                sp.dma_start(X0[:, gh, :, :], A["x"][0, gh]).then_inc(x0_in, 16)
            def step(s, chain):
                sp.wait_ge(y_ok, s + 2)
                for gh in range(GH):
                    sp.dma_start(X0[:, gh, :, :], A["x"][s + 1, gh]).then_inc(x0_in, 16)
                sp.wait_ge(ho_ok, s + 1)
                for gh in range(GH):
                    sp.dma_start(Hf[:, 2 * gh + 1, :], A["txt"][s, gh]).then_inc(txt_in, 16)

            sp.wait_ge(flag_ok, 1)
            graph = sp.value_load(flag[0:1, 0:1])
            with sp.If(graph == 0):
                with sp.Fori(0, STEPS) as s:
                    step(s, True)
            with sp.If(graph != 0):
                with sp.Fori(0, STEPS) as s:
                    step(s, False)

        @block.gpsimd
        def _(pool):
            nc.gpsimd.memset(dX0[:], 0.0)
            nc.gpsimd.memset(mhalf[:], -0.5)
            nc.gpsimd.memset(Pt[:], 0.0)
            nc.gpsimd.memset(A1[:], 0.0)
            nc.gpsimd.memset(A2[:], 0.0)
            nc.gpsimd.memset(X1[:, J * P:], 0.0)
            nc.gpsimd.memset(QC[:], 0.0).then_inc(seeded, 1)
            pool.wait_ge(seeded, 1)
            pool.wait_ge(setup_sb, 2)
            nc.gpsimd.memset(Y[:].rearrange("p c a j r -> p (c a j r)"), 1.0).then_inc(y_pad, 1)
            def step(s, chain):
                if chain:
                    pool.wait_ge(parts_ok, s * 2 + 1)
                for c in range(NCH) if chain else ():
                    n = joints(c) * P
                    last = min(NCH - 1, (CJ * c + joints(c)) // CJ)
                    pool.wait_ge(x_ok, s * TASKS + last + 1)
                    if c >= 2:
                        pool.wait_ge(d_ps, s * AGG + GH * (c - 1) + 1)
                    else:
                        pool.wait_ge(d_ps, s * AGG + 1)
                    o = c * NCOL
                    nc.gpsimd.tensor_tensor(DX[:, c % 2, 0:n], X1[:, o + P:o + P + n], X1[:, o:o + n],
                                            ALU.subtract).then_inc(dx_ok, 1)
                pool.wait_ge(fp_ps, s + 1)
                nc.gpsimd.tensor_tensor(carrier[:, 0:1], mhalf[:], mhalf[:], ALU.add)
                nc.gpsimd.memset(Y[:].rearrange("p c a j r -> p (c a j r)"), 1.0).then_inc(y_pad, 1)

            pool.wait_ge(flag_ok, 1)
            graph = pool.value_load(flag[0:1, 0:1])
            with pool.If(graph == 0):
                with pool.Fori(0, STEPS) as s:
                    step(s, True)
            with pool.If(graph != 0):
                with pool.Fori(0, STEPS) as s:
                    step(s, False)

        @block.tensor
        def _(pe):
            pe.wait_ge(c_loaded, 16 * NCONST)
            mm = nc.tensor.matmul
            for d in range(DIN):
                mm(bank[0][:, 8 * d:8 * d + 8], W0T[:, d:d + 1].to_broadcast([F0, P]), abd0[:], start=True, stop=True)
            mm(bank[0][:, 32:40], W1T[:], abd1[:], start=True, stop=True)
            mm(bank[0][:, 40:48], W2T[:], abd2[:], start=True, stop=True)
            mm(bank[0][:, 48:49], C1[:], v("bg1"), start=True, stop=True)
            mm(bank[0][:, 49:50], C2[:], v("bg2"), start=True, stop=True)
            mm(bank[1][:, 0:F1], W1T[:], C1[:], start=True, stop=False)
            mm(bank[1][:, 0:F1], R1T[:], C1[:], start=False, stop=True)
            mm(bank[2][:, 0:F2], W2T[:], C2[0:F2, 0:F2], start=True, stop=False)
            mm(bank[2][:, 0:F2], R2T[:], C2[0:F2, 0:F2], start=False, stop=True)
            for q in range(CJ * GH):
                last = mm(bank[3][:, F0 * q:F0 * q + F0], raw0[:, P * q:P * q + P], C2[0:F0, 0:F0], start=True, stop=True)
            last.then_inc(setup_ps, 1)
            pe.wait_ge(setup_sb, 2)
            pe.wait_ge(hot_ok, 1)
            for j in range(J):
                for t in range(2):
                    last = mm(bank[j // 9][:, j % 9 * JP:(j % 9 + 1) * JP], HOT_S[:, t, j:j + 1].to_broadcast([EH, P]),
                              HOT_D[:, t, :], start=(t == 0), stop=(t == 1))
            last.then_inc(cn_ps, 1)
            pe.wait_ge(setup_sb, 2)
            def keep_warm(k, b=bV):
                for _ in range(k):
                    mm(b[:], sel1[:, 0, :], sel1[:, 0:4, :].rearrange("p j f -> p (j f)"), start=True, stop=True)

            def neighbours_any(s, l):
                nt = NT[l]
                ng = (nt + 3) // 4

                def group(jp1, g):
                    gi = s * GROUPS + (0 if l == 1 else GROUPS1) + jp1 * ng + g
                    pe.wait_ge(g_use, gi + 1)

                for g in range(ng):
                    group(0, g)
                    for n in range(4 * g, min(4 * g + 4, nt)):
                        c, gh = task(l, n)
                        cols, o, b = joints(c) * P, c * NCOL, bank[2 + n % 4]
                        if l == 1:
                            r = slice(64 * gh, 64 * gh + 64)
                            last = mm(b[:, 0:cols], W1[r, :], X1[r, o:o + cols], start=True, stop=True)
                        else:
                            for h in range(GH):
                                last = mm(b[64 * h:64 * h + 64, 0:cols], W2[:], X2[:, h, o:o + cols], start=True, stop=True)
                    last.then_inc(g_mm, 1)
                with pe.Fori(0, J) as jp:
                    pe.wait_ge(g_parts, (s * 2 + (l - 1)) * J + jp + 1)
                    for gh in range(GH):
                        atp = bank[gh][:].bitcast(bf16)
                        for t in range(2):
                            for q in range(CJ):
                                o = (t * CJ + q) * P
                                nc.tensor.transpose(atp[0:AR, o:o + P],
                                                    Pt[:, gh * CJ + q, t, :, :].rearrange("p k n -> p (k n)"), identb[:])
                    pe.wait_ge(g_xj, (s * 2 + (l - 1)) * J + jp + 1)
                    for gh in range(GH):
                        if l == 1:
                            r = slice(64 * gh, 64 * gh + 64)
                            last = mm(bank[6 + gh][:, 0:P], W1[r, :], XJ[r, 0, :], start=True, stop=True)
                        else:
                            last = mm(bank[6][64 * gh:64 * gh + 64, 0:P], W2[:], XJ[:, gh, :], start=True, stop=True)
                    last.then_inc(g_tp, 1)
                    pe.wait_ge(g_at, (s * 2 + (l - 1)) * J + jp + 1)
                    for g in range(ng):
                        group(jp + 1, g)
                        for n in range(4 * g, min(4 * g + 4, nt)):
                            c, gh = task(l, n)
                            cols, o, b = joints(c) * P, (c // JS) * NCOL, bank[2 + n % 4]
                            if l == 1:
                                last = mm(b[:, 0:cols], sel1[:, c % JS, :], AT[:, 0, gh, o:o + cols], start=True, stop=True)
                            else:
                                for h in range(GH):
                                    last = mm(b[64 * h:64 * h + 64, 0:cols], sel2[:, c % JS, :], AT[:, 0, h, o:o + cols],
                                              start=True, stop=True)
                        last.then_inc(g_mm, 1)

            def step(s, chain):
                pe.wait_ge(y_ok, s + 2)
                pe.wait_ge(hid_sb, s * E * MT + 1)
                for b in range(4):
                    for c in range(4 * b, min(4 * b + 4, NCH)):
                        last = nc.tensor.transpose(bank[4 + b][:, (c - 4 * b) * P:(c - 4 * b + 1) * P],
                                                   Y[:, c, :, :, :].rearrange("p a j r -> p (a j r)"), ident)
                    last.then_inc(yt_ps, 1)
                for l in range(3):
                    base, a0 = T0[l], T0[l] - NCH
                    if l == 0:
                        pe.wait_ge(yt_sb, s * 4 + 4)
                    else:
                        pe.wait_ge(sr_sb, s * 2 + l)
                        SC = score_rows(l)
                        nr = SR1 if l == 1 else SR
                        for b in range(2):
                            for q in range(CJ):
                                last = nc.tensor.transpose(bank[6 + b][:, q * nr:q * nr + nr], SC[:, b, q * P:q * P + P],
                                                           ident[0:nr, 0:nr])
                        last.then_inc(s_ps, 1)
                    def alpha_parts():
                        pe.wait_ge(exp_ok, s * 3 + l + 1)
                        keep_warm(32)
                        pe.wait_ge(parts_ok, s * 2 + l)
                        for k in range(4):
                            atp = bA[k // 2][k % 2][:].bitcast(bf16)
                            for t in range(2):
                                for q in range(CJ):
                                    src = Pt[:, k * CJ + q, t, :, :].rearrange("p k n -> p (k n)")
                                    o = (t * CJ + q) * P
                                    last = nc.tensor.transpose(atp[0:AR, o:o + P], src, identb[:])
                            last.then_inc(at_ps, 1)
                        pe.wait_ge(at_act, s * 4 + 2 * l)
                        pe.wait_ge(at_dve, s * 4 + 2 * l)

                    def product_d(n):
                        c, gh = task(l, n)
                        k, cols = a0 + n, joints(c) * P
                        o = c * NCOL
                        if k > 0:
                            pe.wait_ge(d_sb, s * AGG + k)
                        if l == 1:
                            pe.wait_ge(dx_ok, s * NCH + c + 1)
                            mm(bD[:, 0:cols], W1[64 * gh:64 * gh + 64, :], DX[64 * gh:64 * gh + 64, c % 2, 0:cols],
                               start=True, stop=True).then_inc(d_ps, 1)
                        else:
                            mm(bD[0:64, 0:cols], W2[:], X2[:, 0, o:o + cols], start=True, stop=True)
                            mm(bD[64:128, 0:cols], W2[:], X2[:, 1, o:o + cols], start=True, stop=True)\
                                .then_inc(d_ps, 1)

                    def spread_alpha(n):
                        c, gh = task(l, n)
                        k, cols = a0 + n, joints(c) * P
                        if k >= 2:
                            pe.wait_ge(t_ok, s * AGG + k)
                        o = (c // JS) * NCOL
                        for sign in range(2):
                            b = bA[k % 2][sign]
                            if l == 1:
                                last = mm(b[:, 0:cols], sel1[:, c % JS, :], AT[:, sign, gh, o:o + cols], start=True, stop=True)
                            else:
                                for g in range(GH):
                                    last = mm(b[64 * g:64 * g + 64, 0:cols], sel2[:, c % JS, :],
                                              AT[:, sign, g, o:o + cols], start=True, stop=True)
                        last.then_inc(a_ps, 1)

                    def own(n):
                        c, gh = task(l, n)
                        k, cols = base + n, joints(c) * P
                        o = c * NCOL
                        z = bZ[k % 2]
                        if k >= 2:
                            pe.wait_ge(zs_ok, s * TASKS + k - 1)
                            pe.wait_ge(sq_ok, s * TASKS + k - 1)
                        if l == 0:
                            for j in range(joints(c)):
                                last = mm(z[:, j * P:j * P + P], W0bd[:, j, :], YT[:, c * P:c * P + P], start=True, stop=True)
                            last.then_inc(z_ps, 1)
                        elif l == 1:
                            mm(z[:, 0:cols], WR1[64 * gh:64 * gh + 64, :], X1[64 * gh:64 * gh + 64, o:o + cols],
                               start=True, stop=False)
                        else:
                            for g in range(GH):
                                mm(z[64 * g:64 * g + 64, 0:cols], WR2[:], X2[:, g, o:o + cols], start=True, stop=False,
                                   skip_group_check=True)

                    def plus_neighbours(n):
                        c, gh = task(l, n)
                        k, cols = base + n, joints(c) * P
                        pe.wait_ge(t_ok, s * AGG + k - NCH + 2)
                        mm(bZ[k % 2][:, 0:cols], (C1 if l == 1 else C2)[:], TA[:, (k - NCH) % 2, 0:cols],
                           start=False, stop=True, skip_group_check=(l == 2)).then_inc(z_ps, 1)

                    def variance(n):
                        c, gh = task(l, n)
                        k, cols = base + n, joints(c) * P
                        pe.wait_ge(sq_ok, s * TASKS + k + 1)
                        row = c if gh is None else gh * NCH + c
                        mm(bV[0:VR, 0:cols], (V1 if l == 1 else V2)[:, VR - 1 - row:2 * VR - 1 - row], SQ[:, k % 2, 0:cols],
                           start=(n == 0), stop=(n == NT[l] - 1), skip_group_check=True).then_inc(v_ps, 1)

                    def spread_rstd(n):
                        c, gh = task(l, n)
                        k, cols = base + n, joints(c) * P
                        if n >= 4:
                            pe.wait_ge(u_ok, s * TASKS + k - 3)
                        sel = selr2[:, c, :] if gh is None else selr1[:, gh * NCH + c, :]
                        mm(bA[n % 2][n // 2 % 2][:, 0:cols], sel, RP[:, 0:cols], start=True, stop=True)\
                            .then_inc(r_ps, 1)

                    def scores(n):
                        c, gh = task(l, n)
                        cols, o = joints(c) * P, c * NCOL
                        pe.wait_ge(x_ok, s * TASKS + base + n + 1)
                        if l == 0:
                            w = SR1 - 16 * (c % C1S + 1)
                            last = mm(bank[3 + c // C1S][0:SR1, 0:cols], A1[:, w:w + SR1], X1[:, o:o + cols],
                                      start=(c % C1S == 0), stop=(c in (C1S - 1, NCH - 1)), skip_group_check=True)
                        else:
                            w = SR - 8 * (c + 1)
                            last = mm(bank[3 + gh][0:SR, 0:cols], A2[:, w:w + SR], X2[:, gh, o:o + cols],
                                      start=(c == 0), stop=(c == NCH - 1), skip_group_check=True)
                        if n == NT[l] - 1:
                            last.then_inc(sr_ps, 1)

                    def projection(n):
                        pe.wait_ge(x_ok, s * TASKS + base + n + 1)
                        for j in range(CJ * n, CJ * n + joints(n)):
                            for gh in range(GH):
                                r = slice(64 * gh, 64 * gh + 64)
                                last = mm(bank[3 + gh][:, 0:P], X1[r, j * P:j * P + P], fpW[r, j * P:j * P + P],
                                          start=(j == 0), stop=(j == J - 1))
                        if n == NCH - 1:
                            last.then_inc(fp_ps, 1)

                    early = 2 if l and chain else 0
                    for n in range(early):
                        own(n)
                    if l == 2 and chain:
                        product_d(0)
                    if l and chain:
                        alpha_parts()
                    elif l:
                        neighbours_any(s, l)
                    for n in range(NT[l] + 2):
                        if l and n < NT[l] and chain:
                            spread_alpha(n)
                            if l == 1:
                                product_d(n)
                            elif n + 1 < NT[l]:
                                product_d(n + 1)
                        if 1 <= n <= NT[l]:
                            if n - 1 >= early:
                                own(n - 1)
                            if l:
                                plus_neighbours(n - 1)
                        if n >= 2:
                            variance(n - 2)
                    pe.wait_ge(vw_sb, s * 3 + l + 1)
                    keep_warm(1)
                    for q in range(CJ):
                        last = nc.tensor.transpose(bank[0][:, q * VR:q * VR + VR], VW[:, q * P:q * P + P], ident[0:VR, 0:VR])
                    last.then_inc(vt_ps, 1)
                    keep_warm(18)
                    pe.wait_ge(rg_ok, s * 3 + l + 1)
                    for q in range(CJ):
                        last = nc.tensor.transpose(bank[0][:].bitcast(bf16)[0:RR, q * P:q * P + P],
                                                   RG[:, q, :, :].rearrange("p k n -> p (k n)"), identb[:])
                    last.then_inc(rg_ps, 1)
                    keep_warm(4)
                    pe.wait_ge(rp_ok, s * 3 + l + 1)
                    for n in range(NT[l] + 3):
                        if n < NT[l]:
                            spread_rstd(n)
                        if n >= 3:
                            if n == 3:
                                keep_warm(5)
                            if l < 2:
                                scores(n - 3)
                            else:
                                projection(n - 3)
                keep_warm(26)
                pe.wait_ge(h_ok, s + 1)
                for t in range(4):
                    last = nc.tensor.transpose(bank[1][:, t * P:t * P + P], Xn[:, t, :], ident[:])
                last.then_inc(xt_ps, 1)
                keep_warm(2)
                pe.wait_ge(xt_sb, s * 2 + 1)
                mm(bank[2][:], wq1[:], XT[:], start=True, stop=True).then_inc(q1_ps, 1)
                keep_warm(4)
                pe.wait_ge(q1_sb, s + 1)
                mm(bank[3][:], wq2[:], Q1, start=True, stop=True).then_inc(q2_ps, 1)
                keep_warm(14)
                pe.wait_ge(cs_ok, s + 1)
                for t in range(4):
                    last = mm(bank[4][:, t:t + 1], QS[:, t * P:t * P + P], ones[:, 0:1], start=True, stop=True)
                last.then_inc(ss_ps, 1)
                keep_warm(8)
                pe.wait_ge(nr_ok, s + 1)
                for t in range(4):
                    last = mm(bank[5][:, t * P:t * P + P], rs[:, t:t + 1].to_broadcast([P, P]), ident, start=True, stop=True)
                last.then_inc(nb_ps, 1)
                keep_warm(3, bank[0])
                pe.wait_ge(kn_ok, s + 1)
                for m in range(2):
                    mm(bank[6 - m][:], mw1[:, m * P:m * P + P], KN, start=True, stop=True).then_inc(mh_ps, 1)
                keep_warm(4, bank[0])
                pe.wait_ge(mh_sb, s * 2 + 2)
                for m in range(2):
                    last = mm(bank[7][:], mw2[:, m * P:m * P + P], MH[:, m, :], start=(m == 0), stop=(m == 1))
                last.then_inc(rt_ps, 1)
                keep_warm(3, bank[0])
                pe.wait_ge(rt_sb, s + 1)
                for t in range(4):
                    last = mm(bank[0][:, t * P:t * P + P], RT[:, t * P:t * P + P], wout[:], start=True, stop=True)
                last.then_inc(o_ps, 1)
                keep_warm(14)
                pe.wait_ge(ho_ok, s + 2)
                for t in range(4):
                    last = nc.tensor.transpose(bank[1][:, t * P:t * P + P], Xn[:, t, :], ident[:])
                last.then_inc(xt_ps, 1)
                keep_warm(2)
                pe.wait_ge(xt_sb, s * 2 + 2)
                for t in range(4):
                    last = mm(bank[2][:, 8 * t:8 * t + 8], XT[:, t * P:t * P + P], rw[:], start=True, stop=True)
                last.then_inc(lg_ps, 1)

                def up(e):
                    for m in range(MT):
                        k = e * MT + m
                        if k >= 4:
                            pe.wait_ge(hid_sb, s * E * MT + k - 2)
                        mm(bank[4 + k % 4][:], w1[:, (e * MT + m) * P:(e * MT + m + 1) * P], XT[:], start=True, stop=True)\
                            .then_inc(hid_ps, 1)

                def down(e):
                    pe.wait_ge(hid_sb, s * E * MT + (e + 1) * MT + 1)
                    if e >= 2:
                        pe.wait_ge(acc_ok, s * E + e)
                    for t in range(4):
                        b = bank[e % 2][:, t * P:t * P + P]
                        for m in range(MT):
                            last = mm(b, HD[:, e % 2, m, t * P:t * P + P], w2[:, (e * MT + m) * P:(e * MT + m + 1) * P],
                               start=(m == 0), stop=(m == MT - 1))
                    last.then_inc(eo_ps, 1)

                up(0)
                for e in range(E):
                    if e + 1 < E:
                        up(e + 1)
                    if e == 0:
                        pe.wait_ge(gate_ok, s + 1)
                        for t in range(4):
                            last = nc.tensor.transpose(bank[3][0:E, t * P:t * P + P], gate[:, t, :], ident)
                        last.then_inc(gt_ps, 1)
                        pe.wait_ge(gt_sb, s + 1)
                        for t in range(4):
                            last = mm(bank[2][:, t * P:t * P + P], GT[0:E, t * P:t * P + P], b2, start=True, stop=True)
                        last.then_inc(bo_ps, 1)
                    down(e)

            pe.wait_ge(flag_ok, 1)
            graph = pe.value_load(flag[0:1, 0:1])
            with pe.If(graph == 0):
                with pe.Fori(0, STEPS) as s:
                    step(s, True)
            with pe.If(graph != 0):
                with pe.Fori(0, STEPS) as s:
                    step(s, False)

        @block.scalar
        def _(act):
            A_ = nc.scalar.activation
            act.wait_ge(setup_ps, 1)
            A_(W0bd[:].rearrange("p j f -> p (j f)"), bank[3][:], ACT.Copy)
            A_(sel1[:].rearrange("p j f -> p (j f)"), sel1f[:], ACT.Copy)
            A_(sel2[:].rearrange("p j f -> p (j f)"), sel2f[:], ACT.Copy)
            A_(selr1[:].rearrange("p j f -> p (j f)"), selr1f[:], ACT.Copy)
            A_(selr2[:].rearrange("p j f -> p (j f)"), selr2f[:], ACT.Copy)
            A_(identb[:], ident[:], ACT.Copy).then_inc(setup_sb, 1)
            def softmax_any(s, l):
                for again in range(2):
                    with act.Fori(0, J) as jp:
                        if l == 1 and again:
                            A_(XJ[:, 0, :], X1[:, bass.ds(jp * P, P)], ACT.Copy).then_inc(g_xj, 1)
                        if l == 2 and again:
                            A_(XJ, X2[:, :, bass.ds(jp * P, P)], ACT.Copy).then_inc(g_xj, 1)
                        act.wait_ge(ge_in, ((s * 3 + l) * 2 + again) * J + jp + 1)
                        A_(GW, GW, ACT.Exp).then_inc(ge_out, 1)
                        if l and again:
                            act.wait_ge(g_tp, (s * 2 + (l - 1)) * J + jp + 1)
                            for gh in range(GH):
                                A_(AT[:, 0, gh, :], bank[gh][0:AR, :].bitcast(bf16), ACT.Copy)
                            if l == 1:
                                A_(HG[:, 0, :], bank[6][:, 0:P], ACT.Copy)
                                A_(HG[:, 1, :], bank[7][:, 0:P], ACT.Copy).then_inc(g_at, 1)
                            else:
                                A_(HG[:, 0, :], bank[6][:, 0:P], ACT.Copy).then_inc(g_at, 1)

            def numerators(s, l, F):
                act.wait_ge(f_ok, s * 3 + l + 1)
                A_(F[:].rearrange("p k n -> p (k n)"), F[:].rearrange("p k n -> p (k n)"), ACT.Exp).then_inc(exp_ok, 1)

            def step(s, chain):
                for l in range(3):
                    base, a0 = T0[l], T0[l] - NCH
                    if l:
                        act.wait_ge(sr_ps, s * 2 + l)
                        SC = score_rows(l)
                        nr = SR1 if l == 1 else SR
                        A_(SC[:, 0, :], bank[3][0:nr, :], ACT.Copy)
                        A_(SC[:, 1, :], bank[4][0:nr, :], ACT.Copy).then_inc(sr_sb, 1)
                        act.wait_ge(s_ps, s * 2 + l)
                        for gh in range(GH):
                            if l == 2:
                                last = A_(S[:, gh, 1:JP + 1, :].rearrange("p (c q) r -> p q c r", q=CJ),
                                          bank[6 + gh][:, 0:CJ * SR].rearrange("p (q c r) -> p q c r", q=CJ, r=8), ACT.Copy)
                            else:
                                for b, chunks in ((0, C1S), (1, NCH - C1S)):
                                    j0 = 1 + CJ * C1S * b
                                    t = bank[6 + b][:, 0:CJ * SR1].rearrange("p (q c g r) -> p q c g r", q=CJ, c=C1S, g=GH)
                                    last = A_(S[:, gh, j0:j0 + CJ * chunks, :].rearrange("p (c q) r -> p q c r", q=CJ),
                                              t[:, :, 0:chunks, gh, :], ACT.Copy)
                        last.then_inc(s_sb, 1)
                    if l and not chain:
                        softmax_any(s, l)
                    if l and chain:
                        numerators(s, l, Fb)
                        for k in range(2):
                            act.wait_ge(at_ps, s * 8 + 4 * (l - 1) + k + 1)
                            A_(AT[:, 0, k, :], bA[0][k][0:AR, :].bitcast(bf16), ACT.Copy).then_inc(at_act, 1)
                    if l == 0:
                        for b in range(4):
                            act.wait_ge(yt_ps, s * 4 + b + 1)
                            n = min(4, NCH - 4 * b) * P
                            A_(YT[:, 4 * b * P:4 * b * P + n], bank[4 + b][:, 0:n], ACT.Copy).then_inc(yt_sb, 1)

                    def take_d(n):
                        c, gh = task(l, n)
                        k, cols = a0 + n, joints(c) * P
                        act.wait_ge(d_ps, s * AGG + k + 2)
                        if l == 1:
                            if n >= 2:
                                act.wait_ge(t_ok, s * AGG + k)
                            A_(DR[:, gh, c % 2, 0:cols], bD[:, 0:cols], ACT.Copy).then_inc(d_sb, 1)
                        else:
                            if n >= 3:
                                act.wait_ge(t_ok, s * AGG + k - 1)
                            A_(HS[c % 3][:, 0:cols], bD[:, 0:cols], ACT.Copy).then_inc(d_sb, 1)

                    def square(n):
                        c, gh = task(l, n)
                        k, cols = base + n, joints(c) * P
                        act.wait_ge(z_ps, s * TASKS + k + 1)
                        if k >= 2:
                            act.wait_ge(v_ps, s * TASKS + k - 1)
                        bias = bgc[:, l - 1:l] if l else 0.0
                        o = c * NCOL
                        dst = X2[:, gh, o:o + cols] if l == 1 else X1[:, o:o + cols]
                        A_(dst, bZ[k % 2][:, 0:cols], ACT.Identity, bias=bias).then_inc(zs_ok, 1)
                        A_(SQ[:, k % 2, 0:cols], bZ[k % 2][:, 0:cols], ACT.Square, bias=bias).then_inc(sq_ok, 1)

                    def gelu(n):
                        c, gh = task(l, n)
                        k, cols = base + n, joints(c) * P
                        o = c * NCOL
                        act.wait_ge(u_ok, s * TASKS + k + 1)
                        dst = X2[:, gh, o:o + cols] if l == 1 else X1[:, o:o + cols]
                        A_(dst, dst, ACT.Gelu, bias=v(f"b{l}"), scale=v(f"g{l}"))\
                            .then_inc(x_ok, 1)

                    if l == 2 and chain:
                        take_d(0)
                    for n in range(NT[l] + 1):
                        if l == 1 and n < NT[l] and chain:
                            take_d(n)
                        if l == 2 and n + 1 < NT[l] and chain:
                            take_d(n + 1)
                        if 1 <= n <= NT[l]:
                            square(n - 1)
                    act.wait_ge(v_ps, s * TASKS + base + NT[l])
                    A_(VW, bV[0:VR, :], ACT.Copy).then_inc(vw_sb, 1)
                    A_(carrier[:, 2:3], mhalf[:], ACT.Gelu)
                    act.wait_ge(rg_ps, s * 3 + l + 1)
                    A_(RP[:], bank[0][0:RR, 0:NCOL // 2].bitcast(bf16), ACT.Copy).then_inc(rp_ok, 1)
                    for n in range(NT[l]):
                        gelu(n)
                act.wait_ge(xt_ps, s * 2 + 1)
                A_(XT[:], bank[1][:], ACT.Copy).then_inc(xt_sb, 1)
                act.wait_ge(q1_ps, s + 1)
                A_(Q1, bank[2][:], ACT.Silu).then_inc(q1_sb, 1)
                act.wait_ge(q2_ps, s + 1)
                A_(QC[:, :, 3:], bank[3][:].rearrange("p (b t) -> p b t", b=GH), ACT.Copy).then_inc(q2_sb, 1)
                act.wait_ge(cv_ok, s + 1)
                A_(QD, QD, ACT.Silu, bias=v("cb")).then_inc(cs_self, 1)
                act.wait_ge(cs_self, s + 1)
                A_(QS, QD, ACT.Square).then_inc(cs_ok, 1)
                for m in range(2):
                    act.wait_ge(mh_ps, s * 2 + m + 1)
                    A_(MH[:, m, :], bank[6 - m][:], ACT.Silu).then_inc(mh_sb, 1)
                act.wait_ge(rt_ps, s + 1)
                A_(RT[:], bank[7][:], ACT.Copy).then_inc(rt_sb, 1)
                if chain:
                    numerators(s + 1, 0, F0b)
                act.wait_ge(xt_ps, s * 2 + 2)
                A_(XT[:], bank[1][:], ACT.Copy).then_inc(xt_sb, 1)
                act.wait_ge(lgm_ok, s + 1)
                A_(LG[:].rearrange("p t e -> p (t e)"), LG[:].rearrange("p t e -> p (t e)"), ACT.Exp)\
                    .then_inc(rexp_ok, 1)
                for k in range(E * MT):
                    e, m = k // MT, k % MT
                    if k == 2 * MT:
                        act.wait_ge(gt_ps, s + 1)
                        A_(GT[0:E, :], bank[3][0:E, :], ACT.Copy).then_inc(gt_sb, 1)
                    act.wait_ge(hid_ps, s * E * MT + k + 1)
                    if e >= 2 and m == 0:
                        act.wait_ge(eo_ps, s * E + e)
                    A_(HD[:, e % 2, m, :], bank[4 + k % 4][:], ACT.Gelu,
                       bias=vec[:, FB1 + k:FB1 + k + 1]).then_inc(hid_sb, 1)
                act.wait_ge(acc_ok, s * E + E + 1)
                for gh in range(GH):
                    act.dma_start(out[s, gh].rearrange("h p d -> p h d"), Ho[:, 2 * gh:2 * gh + 2, :])\
                        .then_inc(stored, 16)
                if not chain:
                    softmax_any(s + 1, 0)

            act.wait_ge(flag_ok, 1)
            graph = act.value_load(flag[0:1, 0:1])
            with act.If(graph == 0):
                numerators(0, 0, F0b)
                with act.Fori(0, STEPS) as s:
                    step(s, True)
            with act.If(graph != 0):
                softmax_any(0, 0)
                with act.Fori(0, STEPS) as s:
                    step(s, False)
            act.wait_ge(stored, STEPS * 32 + 1)

        @block.vector
        def _(dve):
            TT, TS, STT = nc.vector.tensor_tensor, nc.vector.tensor_scalar, nc.vector.scalar_tensor_tensor
            LINKS_ANY = 133
            LINKS_FIRST, LINKS_FIRST_ANY = 25, 9
            LINKS = 225
            links = [0]
            dve.wait_ge(setup_ps, 1)
            nc.vector.tensor_copy(A0b[:].rearrange("p d r -> p (d r)"), bank[0][:, 0:24])
            dve.wait_ge(seeded, 1)
            for gh in range(GH):
                r = slice(64 * gh, 64 * gh + 64)
                nc.vector.tensor_copy(A1[r, SR1 - 16 + 8 * gh:SR1 - 8 + 8 * gh], bank[0][r, 32:40])
            nc.vector.tensor_copy(A2[:, SR - 8:SR], bank[0][:, 40:48])
            nc.vector.tensor_copy(bgc[:], bank[0][:, 48:50])
            nc.vector.tensor_copy(WR1[:], bank[1][:, 0:F1])
            nc.vector.tensor_copy(WR2[:], bank[2][:, 0:F2]).then_inc(setup_sb, 1)
            nc.vector.tensor_copy(EN, edges).then_inc(en_ok, 1)
            dve.wait_ge(en_ok, 1)
            for t in range(2):
                TS(HOT_S[:, t, :], iota[0:EH, 0:J], EN[:, t:t + 1], None, ALU.is_equal)
                last = TS(HOT_D[:, t, :], iota[0:EH, :], EN[:, 2 + t:3 + t], None, ALU.is_equal)
            last.then_inc(hot_ok, 1)
            dve.wait_ge(cn_ps, 1)
            for b in range((J + 8) // 9):
                n = min(9, J - 9 * b)
                last = nc.vector.tensor_copy(CN[:, 9 * b:9 * b + n, :].rearrange("p j i -> p (j i)"), bank[b][:, 0:n * JP])
            last.then_inc(en_ok, 1)
            dve.wait_ge(en_ok, 2)
            cf = CN.rearrange("p j i -> p (j i)")
            TT(chain_counts, chain_counts, cf, ALU.not_equal).then_inc(en_ok, 1)
            dve.wait_ge(en_ok, 3)
            nc.vector.tensor_reduce(other[:], chain_counts, mybir.AxisListType.X, ALU.max).then_inc(en_ok, 1)
            dve.wait_ge(en_ok, 4)
            nc.vector.tensor_copy(flag[:], other[:]).then_inc(flag_ok, 1)
            dve.wait_ge(setup_sb, 2)
            def step(s, chain, warm_up=False):
                per_step, first = (LINKS, LINKS_FIRST) if chain else (LINKS_ANY, LINKS_FIRST_ANY)
                links[0] = 0 if warm_up else first

                def link(ins):
                    links[0] += 1
                    ins.then_inc(dve_link, 1)
                    dve.wait_ge(dve_link, s * per_step + links[0])

                def write_y(gh, heads12):
                    for c0, c1 in ((0, NCH - 1), (NCH - 1, NCH)):
                        a, b = CJ * c0, min(CJ * c1, J)
                        w4 = (b - a) // (c1 - c0)
                        for r0, src in ((0, heads12[:, a:b, :]), (12, X0[:, gh, a:b, :])):
                            n = src.shape[2]
                            last = nc.vector.tensor_copy(Y[:, c0:c1, gh, 0:w4, r0:r0 + n],
                                                         src.rearrange("p (c j) r -> p c j r", j=w4))
                    return last

                def sets(fn, rows16, *tensors):
                    for t, (m0, m1) in enumerate(((0, JS), (JS, NCH))):
                        last = fn(lambda k: Pt[:, 0:rows16, t, k, 0:(m1 - m0) * 4],
                                  *(x.rearrange("p (q n) -> p q n", n=NCH * 4)[:, :, m0 * 4:m1 * 4] for x in tensors))
                    return last

                def edges_chain(l, S):
                    Eb = edge_scores(l)
                    for k, (a, b) in enumerate(((1, 1), (2, 1), (0, 1))):
                        for gh in range(GH):
                            es, ed = S[:, gh, a:a + JP, 0:4], S[:, gh, b:b + JP, 4:8]
                            eo = Eb[:, k, gh, :]
                            if l == 0:
                                last = TT(eo.rearrange("p (j h) -> p j h", h=4), es, ed, ALU.add)
                            else:
                                last = TT(eo.rearrange("p (q m h) -> p q m h", q=CJ, h=4),
                                          es.rearrange("p (m q) h -> p q m h", q=CJ),
                                          ed.rearrange("p (m q) h -> p q m h", q=CJ), ALU.add)
                    link(last)
                    end = (J - 1) * 4 if l == 0 else ((J - 1) % CJ * NCH + (J - 1) // CJ) * 4
                    nc.vector.memset(Eb[:, 1, :, end:end + 4], NEG)
                    link(nc.vector.memset(Eb[:, 2, :, 0:4], NEG))

                def exponents_chain(l, Fb, Mx):
                    ef = edge_scores(l).rearrange("p k a n -> p (k a n)")
                    ff = Fb[:].rearrange("p k n -> p (k n)")
                    link(STT(ff, ef, 0.2, ef, ALU.mult, ALU.max))
                    link(TT(Mx[:], Fb[:, 0, :], Fb[:, 1, :], ALU.max))
                    link(TT(Mx[:], Mx[:], Fb[:, 2, :], ALU.max))
                    TT(Fb[:], Fb[:], Mx[:].unsqueeze(1).to_broadcast([P, 3, N4]), ALU.subtract).then_inc(f_ok, 1)

                def alphas_chain(t, l, Fb, Mx, Al):
                    dve.wait_ge(exp_ok, t * 3 + l + 1)
                    link(TT(Mx[:], Fb[:, 0, :], Fb[:, 1, :], ALU.add))
                    link(TT(Mx[:], Mx[:], Fb[:, 2, :], ALU.add))
                    link(nc.vector.reciprocal(Mx[:], Mx[:]))
                    link(TT(Al[:], Fb[:, 1:3, :], Mx[:].unsqueeze(1).to_broadcast([P, 2, N4]), ALU.mult))

                def attend_chain(l):
                    edges_chain(l, S)
                    exponents_chain(l, Fb, Mx)
                    alphas_chain(s, l, Fb, Mx, Al)
                    alf, ref = Al.rearrange("p s n -> p (s n)"), Res.rearrange("p s n -> p (s n)")
                    link(sets(lambda part, al, re: nc.vector.tensor_copy(part(0), al), 16, alf, ref))
                    link(sets(lambda part, al, re: TT(re, al, part(0), ALU.subtract), 16, alf, ref))
                    link(sets(lambda part, al, re: nc.vector.tensor_copy(part(1), re), 16, alf, ref))
                    sets(lambda part, al, re: TT(part(2), re, part(1), ALU.subtract), 16, alf, ref).then_inc(parts_ok, 1)
                    for k in range(2):
                        dve.wait_ge(at_ps, s * 8 + 4 * (l - 1) + k + 3)
                        nc.vector.tensor_copy(AT[:, 1, k, :], bA[1][k][0:AR, :].bitcast(bf16))\
                            .then_inc(at_dve, 1)

                def scores_0(gh):
                    sg, s2 = S0[:, gh, 1:J + 1, :], S2[:, gh, 1:J + 1, :]
                    for d in range(DIN):
                        xd = X0[:, gh, :, d:d + 1].to_broadcast([P, J, 8])
                        ad = A0b[:, d:d + 1, :].to_broadcast([P, J, 8])
                        if d == 0:
                            TT(sg, xd, ad, ALU.mult)
                        else:
                            link(TT(s2, xd, ad, ALU.mult))
                            link(TT(sg, sg, s2, ALU.add))

                def pad_scores(S):
                    nc.vector.memset(S[:, :, 0, :], 0.0)
                    link(nc.vector.memset(S[:, :, J + 1:, :], 0.0))

                def coordinates_0(gh):
                    def al(k):
                        o = gh * JP * HEADS
                        return Al0[:, k, o:o + J * HEADS].rearrange("p (j h) -> p j h", h=4)\
                            .unsqueeze(3).to_broadcast([P, J, HEADS, DIN])

                    def heads(a):
                        return a.unsqueeze(2).to_broadcast([P, J, HEADS, DIN])

                    def t4(t):
                        return t[:].rearrange("p j (h d) -> p j h d", h=HEADS)

                    TT(t4(Tc), al(0), heads(dX0[:, gh, 1:J + 1, :]), ALU.mult)
                    link(TT(t4(Td), al(1), heads(dX0[:, gh, 0:J, :]), ALU.mult))
                    link(TT(Tc[:], Tc[:], Td[:], ALU.subtract))
                    link(TT(t4(Tc), t4(Tc), heads(X0[:, gh, :, :]), ALU.add))
                    return write_y(gh, Tc)

                def attend_0(t, part):
                    if part == 0:
                        dve.wait_ge(x0_in, t * 32 + 32)
                        scores_0(0)
                    elif part == 1:
                        scores_0(1)
                        nc.vector.tensor_tensor(dX0[:, :, 1:J, :].rearrange("p a j d -> p a (j d)"),
                                                X0[:, :, 1:J, :].rearrange("p a j d -> p a (j d)"),
                                                X0[:, :, 0:J - 1, :].rearrange("p a j d -> p a (j d)"), ALU.subtract)
                        pad_scores(S0)
                    elif not chain:
                        if part == 2:
                            attend_any(t, 0)
                    elif part == 2:
                        edges_chain(0, S0)
                    elif part == 3:
                        exponents_chain(0, F0b, M0)
                    elif part == 4:
                        alphas_chain(t, 0, F0b, M0, Al0)
                    elif part == 5:
                        dve.wait_ge(y_pad, t + 1)
                        link(coordinates_0(0))
                    else:
                        coordinates_0(1).then_inc(y_ok, 1)

                def attend_any(s, l):
                    Sl = S if l else S0
                    def per_gh(x, gh):
                        x = x[:, gh * JP * HEADS:(gh + 1) * JP * HEADS]
                        if l == 0:
                            return x.rearrange("p (j h) -> p j h", h=4)
                        return x.rearrange("p (q m h) -> p q m h", q=CJ, h=4)

                    def order(x):
                        if l == 0:
                            return x
                        return x.rearrange("p (m q) h -> p q m h", q=CJ)

                    def every_joint(x):
                        if l == 0:
                            return x.unsqueeze(1).to_broadcast([P, JP, 4])
                        return x.unsqueeze(1).unsqueeze(1).to_broadcast([P, CJ, NCH, 4])

                    def counts(jp):
                        return order(CN[:, jp, :].unsqueeze(2).to_broadcast([P, JP, 4]))

                    def scores(jp):
                        for gh in range(GH):
                            TT(per_gh(GW, gh), every_joint(Sl[:, gh, jp + 1, 0:4]), order(Sl[:, gh, 1:JP + 1, 4:8]), ALU.add)
                        TS(GK, CN[:, jp, :], 0.0, NEG, ALU.is_equal, ALU.mult)
                        dve.drain()
                        STT(GW, GW, 0.2, GW, ALU.mult, ALU.max)
                        dve.drain()
                        for gh in range(GH):
                            TT(per_gh(GW, gh), per_gh(GW, gh), order(GK.unsqueeze(2).to_broadcast([P, JP, 4])), ALU.add)
                        dve.drain()

                    def numerators(jp, again):
                        scores(jp)
                        TT(GW, GW, GM, ALU.subtract).then_inc(ge_in, 1)
                        dve.wait_ge(ge_out, ((s * 3 + l) * 2 + again) * J + jp + 1)
                        for gh in range(GH):
                            TT(per_gh(GW, gh), per_gh(GW, gh), counts(jp), ALU.mult)
                        dve.drain()

                    nc.vector.memset(GM, NEG)
                    nc.vector.memset(GD, 0.0)
                    dve.drain()
                    with dve.Fori(0, J) as jp:
                        scores(jp)
                        TT(GM, GM, GW, ALU.max)
                        dve.drain()
                    with dve.Fori(0, J) as jp:
                        numerators(jp, 0)
                        TT(GD, GD, GW, ALU.add)
                        dve.drain()
                    TS(GD, GD, 0.5, None, ALU.max)
                    dve.drain()
                    nc.vector.reciprocal(GD, GD)
                    dve.drain()
                    if l == 0:
                        nc.vector.memset(GY.rearrange("p g j r -> p (g j r)"), 0.0)
                        dve.drain()
                        with dve.Fori(0, J) as jp:
                            numerators(jp, 1)
                            TT(GW, GW, GD, ALU.mult)
                            dve.drain()
                            for gh in range(GH):
                                wj = GW[:, gh * JP * HEADS:gh * JP * HEADS + J * HEADS].rearrange("p (j h) -> p j h", h=4)
                                xj = X0[:, gh, jp, :].unsqueeze(1).unsqueeze(1).to_broadcast([P, J, HEADS, DIN])
                                TT(GT4, wj.unsqueeze(3).to_broadcast([P, J, HEADS, DIN]), xj, ALU.mult)
                                dve.drain()
                                TT(GY[:, gh, :, :], GY[:, gh, :, :], GT4.rearrange("p j h d -> p j (h d)"), ALU.add)
                                dve.drain()
                        dve.wait_ge(y_pad, s + 1)
                        for gh in range(GH):
                            last = write_y(gh, GY[:, gh, :, :])
                        last.then_inc(y_ok, 1)
                        return
                    nt = NT[l]
                    ng = (nt + 3) // 4

                    def group(jp1, g, fn):
                        gi = s * GROUPS + (0 if l == 1 else GROUPS1) + jp1 * ng + g
                        dve.wait_ge(g_mm, gi + 1)
                        for n in range(4 * g, min(4 * g + 4, nt)):
                            c, gh = task(l, n)
                            cols, o = joints(c) * P, c * NCOL
                            dst = X2[:, gh, o:o + cols] if l == 1 else X1[:, o:o + cols]
                            last = fn(dst, bank[2 + n % 4][:, 0:cols], gh or 0, joints(c))
                        last.then_inc(g_use, 1)

                    for g in range(ng):
                        group(0, g, lambda dst, src, gh, k: TS(dst, src, -1.0, None, ALU.mult))

                    def add_source(dst, src, gh, k):
                        h = HG[:, gh, :].unsqueeze(1).to_broadcast([P, k, P])
                        TT(TB[:, 0:k * P].rearrange("p (j g) -> p j g", j=k), src.rearrange("p (j g) -> p j g", j=k), h, ALU.mult)
                        dve.drain()
                        last = TT(dst, dst, TB[:, 0:k * P], ALU.add)
                        dve.drain()
                        return last

                    with dve.Fori(0, J) as jp:
                        numerators(jp, 1)
                        TT(GW, GW, GD, ALU.mult)
                        dve.drain()
                        sets(lambda part, al, re: nc.vector.tensor_copy(part(0), al), 8, GW, GR)
                        dve.drain()
                        sets(lambda part, al, re: TT(re, al, part(0), ALU.subtract), 8, GW, GR)
                        dve.drain()
                        sets(lambda part, al, re: nc.vector.tensor_copy(part(1), re), 8, GW, GR)
                        dve.drain()
                        sets(lambda part, al, re: TT(part(2), re, part(1), ALU.subtract), 8, GW, GR).then_inc(g_parts, 1)
                        dve.wait_ge(g_at, (s * 2 + (l - 1)) * J + jp + 1)
                        for g in range(ng):
                            group(jp + 1, g, add_source)

                def newton(y, v, t, done=None):
                    link(STT(t, y, -0.5, v, ALU.mult, ALU.mult))
                    link(TT(t, t, y, ALU.mult))
                    ins = STT(y, t, 1.5, y, ALU.add, ALU.mult)
                    if done is None:
                        link(ins)
                    else:
                        ins.then_inc(done, 1)

                def rsqrt(y, v, t, done=None):
                    link(TS(t.bitcast(i32), v.bitcast(i32), 1, None, ALU.logical_shift_right))
                    link(TS(y.bitcast(i32), t.bitcast(i32), -1.0, float(0x5f3759df), ALU.mult, ALU.add))
                    for k in range(3):
                        newton(y, v, t, done if k == 2 else None)

                if warm_up:
                    for part in range(7):
                        attend_0(s, part)
                    assert links[0] == first, links[0]
                    return
                for l in range(3):
                    base, a0 = T0[l], T0[l] - NCH
                    if l:
                        dve.wait_ge(s_sb, s * 2 + l)
                        pad_scores(S)
                        if chain:
                            attend_chain(l)
                        else:
                            attend_any(s, l)

                    def neighbours(n):
                        c, gh = task(l, n)
                        k, cols = a0 + n, joints(c) * P
                        slot = gh or 0
                        if not chain:
                            if k >= 2:
                                dve.wait_ge(z_ps, s * TASKS + NCH + k - 1)
                            o = c * NCOL
                            dst = X2[:, gh, o:o + cols] if l == 1 else X1[:, o:o + cols]
                            nc.vector.tensor_copy(TA[:, k % 2, 0:cols], dst).then_inc(t_ok, 1)
                            return
                        if l == 2:
                            dve.wait_ge(t_ok, s * AGG + k + 1)
                            dve.wait_ge(d_sb, s * AGG + a0 + min(n + 2, NCH))
                            d, h = DR[:, 0, c % 2, :], HS[c % 3]
                            if c + 1 < NCH:
                                TT(d[:, cols - P:cols], HS[(c + 1) % 3][:, 0:P], h[:, cols - P:cols], ALU.subtract)
                            else:
                                nc.vector.memset(d[:, cols - P:cols], 0.0)
                            link(TT(d[:, 0:cols - P], h[:, P:cols], h[:, 0:cols - P], ALU.subtract))
                        else:
                            dve.wait_ge(d_sb, s * AGG + k + 1)
                        dve.wait_ge(a_ps, s * AGG + k + 1)
                        if k >= 2:
                            dve.wait_ge(z_ps, s * TASKS + NCH + k - 1)
                        dve.wait_ge(t_ok, s * AGG + k + 1)
                        ap, am = bA[k % 2]
                        ta = TA[:, k % 2, :]
                        TT(ta[:, 0:cols], ap[:, 0:cols], DR[:, slot, c % 2, 0:cols], ALU.mult)
                        if c == 0:
                            nc.vector.memset(TB[:, 0:P], 0.0)
                        else:
                            TT(TB[:, 0:P], am[:, 0:P], DR[:, slot, (c - 1) % 2, NCOL - P:NCOL], ALU.mult)
                        link(TT(TB[:, P:cols], am[:, P:cols], DR[:, slot, c % 2, 0:cols - P], ALU.mult))
                        TT(ta[:, 0:cols], ta[:, 0:cols], TB[:, 0:cols], ALU.subtract).then_inc(t_ok, 1)

                    def normalise(n):
                        c, gh = task(l, n)
                        k, cols = base + n, joints(c) * P
                        o = c * NCOL
                        dve.wait_ge(r_ps, s * TASKS + k + 1)
                        dst = X2[:, gh, o:o + cols] if l == 1 else X1[:, o:o + cols]
                        TT(dst, dst, bA[n % 2][n // 2 % 2][:, 0:cols], ALU.mult).then_inc(u_ok, 1)

                    if l:
                        for n in range(NT[l]):
                            neighbours(n)
                    dve.wait_ge(vt_ps, s * 3 + l + 1)
                    link(TS(VB, bank[0][:, 0:NVR], EPS, None, ALU.add))
                    rsqrt(RV, VB, RN)
                    vp, rp = (x.rearrange("p (q n) -> p q n", q=CJ) for x in (VB, RV))
                    link(nc.vector.tensor_copy(RG[:, :, 0, :], rp))
                    link(TT(vp, rp, RG[:, :, 0, :], ALU.subtract))
                    link(nc.vector.tensor_copy(RG[:, :, 1, :], vp))
                    TT(RG[:, :, 2, :], vp, RG[:, :, 1, :], ALU.subtract).then_inc(rg_ok, 1)
                    dve.wait_ge(zs_ok, s * TASKS + base + NT[l])
                    for n in range(NT[l]):
                        normalise(n)

                def stats(srcs):
                    n = len(srcs)
                    for t, src in enumerate(srcs):
                        last = nc.vector.bn_stats(st[:, t, :], src)
                    link(last)
                    nc.vector.memset(carrier[:, 1:2], 0.0)
                    for t in range(n):
                        last = nc.vector.bn_aggr(mv[:, t, :], st[:, t, :])
                    link(last)
                    link(TS(rv[:, 0:n], mv[:, 0:n, 1], EPS, None, ALU.add))
                    rsqrt(rs[:, 0:n], rv[:, 0:n], rt[:, 0:n])

                dve.wait_ge(fp_ps, s + 1)
                pose = Hf[:].rearrange("p (g h) d -> p g h d", g=GH)[:, :, 0, :]

                def row(k):
                    return rows[:, k * P:k * P + P].unsqueeze(1).to_broadcast([P, GH, P])

                for gh in range(GH):
                    last = TT(Hf[:, 2 * gh, :], bank[3 + gh][:, 0:P], rows[:, 0:P], ALU.add)
                link(last)
                stats([Hf[:, 0, :], Hf[:, 2, :]])
                for gh in range(GH):
                    h = Hf[:, 2 * gh, :]
                    last = TS(h, h, mv[:, gh, 0:1], rs[:, gh:gh + 1], ALU.subtract, ALU.mult)
                link(last)
                link(TT(pose, pose, row(1), ALU.mult))
                link(TT(pose, pose, row(2), ALU.add))
                dve.wait_ge(txt_in, s * 32 + 32)
                stats([Hf[:, t, :] for t in range(4)])
                for t in range(4):
                    last = TS(Xn[:, t, :], Hf[:, t, :], mv[:, t, 0:1], rs[:, t:t + 1], ALU.subtract, ALU.mult)
                last.then_inc(h_ok, 1)
                if chain:
                    attend_0(s + 1, 0)
                    attend_0(s + 1, 1)
                dve.wait_ge(q2_sb, s + 1)
                qd = QD.rearrange("p (b t) -> p b t", b=GH)
                link(TS(qd, QC[:, :, 3:3 + 2 * P], v("cw3"), None, ALU.mult))
                for k in range(3):
                    ins = STT(qd, QC[:, :, k:k + 2 * P], v(f"cw{k}"), qd, ALU.mult, ALU.add)
                    if k < 2:
                        link(ins)
                ins.then_inc(cv_ok, 1)
                dve.wait_ge(ss_ps, s + 1)
                link(TS(rv[:], bank[4][:, 0:4], 1e-24, None, ALU.max))
                rsqrt(rs[:], rv[:], rt[:], nr_ok)
                dve.wait_ge(nb_ps, s + 1)
                TT(KN, QD, bank[5][:], ALU.mult).then_inc(kn_ok, 1)
                if chain:
                    attend_0(s + 1, 2)
                    attend_0(s + 1, 3)
                dve.wait_ge(o_ps, s + 1)
                dve.wait_ge(stored, s * 32 + 1)
                hof, hff = Ho[:].rearrange("p t d -> p (t d)"), Hf[:].rearrange("p t d -> p (t d)")
                link(TT(hof, bank[0][:], hff, ALU.add))
                stats([Ho[:, t, :] for t in range(4)])
                for t in range(4):
                    last = TS(Xn[:, t, :], Ho[:, t, :], mv[:, t, 0:1], rs[:, t:t + 1], ALU.subtract, ALU.mult)
                last.then_inc(ho_ok, 1)
                dve.wait_ge(lg_ps, s + 1)
                lg3 = bank[2][:, 0:32].rearrange("p (t e) -> p t e", t=4)
                link(nc.vector.tensor_reduce(mx4[:], lg3, mybir.AxisListType.X, ALU.max))
                m3 = mx4[:].unsqueeze(2).to_broadcast([P, 4, 8])
                TT(LG[:], lg3, m3, ALU.subtract).then_inc(lgm_ok, 1)
                dve.wait_ge(rexp_ok, s + 1)
                link(nc.vector.tensor_reduce(den4[:], LG[:], mybir.AxisListType.X, ALU.add))
                link(nc.vector.reciprocal(den4[:], den4[:]))
                link(TT(PB[:], LG[:], den4[:].unsqueeze(2).to_broadcast([P, 4, 8]), ALU.mult))
                nc.vector.memset(carrier[:, 1:2], 0.0)
                for t in range(4):
                    last = nc.vector.max(top[:, t, :], PB[:, t, :])
                link(last)
                nc.vector.memset(carrier[:, 1:2], 0.0)
                for t in range(4):
                    last = nc.vector.max_index(tix[:, t, :], top[:, t, :], PB[:, t, :])
                link(last)
                link(nc.vector.tensor_copy(tif[:], tix[:]))
                link(TT(mx4[:], top[:, :, 0], top[:, :, 1], ALU.add))
                link(TS(mx4[:], mx4[:], 1e-9, None, ALU.add))
                link(nc.vector.reciprocal(mx4[:], mx4[:]))
                link(TT(gw[:], top[:, :, 0:2], mx4[:].unsqueeze(2).to_broadcast([P, 4, 2]), ALU.mult))
                i3 = iota8[:].rearrange("p (t e) -> p t e", t=4)
                for k in range(2):
                    g = gate if k == 0 else gtmp
                    link(TT(g[:], i3, tif[:, :, k:k + 1].to_broadcast([P, 4, 8]), ALU.is_equal))
                    link(TT(g[:], g[:], gw[:, :, k:k + 1].to_broadcast([P, 4, 8]), ALU.mult))
                TT(gate[:], gate[:], gtmp[:], ALU.add).then_inc(gate_ok, 1)
                dve.wait_ge(gate_ok, s + 1)
                dve.wait_ge(bo_ps, s + 1)
                link(TT(hof, bank[2][:], hof, ALU.add))
                for e in range(E):
                    dve.wait_ge(eo_ps, s * E + e + 2)
                    if e:
                        dve.wait_ge(acc_ok, s * E + e + 1)
                    for t in range(4):
                        last = STT(Ho[:, t, :], bank[e % 2][:, t * P:t * P + P], gate[:, t, e:e + 1], Ho[:, t, :],
                                   ALU.mult, ALU.add)
                    last.then_inc(acc_ok, 1)
                    if chain and e < 3:
                        attend_0(s + 1, 4 + e)
                if not chain:
                    for part in range(7):
                        attend_0(s + 1, part)
                assert links[0] == per_step + first, links[0]


            dve.wait_ge(flag_ok, 1)
            graph = dve.value_load(flag[0:1, 0:1])
            with dve.If(graph == 0):
                step(0, True, warm_up=True)
                with dve.Fori(0, STEPS) as s:
                    step(s, True)
            with dve.If(graph != 0):
                step(0, False, warm_up=True)
                with dve.Fori(0, STEPS) as s:
                    step(s, False)

def _layout(i):
    f = np.float32
    a = {k: np.asarray(x) for k, x in i.items()}
    t = {k[7:]: x for k, x in a.items() if k.startswith("L0_tok_")}
    m = {k[8:]: x for k, x in a.items() if k.startswith("L0_attn_")}
    n = {k[7:]: x for k, x in a.items() if k.startswith("L0_ffn_")}
    o = {}
    x = a["x"].reshape(STEPS, GH, P, J, DIN)
    o["x"] = np.concatenate([x, x[0:1]])
    o["txt"] = a["txt"].reshape(STEPS, GH, P, P)

    def blocks(s, d):
        h, c = s.shape
        r = np.zeros((h, c, 2, h), f)
        for k in range(h):
            r[k, :, 0, k] = s[k]
            r[k, :, 1, k] = d[k]
        return r.reshape(h * c, 2 * h)

    def twice(x, axis=0):
        return np.concatenate([x, x], axis)

    for l in range(3):
        o[f"abd{l}"] = blocks(t[f"as{l}"], t[f"ad{l}"])
    o["W0T"] = t["W0"].T
    rows0 = np.zeros((16, HEADS, F0 // HEADS), f)
    for h in range(HEADS):
        rows0[3 * h:3 * h + 3, h] = t["W0"].reshape(DIN, HEADS, -1)[:, h]
    rows0[12:15] = t["R0"].reshape(DIN, HEADS, -1)
    rows0[15] = t["bg0"].reshape(HEADS, -1)
    raw = np.zeros((F0, CJ, GH, GH, CJ, 16), f)
    for j in range(CJ):
        for g in range(GH):
            raw[:, j, g, g, j, :] = rows0.reshape(16, F0).T
    o["raw0"] = raw.reshape(F0, CJ * GH * P)
    o["edges"] = t["edge_index"].reshape(2, 2, J_EDGES // 2).transpose(2, 0, 1).reshape(J_EDGES // 2, 4)
    o["iota"] = np.broadcast_to(np.arange(JP, dtype=f)[None], (P, JP))
    apart = np.arange(J)[:, None] - np.arange(JP)[None]
    chain = ((abs(apart) <= 1) & (np.arange(JP) < J)[None]).astype(f)
    o["chain"] = np.broadcast_to(chain.reshape(1, J * JP), (P, J * JP))
    o["W1T"], o["R1T"], o["W1"] = twice(t["W1"].T, 1), twice(t["R1"].T, 1), twice(t["W1"])
    o["W2T"], o["R2T"], o["W2"] = t["W2"].T, t["R2"].T, t["W2"]

    def centre(k):
        return np.eye(k, dtype=f) - f(1.0 / k)

    def twin(x):
        z = np.zeros_like(x)
        return np.block([[x, z], [z, x]])

    o["C1"], o["C2"] = centre(F1), twin(centre(F2))
    v1, v2 = np.zeros((P, 2 * VR - 1), f), np.zeros((P, 2 * VR - 1), f)
    v1[:, VR - 1] = 1.0 / F1
    v2[:F2, VR - 1] = 1.0 / F2
    v2[F2:, VR - 1 + NCH] = 1.0 / F2
    o["V1"], o["V2"] = v1, v2
    r1, r2 = np.zeros((RR, GH * NCH, P), f), np.zeros((RR, NCH, P), f)
    for part in range(3):
        for c in range(NCH):
            for g in range(GH):
                r1[VR * part + g * NCH + c, g * NCH + c] = 1.0
                r2[VR * part + g * NCH + c, c, F2 * g:F2 * g + F2] = 1.0
    o["selr1"], o["selr2"] = r1.reshape(RR, -1), r2.reshape(RR, -1)
    o["ones"], o["ident"] = np.ones((P, P), f), np.eye(P, dtype=f)
    for name, width in (("sel1", F1), ("sel2", F2)):
        s = np.zeros((3, JS, HEADS, JS, HEADS, width // HEADS), f)
        for j in range(JS):
            for h in range(HEADS):
                s[:, j, h, j, h, :] = 1.0
        o[name] = s.reshape(AR, JS * width)
    cols = [t["bg1"], twice(t["bg2"]), twice(t["g0"]), twice(t["b0"]), t["g1"], t["b1"], twice(t["g2"]), twice(t["b2"]),
            m["conv_q_b"]] + [m["conv_q_w"][:, 0, k] for k in range(4)]
    o["vec"] = np.concatenate([np.stack(cols, 1), n["b1"].reshape(E * MT, P).T], 1)
    o["rows"] = np.broadcast_to(np.concatenate([t["fpb"], t["fng"], t["fnb"]])[None], (P, 3 * P))
    o["fpW"] = twice(t["fpW"].reshape(J, F2, P).transpose(1, 0, 2).reshape(F2, J * P))
    o["wq1"], o["wq2"], o["wout"] = m["w_q1"].T, m["w_q2"].T, m["w_out"].T
    o["mw1"] = m["mem_w1"].T
    o["mw2"] = m["mem_w2"].T.reshape(2, P, P).transpose(1, 0, 2).reshape(P, 2 * P)
    o["rw"] = n["router_w"].T
    o["w1"] = n["w1"].transpose(2, 0, 1).reshape(P, E * FF)
    o["w2"] = n["w2"].transpose(2, 0, 1).reshape(MT, P, E, P).transpose(1, 2, 0, 3).reshape(P, E * FF)
    o["b2"] = n["b2"]
    o["iota8"] = np.broadcast_to(np.tile(np.arange(8, dtype=f), 4)[None], (P, 32))
    return {k: np.ascontiguousarray(x) for k, x in o.items()}


def kernel(**inputs):
    import concourse.bacc as _bacc
    from concourse.bass_utils import run_bass_kernel_spmd as _run

    laid = _layout(inputs)
    nc = _bacc.Bacc("TRN2", target_bir_lowering=False, num_devices=1)
    arrays, aps = {}, {}
    for name, a in laid.items():
        arrays[f"in_{name}"] = a
        aps[name] = nc.dram_tensor(f"in_{name}", a.shape, mybir.dt.from_np(a.dtype), kind="ExternalInput").ap()
    out = nc.dram_tensor("out_0", (STEPS, GH, 2, P, P), mybir.dt.float32, kind="ExternalOutput").ap()
    build(nc, aps, out)
    r = _run(nc, [arrays], core_ids=[0])
    return r.results[0]["out_0"].reshape(STEPS * GH, 2 * P, P)
```
